# Optimizing a Trainium2 kernel written in Bass

```python
import numpy as np
import jax
import jax.numpy as jnp

def _softmax(x, axis=-1):
    return jax.nn.softmax(x, axis=axis)

def _gelu(x):
    return jax.nn.gelu(x, approximate=True)

def _silu(x):
    return jax.nn.silu(x)

def _sigmoid(x):
    return jax.nn.sigmoid(x)

def _layernorm(x, axis=-1, eps=1e-05):
    m = jnp.mean(x, axis=axis, keepdims=True)
    v = jnp.var(x, axis=axis, keepdims=True)
    return (x - m) / jnp.sqrt(v + eps)

def _scatter_add(tgt, idx, src, axis=0):
    return tgt.at[idx].add(src)

def _segment_sum(src, seg, n):
    return jax.ops.segment_sum(src, seg, n)
kernel_name = 'mk_prb_d1_jaxref_r2_0794ee'

def setup_inputs(seed: int=0):
    np.random.seed(seed)
    _w = jnp.asarray

    def _L0_attn_setup():
        import jax, jax.numpy as jnp
        import numpy as np
        NUM_HEADS = 16
        LN_EPS = 1e-05
        NORM_EPS = 1e-12

        def _l2norm(t):
            return t / jnp.maximum(jnp.linalg.norm(t, axis=-1, keepdims=True), NORM_EPS)

        def _forward(x, Wq, Wk, Wv, Wf1, Wf2, Wg, Wo1, Wo2, ln_w, Wout):
            B, N, D = x.shape
            H = NUM_HEADS
            HD = D // H
            q = jax.nn.silu(x @ Wq)
            k = jax.nn.silu(x @ Wk)
            v = jax.nn.silu(x @ Wv)
            log_f = jax.nn.log_sigmoid(x @ Wf1 @ Wf2)
            gamma = -jax.nn.sigmoid(x @ Wg)
            q = q.reshape(B, N, H, HD)
            k = k.reshape(B, N, H, HD)
            v = v.reshape(B, N, H, HD)
            log_f = log_f.reshape(B, N, H, HD)
            k = _l2norm(k)
            a = k * gamma[..., None]

            def step(S, inp):
                qt, kt, vt, at, gft = inp
                bs1 = jnp.einsum('bhk,bhkv->bhv', kt, S)
                S1 = S + at[..., :, None] * bs1[..., None, :]
                S2 = jnp.exp(gft)[..., None] * S1
                bs2 = jnp.einsum('bhk,bhkv->bhv', kt, S2)
                S3 = S2 + at[..., :, None] * bs2[..., None, :] + kt[..., :, None] * vt[..., None, :]
                o = jnp.einsum('bhk,bhkv->bhv', qt, S3)
                return (S3, o)
            to_time = lambda t: jnp.moveaxis(t, 1, 0)
            S0 = jnp.zeros((B, H, HD, HD), dtype=x.dtype)
            _, o = jax.lax.scan(step, S0, (to_time(q), to_time(k), to_time(v), to_time(a), to_time(log_f)))
            o = jnp.moveaxis(o, 0, 1)
            z = jnp.zeros_like(o)
            out3 = jnp.stack([z, z, o], axis=2).reshape(B, 3 * N, H, HD)
            out = out3[:, -N:]
            out = out.reshape(B, N, D)
            gate = jax.nn.sigmoid(x @ Wo1 @ Wo2)
            out = out * gate
            mu = jnp.mean(out, axis=-1, keepdims=True)
            var = jnp.mean((out - mu) ** 2, axis=-1, keepdims=True)
            out = (out - mu) * jax.lax.rsqrt(var + LN_EPS) * ln_w
            return out @ Wout
        key = jax.random.key(seed)
        ks = jax.random.split(key, 12)
        B, N, D = (2, 512, 512)
        HD = D // NUM_HEADS
        s = 0.02
        inp = {'x': jax.random.normal(ks[0], (B, N, D), dtype=jnp.float32), 'Wq': jax.random.normal(ks[1], (D, D), dtype=jnp.float32) * s, 'Wk': jax.random.normal(ks[2], (D, D), dtype=jnp.float32) * s, 'Wv': jax.random.normal(ks[3], (D, D), dtype=jnp.float32) * s, 'Wf1': jax.random.normal(ks[4], (D, HD), dtype=jnp.float32) * s, 'Wf2': jax.random.normal(ks[5], (HD, D), dtype=jnp.float32) * s, 'Wg': jax.random.normal(ks[6], (D, NUM_HEADS), dtype=jnp.float32) * s, 'Wo1': jax.random.normal(ks[7], (D, HD), dtype=jnp.float32) * s, 'Wo2': jax.random.normal(ks[8], (HD, D), dtype=jnp.float32) * s, 'ln_w': jnp.ones((D,), dtype=jnp.float32), 'Wout': jax.random.normal(ks[9], (D, D), dtype=jnp.float32) * s}
        return inp
    _L0_attn_in = _L0_attn_setup()

    def _L0_ffn_setup():
        import jax, jax.numpy as jnp
        import numpy as np
        FEATURES = 512
        D_IN = 512

        def fp8_gemm_optimized(x, input_scale, kernel, kernel_scale):
            s_in = input_scale[0]
            s_k = kernel_scale[0]
            x_q = (x.astype(jnp.float32) / s_in).astype(jnp.float8_e4m3fn)
            k_q = (kernel.astype(jnp.float32) / s_k).astype(jnp.float8_e4m3fn)
            y = jnp.dot(x_q.astype(jnp.float32), k_q.astype(jnp.float32), preferred_element_type=jnp.float32)
            return y * (s_in * s_k)
        key = jax.random.key(seed)
        kx, kk, kb = jax.random.split(key, 3)
        x = jax.random.normal(kx, (4, 4096, D_IN), dtype=jnp.float32)
        limit = np.sqrt(6.0 / (D_IN + FEATURES)).astype(np.float32)
        kernel = jax.random.uniform(kk, (D_IN, FEATURES), dtype=jnp.float32, minval=-limit, maxval=limit).astype(jnp.bfloat16)
        input_scale = jnp.ones((1,), dtype=jnp.float32)
        kernel_scale = jnp.ones((1,), dtype=jnp.float32)
        bias = jnp.zeros((FEATURES,), dtype=jnp.bfloat16)
        return {'x': x, 'kernel': kernel, 'input_scale': input_scale, 'kernel_scale': kernel_scale, 'bias': bias}
    _L0_ffn_in = _L0_ffn_setup()
    _d = {'L0_attn_x': _L0_attn_in['x'], 'L0_attn_Wq': _L0_attn_in['Wq'], 'L0_attn_Wk': _L0_attn_in['Wk'], 'L0_attn_Wv': _L0_attn_in['Wv'], 'L0_attn_Wf1': _L0_attn_in['Wf1'], 'L0_attn_Wf2': _L0_attn_in['Wf2'], 'L0_attn_Wg': _L0_attn_in['Wg'], 'L0_attn_Wo1': _L0_attn_in['Wo1'], 'L0_attn_Wo2': _L0_attn_in['Wo2'], 'L0_attn_ln_w': _L0_attn_in['ln_w'], 'L0_attn_Wout': _L0_attn_in['Wout'], 'L0_ffn_kernel': _L0_ffn_in['kernel'], 'L0_ffn_input_scale': _L0_ffn_in['input_scale'], 'L0_ffn_kernel_scale': _L0_ffn_in['kernel_scale'], 'L0_ffn_bias': _L0_ffn_in['bias']}
    _x0 = _d['L0_attn_x']
    _d['L0_attn_x'] = jax.random.normal(jax.random.fold_in(jax.random.key(seed), 1), (1, 8192, 512), dtype=_x0.dtype)
    del _x0
    return _d

def reference(L0_attn_x, L0_attn_Wq, L0_attn_Wk, L0_attn_Wv, L0_attn_Wf1, L0_attn_Wf2, L0_attn_Wg, L0_attn_Wo1, L0_attn_Wo2, L0_attn_ln_w, L0_attn_Wout, L0_ffn_kernel, L0_ffn_input_scale, L0_ffn_kernel_scale, L0_ffn_bias):

    def _L0_attn_ref(x, Wq, Wk, Wv, Wf1, Wf2, Wg, Wo1, Wo2, ln_w, Wout):
        import jax, jax.numpy as jnp
        import numpy as np
        NUM_HEADS = 16
        LN_EPS = 1e-05
        NORM_EPS = 1e-12

        def _l2norm(t):
            return t / jnp.maximum(jnp.linalg.norm(t, axis=-1, keepdims=True), NORM_EPS)

        def _forward(x, Wq, Wk, Wv, Wf1, Wf2, Wg, Wo1, Wo2, ln_w, Wout):
            B, N, D = x.shape
            H = NUM_HEADS
            HD = D // H
            q = jax.nn.silu(x @ Wq)
            k = jax.nn.silu(x @ Wk)
            v = jax.nn.silu(x @ Wv)
            log_f = jax.nn.log_sigmoid(x @ Wf1 @ Wf2)
            gamma = -jax.nn.sigmoid(x @ Wg)
            q = q.reshape(B, N, H, HD)
            k = k.reshape(B, N, H, HD)
            v = v.reshape(B, N, H, HD)
            log_f = log_f.reshape(B, N, H, HD)
            k = _l2norm(k)
            a = k * gamma[..., None]

            def step(S, inp):
                qt, kt, vt, at, gft = inp
                bs1 = jnp.einsum('bhk,bhkv->bhv', kt, S)
                S1 = S + at[..., :, None] * bs1[..., None, :]
                S2 = jnp.exp(gft)[..., None] * S1
                bs2 = jnp.einsum('bhk,bhkv->bhv', kt, S2)
                S3 = S2 + at[..., :, None] * bs2[..., None, :] + kt[..., :, None] * vt[..., None, :]
                o = jnp.einsum('bhk,bhkv->bhv', qt, S3)
                return (S3, o)
            to_time = lambda t: jnp.moveaxis(t, 1, 0)
            S0 = jnp.zeros((B, H, HD, HD), dtype=x.dtype)
            _, o = jax.lax.scan(step, S0, (to_time(q), to_time(k), to_time(v), to_time(a), to_time(log_f)))
            o = jnp.moveaxis(o, 0, 1)
            z = jnp.zeros_like(o)
            out3 = jnp.stack([z, z, o], axis=2).reshape(B, 3 * N, H, HD)
            out = out3[:, -N:]
            out = out.reshape(B, N, D)
            gate = jax.nn.sigmoid(x @ Wo1 @ Wo2)
            out = out * gate
            mu = jnp.mean(out, axis=-1, keepdims=True)
            var = jnp.mean((out - mu) ** 2, axis=-1, keepdims=True)
            out = (out - mu) * jax.lax.rsqrt(var + LN_EPS) * ln_w
            return out @ Wout
        return _forward(x, Wq, Wk, Wv, Wf1, Wf2, Wg, Wo1, Wo2, ln_w, Wout)

    def _L0_ffn_ref(x, kernel, input_scale, kernel_scale, bias):
        import jax, jax.numpy as jnp
        import numpy as np
        FEATURES = 512
        D_IN = 512

        def fp8_gemm_optimized(x, input_scale, kernel, kernel_scale):
            s_in = input_scale[0]
            s_k = kernel_scale[0]
            x_q = (x.astype(jnp.float32) / s_in).astype(jnp.float8_e4m3fn)
            k_q = (kernel.astype(jnp.float32) / s_k).astype(jnp.float8_e4m3fn)
            y = jnp.dot(x_q.astype(jnp.float32), k_q.astype(jnp.float32), preferred_element_type=jnp.float32)
            return y * (s_in * s_k)
        dtype = jnp.bfloat16
        x = x.astype(dtype)
        orig_shape = x.shape
        x2 = x.reshape(-1, x.shape[-1])
        y = fp8_gemm_optimized(x2, input_scale, kernel, kernel_scale)
        y = y.astype(dtype) + bias
        return y.reshape(orig_shape[:-1] + (FEATURES,))
    x = L0_attn_x
    xn = _layernorm(x, axis=-1)
    x = x + _L0_attn_ref(xn, L0_attn_Wq, L0_attn_Wk, L0_attn_Wv, L0_attn_Wf1, L0_attn_Wf2, L0_attn_Wg, L0_attn_Wo1, L0_attn_Wo2, L0_attn_ln_w, L0_attn_Wout) + _L0_ffn_ref(xn, L0_ffn_kernel, L0_ffn_input_scale, L0_ffn_kernel_scale, L0_ffn_bias)
    return x

_drawn_inputs = setup_inputs


def setup_inputs(seed=0):
    import zlib

    import numpy as np

    out = dict(_drawn_inputs(seed))
    spreads = {'L0_attn_ln_w': (1.0, 0.2), 'L0_ffn_bias': (0.0, 0.1)}
    factors = {'L0_attn_Wf1': 8.0,
     'L0_attn_Wf2': 8.0,
     'L0_attn_Wg': 8.0,
     'L0_attn_Wo1': 8.0,
     'L0_attn_Wo2': 8.0}
    for name, (base, spread) in spreads.items():
        noise = np.random.default_rng([zlib.crc32(name.encode()), seed]).standard_normal(out[name].shape)
        drawn = base * np.exp(spread * noise) if base else spread * noise
        out[name] = jnp.asarray(drawn.astype(out[name].dtype))
    for name, factor in factors.items():
        out[name] = (out[name] * factor).astype(out[name].dtype)
    return out
```

```python
import concourse.bass as bass
from concourse import mybir
from contextlib import ExitStack

F32 = mybir.dt.float32
BF16 = mybir.dt.bfloat16
U32 = mybir.dt.uint32
ALU = mybir.AluOpType
ACT = mybir.ActivationFunctionType

P = 128
T = 8192
D = 512
KD = D // P
HD = 32
H = D // HD
NG = D // P
HG = H // NG
CH = 16
SUB = CH // 2
MI = 2 * CH
NCH = T // CH
BT = 512
QT = 2048
NQ = T // QT
UN = QT // CH
PT = 256
PU = PT // CH
NP = QT // PT
RC = 8
OUT0 = (2 * T) // 3
NOUT = T - OUT0
QCH0 = (OUT0 // (CH * RC)) * RC
OT0 = QCH0 * CH
LN_EPS = 1e-5
NORM_EPS = 1e-12
ZMIN = -21.0
assert UN == P and (2 * T + 1) % 3 == 2


class Count:

    def __init__(self, sem, per):
        self.sem, self.per = sem, per

    def at(self, n, c):
        return n * self.per + c


class Chain:

    def __init__(self, eng, sem, n, per):
        self.eng, self.sem, self.n, self.per, self.c = eng, sem, n, per, 0

    def tick(self, ins):
        self.c += 1
        ins.then_inc(self.sem, 1)
        return self.c

    def wait(self, c=None):
        self.eng.wait_ge(self.sem, self.n * self.per + (self.c if c is None else c) + 1)

    def link(self, ins):
        self.tick(ins)
        self.wait()

    def end(self):
        assert self.c == self.per, (self.c, self.per)


class Semaphores(list):

    def new(self, nc, name):
        self.append(nc.alloc_semaphore(name=name))
        return self[-1]

    def prime(self, nc):
        with nc.Block() as block:
            @block.gpsimd
            def _(pool):
                for s in self:
                    pool.sem_inc(s, 1)

    def clear(self, nc):
        nc.clear_and_free_semaphores(self)
        nc.all_engine_barrier()


def settle(eng, passed):
    eng.sem_inc(passed, 1)


def program(nc, x_d, Wq_d, Wk_d, Wv_d, Wf1_d, Wf2_d, Wg_d, Wo1_d, Wo2_d, lnw_d, Wout_d,
            kern_d, sin_d, sk_d, bias_d, out_d):
    x_r = x_d.rearrange("a t d -> (a t) d")
    out_r = out_d.rearrange("a t d -> (a t) d")
    scratch = dict(
        k=nc.dram_tensor("k_scr", (NQ * NG, P, QT), F32).ap(),
        a=nc.dram_tensor("a_scr", (NQ * NG, P, QT), F32).ap(),
        v=nc.dram_tensor("v_scr", (NQ * NG, P, QT), F32).ap(),
        lf=nc.dram_tensor("lf_scr", (NQ * NG, P, QT), F32).ap(),
        q=nc.dram_tensor("q_scr", (NQ * NG, P, QT), F32).ap(),
        U=nc.dram_tensor("U_scr", (NQ * NG, P, UN, HD), F32).ap(),
        WT=nc.dram_tensor("WT_scr", (NQ * NG, P, UN // RC, MI * RC), F32).ap(),
        R=nc.dram_tensor("R_scr", (NQ * NG, P, UN // RC, HD * RC), F32).ap(),
        gam=nc.dram_tensor("gam_scr", (NQ * NG, P, UN), F32).ap(),
        q0=nc.dram_tensor("q0_scr", (NQ * NG, P, UN // RC, CH * RC), F32).ap(),
        Aq=nc.dram_tensor("Aq_scr", (NQ * NG, P, UN // RC, CH * RC), F32).ap(),
        o=nc.dram_tensor("o_scr", (HG, T, NG * HD), F32).ap(),
    )
    with ExitStack() as top:
        consts = make_constants(nc, top)

        def phase(run, *args):
            sems = Semaphores()
            with ExitStack() as ctx:
                run(nc, sems, ctx, *args)
            sems.clear(nc)

        for has_q, q0, q1 in ((False, 0, 2), (True, 2, NQ)):
            phase(project, consts, scratch, x_r, out_r, Wq_d, Wk_d, Wv_d, Wf1_d, Wf2_d, Wg_d,
                  kern_d, sin_d, sk_d, bias_d, has_q, q0, q1)
        for has_q, q0, q1 in ((False, 0, 2), (True, 2, NQ)):
            phase(chunks, consts, scratch, has_q, q0, q1)
        phase(chain_states, scratch)
        phase(finish, consts, scratch, x_r, out_r, Wo1_d, Wo2_d, lnw_d, Wout_d)


def make_constants(nc, top):
    ident = top.enter_context(nc.sbuf_tensor("ident", [P, P], F32))
    ones_bd = top.enter_context(nc.sbuf_tensor("ones_bd", [P, HG, HD], F32))
    spread = top.enter_context(nc.sbuf_tensor("spread", [H, NG, HG, HD], F32))
    made = top.enter_context(nc.semaphore("consts_made"))
    with nc.Block() as block:
        @block.gpsimd
        def _(pool):
            pool.memset(ident[:], 0.0).then_inc(made, 1)
            pool.memset(ones_bd[:], 1.0).then_inc(made, 1)
            pool.memset(spread[:], 0.0).then_inc(made, 1)
            pool.wait_ge(made, 3)
            pool.affine_select(out=ident[:], in_=ident[:], compare_op=ALU.not_equal, fill=1.0,
                               base=0, pattern=[[-1, P]], channel_multiplier=1).then_inc(made, 1)
            pool.affine_select(out=ones_bd[:], in_=ones_bd[:], compare_op=ALU.is_ge, fill=0.0,
                               base=0, pattern=[[-HD, HG], [0, HD]], channel_multiplier=1).then_inc(made, 1)
            pool.affine_select(out=spread[:], in_=spread[:], compare_op=ALU.not_equal, fill=-1.0,
                               base=0, pattern=[[-HG, NG], [-1, HG], [0, HD]],
                               channel_multiplier=1).then_inc(made, 1)
            pool.wait_ge(made, 6)
            pool.affine_select(out=ones_bd[:], in_=ones_bd[:], compare_op=ALU.is_ge, fill=0.0,
                               base=HD - 1, pattern=[[HD, HG], [0, HD]], channel_multiplier=-1).then_inc(made, 1)
            pool.wait_ge(made, 7)
    return dict(ident=ident, ones_bd=ones_bd, spread=spread)


EXP_BITS = 0x7F800000
FP8_MIN = 2.0 ** -6
FP8_MAGIC = 1.5 * 2.0 ** 20


def project(nc, sems, ctx, consts, scratch, x_r, out_r, Wq_d, Wk_d, Wv_d, Wf1_d, Wf2_d, Wg_d,
            kern_d, sin_d, sk_d, bias_d, has_q, q0, q1):
    tag = "pq" if has_q else "p"

    def sb(name, shape, dt=F32):
        return ctx.enter_context(nc.sbuf_tensor(f"{tag}_{name}", shape, dt))

    def sem(name):
        return sems.new(nc, f"{tag}_{name}")

    NT = BT // P
    NB = QT // BT
    ident, ones_bd, spread = consts["ident"], consts["ones_bd"], consts["spread"]
    wk, wv = sb("wk", [P, KD, D]), sb("wv", [P, KD, D])
    wq = sb("wq", [P, KD, D]) if has_q else None
    wf1, wf2, wg = sb("wf1", [P, KD, HD]), sb("wf2", [HD, D]), sb("wg", [P, KD, H])
    kraw, kq = sb("kraw", [P, KD, D], BF16), sb("kq", [P, KD, D], BF16)
    bias = sb("bias", [P, D], BF16)
    scal = sb("scal", [P, 4])
    rsc = sb("rsc", [P, 2])
    osc = sb("osc", [P, 1])
    x = sb("x", [P, 2, NT, D])
    xn = sb("xn", [P, NT, D])
    xnT = sb("xnT", [P, 2, KD, BT])
    st, mv = sb("st", [P, NT, 6]), sb("mv", [P, NT, 2])
    ve, lnv, rs, nt = sb("ve", [P, NT]), sb("lnv", [P, NT]), sb("rs", [P, NT]), sb("nt", [P, NT])
    vq, cq = sb("vq", [P, KD, BT]), sb("cq", [P, KD, BT])
    xb, xq = sb("xb", [P, KD, BT], BF16), sb("xq", [P, KD, BT], BF16)
    f1 = sb("f1", [HD, BT])
    yg, bg, beta = sb("yg", [H, BT]), sb("bg", [H, BT]), sb("beta", [H, BT])
    kr, k2, kn, av = (sb(n, [P, NG, BT]) for n in ("kr", "k2", "kn", "av"))
    vt, z, lz = (sb(n, [P, NG, BT]) for n in ("vt", "z", "lz"))
    qt = sb("qt", [P, NG, BT]) if has_q else None
    kss = sb("kss", [P, NG, BT])
    yb = sb("yb", [P, NT, D], BF16)
    yo = sb("yo", [P, NT, D])
    nscale = sb("nscale", [P, 1])
    psA = [ctx.enter_context(nc.psum_tensor(f"{tag}_psA{i}", [P, 512], F32)) for i in range(4)]
    psD = [ctx.enter_context(nc.psum_tensor(f"{tag}_psD{i}", [P, 512], F32)) for i in range(4)]

    JA = 4 + 2 + 4 + 4 + (4 if has_q else 0) + 4
    JD = 12
    NLOAD = 11 if has_q else 10
    loaded = sem("weights_loaded")
    x_in = [sem(f"x_in{b}") for b in range(2)]
    setup = sem("setup")
    kern_ready = sem("kern_ready")
    act_psum = Count(sem("act_psum_full"), JA)
    act_free = Count(sem("act_psum_free"), JA)
    dve_psum = Count(sem("dve_psum_full"), JD)
    dve_free = Count(sem("dve_psum_free"), JD)
    var_ready = Count(sem("var_ready"), 1)
    rs_raw = Count(sem("rs_raw"), 1)
    xn_ready = Count(sem("xn_ready"), NT)
    xnT_ready = Count(sem("xnT_ready"), 1)
    v_scaled = Count(sem("v_scaled"), 1)
    cq_ready = Count(sem("magic_ready"), 1)
    xq_ready = Count(sem("xq_ready"), 1)
    k_sq = Count(sem("k_squared"), 1)
    kss_ready = Count(sem("k_sumsq_ready"), 1)
    rn_ready = Count(sem("k_rnorm_ready"), 1)
    kn_ready = Count(sem("kn_ready"), 1)
    z_ready = Count(sem("z_ready"), 1)
    lz_ready = Count(sem("log_z_ready"), 1)
    lf_ready = Count(sem("lf_ready"), 1)
    bln_ready = Count(sem("beta_log_ready"), 1)
    blm_ready = Count(sem("beta_arg_ready"), 1)
    beta_ready = Count(sem("beta_ready"), 1)
    a_ready = Count(sem("a_ready"), 1)
    silu_k = Count(sem("silu_k_ready"), 1)
    silu_v = Count(sem("silu_v_ready"), 1)
    silu_q = Count(sem("silu_q_ready"), 1)
    yb_ready = Count(sem("ffn_ready"), NT)
    yo_ready = Count(sem("rows_ready"), NT)
    stored_y = sem("stored_rows")
    stored_k, stored_a, stored_v, stored_lf, stored_q = (sem(f"stored_{n}") for n in ("k", "a", "v", "lf", "q"))
    act_self, dve_self, pool_self = sem("act_steps"), sem("dve_steps"), sem("pool_steps")
    kern_steps = sem("kernel_steps")
    turns = q1 - q0

    passed_sp, passed_dve, passed_pool = (sem(f"passed_{e}") for e in ("sp", "dve", "pool"))
    sems.prime(nc)

    with nc.Block() as block:
        def store_block(sp, i, s):
            n = i * NB + s
            it = (i + q0) * NG
            cols = slice(s * BT, (s + 1) * BT)
            sp.wait_ge(silu_v.sem, silu_v.at(n, 1) + 1)
            settle(sp, passed_sp)
            sp.dma_start(scratch["v"][bass.ds(it, NG), :, cols].rearrange("g p t -> p g t"), vt[:]).then_inc(stored_v, 16)
            if has_q:
                sp.wait_ge(silu_q.sem, silu_q.at(n, 1) + 1)
                settle(sp, passed_sp)
                sp.dma_start(scratch["q"][bass.ds(it, NG), :, cols].rearrange("g p t -> p g t"), qt[:]).then_inc(stored_q, 16)
            sp.wait_ge(lf_ready.sem, lf_ready.at(n, 1) + 1)
            settle(sp, passed_sp)
            sp.dma_start(scratch["lf"][bass.ds(it, NG), :, cols].rearrange("g p t -> p g t"), z[:]).then_inc(stored_lf, 16)
            sp.wait_ge(kn_ready.sem, kn_ready.at(n, 1) + 1)
            settle(sp, passed_sp)
            sp.dma_start(scratch["k"][bass.ds(it, NG), :, cols].rearrange("g p t -> p g t"), kn[:]).then_inc(stored_k, 16)
            sp.wait_ge(a_ready.sem, a_ready.at(n, 1) + 1)
            settle(sp, passed_sp)
            sp.dma_start(scratch["a"][bass.ds(it, NG), :, cols].rearrange("g p t -> p g t"), av[:]).then_inc(stored_a, 16)
            sp.wait_ge(yo_ready.sem, yo_ready.at(n, 2 * NT) + 1)
            settle(sp, passed_sp)
            row = (i * NB + (q0 * NB + s)) * BT
            sp.dma_start(out_r[bass.ds(row, BT), :].rearrange("(j p) d -> p j d", p=P), yo[:]).then_inc(stored_y, 16)

        @block.sync
        def _(sp):
            for dst, src in ((wk, Wk_d), (wv, Wv_d), (wf1, Wf1_d), (wg, Wg_d), (kraw, kern_d)) \
                    + (((wq, Wq_d),) if has_q else ()):
                sp.dma_start(dst[:], src.rearrange("(k p) n -> p k n", p=P)).then_inc(loaded, 16)
            sp.dma_start(wf2[:], Wf2_d).then_inc(loaded, 16)
            sp.dma_start(bias[:], bias_d.rearrange("(a n) -> a n", a=1).to_broadcast([P, D])).then_inc(loaded, 16)
            for c, s in ((0, sin_d), (1, sk_d)):
                sp.dma_start(scal[:, c:c + 1], s.rearrange("(a n) -> a n", a=1).to_broadcast([P, 1])).then_inc(loaded, 16)
            sp.dma_start(scal[:, 2:3], sin_d.rearrange("(a n) -> a n", a=1).to_broadcast([P, 1])).then_inc(loaded, 16)
            with sp.Fori(0, turns) as i:
                for s in range(NB):
                    n = i * NB + s
                    sp.wait_ge(yo_ready.sem, n * NT + 1)
                    settle(sp, passed_sp)
                    row = (i * NB + (q0 * NB + s)) * BT
                    sp.dma_start(x[:, s % 2, :, :],
                                 x_r[bass.ds(row, BT), :].rearrange("(j p) d -> p j d", p=P)).then_inc(x_in[s % 2], 16)
                    if s > 0:
                        store_block(sp, i, s - 1)
                store_block(sp, i, NB - 1)
            for sm in (stored_y, stored_k, stored_a, stored_v, stored_lf) + ((stored_q,) if has_q else ()):
                sp.wait_ge(sm, 16 * turns * NB + 1)

        @block.gpsimd
        def _(pool):
            pool.sem_inc(yo_ready.sem, NT)
            with pool.Fori(0, turns) as i:
                for s in range(NB):
                    n = i * NB + s
                    b = s % 2
                    ch = Chain(pool, pool_self, n, 2 + NT)
                    pool.wait_ge(xnT_ready.sem, xnT_ready.at(n, 1) + 1)
                    if s == 0:
                        pool.wait_ge(kern_ready, 1 + 1)
                    pool.wait_ge(yb_ready.sem, n * NT + 1)
                    settle(pool, passed_pool)
                    ch.link(pool.tensor_copy(xb[:], xnT[:, b]))
                    settle(pool, passed_pool)
                    pool.tensor_scalar(vq[:], xb[:], rsc[:, 0:1], None, ALU.mult).then_inc(v_scaled.sem, 1)
                    pool.wait_ge(cq_ready.sem, cq_ready.at(n, 1) + 1)
                    ch.link(pool.tensor_tensor(vq[:], vq[:], cq[:], ALU.add))
                    pool.tensor_tensor(xq[:], vq[:], cq[:], ALU.subtract).then_inc(xq_ready.sem, 1)
                    pool.wait_ge(silu_k.sem, silu_k.at(n, 1) + 1)
                    pool.tensor_tensor(k2[:], kr[:], kr[:], ALU.mult).then_inc(k_sq.sem, 1)
                    pool.wait_ge(rn_ready.sem, rn_ready.at(n, 1) + 1)
                    pool.wait_ge(stored_k, n * 16 + 1)
                    pool.wait_ge(a_ready.sem, n + 1)
                    pool.tensor_tensor(kn[:], kr[:], kss[:], ALU.mult).then_inc(kn_ready.sem, 1)
                    pool.wait_ge(stored_y, n * 16 + 1)
                    for j in range(NT):
                        pool.wait_ge(yb_ready.sem, yb_ready.at(n, j + 1) + 1)
                        ch.link(pool.tensor_tensor(yb[:, j], yb[:, j], bias[:], ALU.add))
                        pool.tensor_tensor(yo[:, j], yb[:, j], x[:, b, j], ALU.add).then_inc(yo_ready.sem, 1)
                    ch.end()

        @block.scalar
        def _(act):
            act.sem_inc(act_free.sem, 3)
            act.wait_ge(setup, 1 + 1)
            with act.Fori(0, turns) as i:
                for s in range(NB):
                    n = i * NB + s
                    b = s % 2
                    job = [0]
                    ch = Chain(act, act_self, n, 1 + 2 + 2 + 1)

                    def take(out, func, done=None, scale=1.0, rows=P):
                        act.wait_ge(act_psum.sem, act_psum.at(n, job[0] + 1) + 1)
                        act.activation(out, psA[(s * JA + job[0]) % 4][0:rows, :], func, scale=scale)\
                           .then_inc(act_free.sem, 1)
                        job[0] += 1

                    act.wait_ge(var_ready.sem, var_ready.at(n, 1) + 1)
                    act.wait_ge(xn_ready.sem, n * NT + 1)
                    ch.link(act.activation(lnv[:], ve[:], ACT.Ln))
                    act.activation(rs[:], lnv[:], ACT.Exp, scale=-0.5).then_inc(rs_raw.sem, 1)
                    act.wait_ge(xq_ready.sem, n + 1)
                    for kd in range(KD):
                        take(xnT[:, b, kd, :], ACT.Copy)
                    act.wait_ge(act_free.sem, act_free.at(n, job[0] + 3) + 1)
                    act.sem_inc(xnT_ready.sem, 1)
                    act.wait_ge(dve_psum.sem, dve_psum.at(n, 0) + 1)
                    take(f1[:], ACT.Copy, rows=HD)
                    take(yg[:], ACT.Copy, rows=H)
                    act.wait_ge(a_ready.sem, n + 1)
                    act.wait_ge(kn_ready.sem, n + 1)
                    for g in range(NG):
                        take(kr[:, g, :], ACT.Silu)
                    act.wait_ge(act_free.sem, act_free.at(n, job[0] + 3) + 1)
                    act.sem_inc(silu_k.sem, 1)
                    act.wait_ge(stored_v, n * 16 + 1)
                    for g in range(NG):
                        take(vt[:, g, :], ACT.Silu)
                    act.wait_ge(act_free.sem, act_free.at(n, job[0] + 3) + 1)
                    act.sem_inc(silu_v.sem, 1)
                    if has_q:
                        act.wait_ge(stored_q, n * 16 + 1)
                        for g in range(NG):
                            take(qt[:, g, :], ACT.Silu)
                        act.wait_ge(act_free.sem, act_free.at(n, job[0] + 3) + 1)
                        act.sem_inc(silu_q.sem, 1)
                    ch.link(act.activation(bg[:], yg[:], ACT.Abs))
                    ch.link(act.activation(bg[:], bg[:], ACT.Exp, scale=-1.0))
                    act.activation(bg[:], bg[:], ACT.Ln, bias=1.0).then_inc(bln_ready.sem, 1)
                    act.wait_ge(z_ready.sem, z_ready.at(n, 1) + 1)
                    act.wait_ge(lf_ready.sem, n + 1)
                    ch.link(act.activation(lz[:], z[:], ACT.Abs))
                    ch.link(act.activation(lz[:], lz[:], ACT.Exp, scale=-1.0))
                    act.activation(lz[:], lz[:], ACT.Ln, bias=1.0).then_inc(lz_ready.sem, 1)
                    act.wait_ge(blm_ready.sem, blm_ready.at(n, 1) + 1)
                    act.activation(beta[:], yg[:], ACT.Exp).then_inc(beta_ready.sem, 1)
                    act.wait_ge(kss_ready.sem, kss_ready.at(n, 1) + 1)
                    ch.link(act.activation(kss[:], kss[:], ACT.Ln, scale=NSC))
                    act.activation(kss[:], kss[:], ACT.Exp, scale=-0.5, bias=nscale[:]).then_inc(rn_ready.sem, 1)
                    act.wait_ge(yo_ready.sem, n * NT + NT + 1)
                    for j in range(NT):
                        act.wait_ge(act_psum.sem, act_psum.at(n, job[0] + 1) + 1)
                        act.activation(yb[:, j, :], psA[(s * JA + job[0]) % 4][:], ACT.Identity, scale=osc[:])\
                           .then_inc(act_free.sem, 1)
                        job[0] += 1
                        act.wait_ge(act_free.sem, act_free.at(n, job[0] + 3) + 1)
                        act.sem_inc(yb_ready.sem, 1)
                    assert job[0] == JA
                    ch.end()

        @block.vector
        def _(dve):
            ns = [0]

            def slink(ins):
                ns[0] += 1
                ins.then_inc(kern_steps, 1)
                dve.wait_ge(kern_steps, ns[0] + 1)

            dve.sem_inc(dve_free.sem, 3)
            dve.wait_ge(loaded, NLOAD * 16 + 1)
            slink(dve.memset(nscale[:], NBIAS))
            slink(dve.reciprocal(rsc[:, 0:1], scal[:, 0:1]))
            slink(dve.reciprocal(rsc[:, 1:2], scal[:, 1:2]))
            slink(dve.tensor_tensor(osc[:], scal[:, 0:1], scal[:, 1:2], ALU.mult))
            dve.sem_inc(setup, 1)
            wtmp = vq[:]
            slink(dve.tensor_scalar(wtmp, kraw[:], rsc[:, 1:2], None, ALU.mult))
            slink(dve.tensor_scalar(cq[:].bitcast(U32), wtmp.bitcast(U32), EXP_BITS, None, ALU.bitwise_and))
            slink(dve.tensor_scalar(cq[:], cq[:], FP8_MIN, FP8_MAGIC, ALU.max, ALU.mult))
            slink(dve.tensor_tensor(wtmp, wtmp, cq[:], ALU.add))
            slink(dve.tensor_tensor(kq[:], wtmp, cq[:], ALU.subtract))
            dve.sem_inc(kern_ready, 1)
            with dve.Fori(0, turns) as i:
                for s in range(NB):
                    n = i * NB + s
                    b = s % 2
                    ch = Chain(dve, dve_self, n, NT + NT + 1 + 4 + 1)
                    job = [0]

                    def bank():
                        dve.wait_ge(dve_psum.sem, dve_psum.at(n, job[0] + 1) + 1)
                        job[0] += 1
                        return psD[(s * JD + job[0] - 1) % 4]

                    dve.wait_ge(x_in[b], (i * (NB // 2) + s // 2) * 16 + 16 + 1)
                    for j in range(NT):
                        ch.tick(dve.bn_stats(st[:, j, :], x[:, b, j, :]))
                    ch.wait()
                    settle(dve, passed_dve)
                    for j in range(NT):
                        ch.tick(dve.bn_aggr(mv[:, j, :], st[:, j, :]))
                    ch.wait()
                    ch.tick(dve.tensor_scalar(ve[:], mv[:, :, 1], LN_EPS, None, ALU.add))
                    ch.wait()
                    dve.sem_inc(var_ready.sem, 1)
                    dve.wait_ge(rs_raw.sem, rs_raw.at(n, 1) + 1)
                    ch.link(dve.tensor_tensor(nt[:], rs[:], rs[:], ALU.mult))
                    ch.link(dve.tensor_tensor(nt[:], nt[:], ve[:], ALU.mult))
                    ch.link(dve.tensor_scalar(nt[:], nt[:], -0.5, 1.5, ALU.mult, ALU.add))
                    ch.link(dve.tensor_tensor(rs[:], nt[:], rs[:], ALU.mult))
                    dve.wait_ge(xnT_ready.sem, n + 1)
                    for j in range(NT):
                        dve.tensor_scalar(xn[:, j, :], x[:, b, j, :], mv[:, j, 0:1], rs[:, j:j + 1],
                                          ALU.subtract, ALU.mult).then_inc(xn_ready.sem, 1)
                    dve.wait_ge(v_scaled.sem, v_scaled.at(n, 1) + 1)
                    dve.wait_ge(xq_ready.sem, n + 1)
                    ch.link(dve.tensor_scalar(cq[:].bitcast(U32), vq[:].bitcast(U32), EXP_BITS, None, ALU.bitwise_and))
                    dve.tensor_scalar(cq[:], cq[:], FP8_MIN, FP8_MAGIC, ALU.max, ALU.mult).then_inc(cq_ready.sem, 1)
                    dve.wait_ge(stored_lf, n * 16 + 1)
                    for g in range(NG):
                        dve.tensor_scalar(z[:, g, :], bank()[:], ZMIN, None, ALU.max).then_inc(dve_free.sem, 1)
                    dve.wait_ge(dve_free.sem, dve_free.at(n, 4 + 3) + 1)
                    dve.sem_inc(z_ready.sem, 1)
                    dve.wait_ge(bln_ready.sem, bln_ready.at(n, 1) + 1)
                    dve.scalar_tensor_tensor(out=yg[:], in0=yg[:], scalar=0.0, in1=bg[:], op0=ALU.min,
                                             op1=ALU.subtract).then_inc(blm_ready.sem, 1)
                    dve.wait_ge(lz_ready.sem, lz_ready.at(n, 1) + 1)
                    dve.scalar_tensor_tensor(out=z[:], in0=z[:], scalar=0.0, in1=lz[:], op0=ALU.min,
                                             op1=ALU.subtract).then_inc(lf_ready.sem, 1)
                    dve.wait_ge(kn_ready.sem, n + 1)
                    for g in range(NG):
                        dve.tensor_scalar(kss[:, g, :], bank()[:], NORM_EPS ** 2, None, ALU.max).then_inc(dve_free.sem, 1)
                    dve.wait_ge(dve_free.sem, dve_free.at(n, 8 + 3) + 1)
                    dve.sem_inc(kss_ready.sem, 1)
                    dve.wait_ge(kn_ready.sem, kn_ready.at(n, 1) + 1)
                    dve.wait_ge(stored_a, n * 16 + 1)
                    for g in range(NG):
                        dve.tensor_tensor(av[:, g, :], bank()[:], kn[:, g, :], ALU.mult).then_inc(dve_free.sem, 1)
                    dve.wait_ge(dve_free.sem, dve_free.at(n, 12 + 3) + 1)
                    dve.sem_inc(a_ready.sem, 1)
                    ch.end()

        @block.tensor
        def _(pe):
            pe.wait_ge(loaded, NLOAD * 16 + 1)
            pe.wait_ge(kern_ready, 1 + 1)
            with pe.Fori(0, turns) as i:
                for s in range(NB):
                    n = i * NB + s
                    b = s % 2
                    ja, jd = [0], [0]

                    def bank_a():
                        pe.wait_ge(act_free.sem, act_free.at(n, ja[0]) + 1)
                        ja[0] += 1
                        return psA[(s * JA + ja[0] - 1) % 4]

                    def bank_d():
                        pe.wait_ge(dve_free.sem, dve_free.at(n, jd[0]) + 1)
                        jd[0] += 1
                        return psD[(s * JD + jd[0] - 1) % 4]

                    pe.wait_ge(xn_ready.sem, xn_ready.at(n, NT) + 1)
                    for kd in range(KD):
                        ps = bank_a()
                        for j in range(NT):
                            last = nc.tensor.transpose(ps[:, j * P:(j + 1) * P], xn[:, j, kd * P:(kd + 1) * P], ident[:])
                        last.then_inc(act_psum.sem, 1)
                    pe.wait_ge(xnT_ready.sem, xnT_ready.at(n, 1) + 1)

                    def product(ps, w, rows):
                        for kd in range(KD):
                            last = nc.tensor.matmul(ps[0:rows, :], w(kd), xnT[:, b, kd, :],
                                                    start=(kd == 0), stop=(kd == KD - 1))
                        return last

                    product(bank_a(), lambda kd: wf1[:, kd, :], HD).then_inc(act_psum.sem, 1)
                    product(bank_a(), lambda kd: wg[:, kd, :], H).then_inc(act_psum.sem, 1)
                    for w in (wk, wv) + ((wq,) if has_q else ()):
                        for g in range(NG):
                            product(bank_a(), lambda kd: w[:, kd, g * P:(g + 1) * P], P).then_inc(act_psum.sem, 1)
                    for g in range(NG):
                        ps = bank_d()
                        nc.tensor.matmul(ps[:], wf2[:, g * P:(g + 1) * P], f1[:], start=True, stop=True)\
                          .then_inc(dve_psum.sem, 1)
                    pe.wait_ge(k_sq.sem, k_sq.at(n, 1) + 1)
                    for g in range(NG):
                        ps = bank_d()
                        nc.tensor.matmul(ps[:], ones_bd[:].rearrange("p h c -> p (h c)"), k2[:, g, :],
                                         start=True, stop=True).then_inc(dve_psum.sem, 1)
                    pe.wait_ge(beta_ready.sem, beta_ready.at(n, 1) + 1)
                    for g in range(NG):
                        ps = bank_d()
                        nc.tensor.matmul(ps[:], spread[:, g].rearrange("p h c -> p (h c)"), beta[:],
                                         start=True, stop=True).then_inc(dve_psum.sem, 1)
                    pe.wait_ge(xq_ready.sem, xq_ready.at(n, 1) + 1)
                    for j in range(NT):
                        ps = bank_a()
                        for kd in range(KD):
                            last = nc.tensor.matmul(ps[:], xq[:, kd, j * P:(j + 1) * P], kq[:, kd, :],
                                                    start=(kd == 0), stop=(kd == KD - 1))
                        last.then_inc(act_psum.sem, 1)
                    assert ja[0] == JA and jd[0] == JD


NSC = 2.0 ** 20
NBIAS = 10.0 * 0.6931471805599453


def chunks(nc, sems, ctx, consts, scratch, has_q, q0, q1):
    tag = "cq" if has_q else "c"

    def sb(name, shape, dt=F32):
        return ctx.enter_context(nc.sbuf_tensor(f"{tag}_{name}", shape, dt))

    def sem(name):
        return sems.new(nc, f"{tag}_{name}")

    ident = consts["ident"]
    RG = PU // RC
    NS = PT // SUB
    W = PU * MI
    names = ["k", "a", "v", "lf"] + (["q"] if has_q else [])
    src = {m: sb("in_" + m, [P, 2, PT]) for m in names}
    keep = sb("keep", [P, NS, SUB])
    g8 = sb("g8", [P, PT])
    gm = sb("gm", [P, PT, 2])
    dm, he = sb("dm", [P, W]), sb("he", [P, W])
    ep, en, ff, hh = (sb(m, [P, PT, 2]) for m in ("ep", "en", "ff", "hh"))
    ld, rd = sb("ld", [P, 2, PT, 2]), sb("rd", [P, 2, MI, PU])
    l8, r8 = sb("l8", [P, 2, PU, CH]), sb("r8", [P, 2, CH, PU])
    l0, re = sb("l0", [P, PU, MI]), sb("re", [P, PU, MI])
    vm = sb("vm", [P, PT, 2])
    gam = sb("gam", [P, 2, PU])
    l0t, vtm = sb("l0t", [P, NP, HD, PU]), sb("vtm", [P, UN, HD])
    ret = sb("ret", [P, 2, RG, HD, RC])
    bd1 = sb("bd1", [P, 2, HG, MI, PU])
    bd2 = sb("bd2", [P, 2, HG, MI, PU])
    bd3 = sb("bd3", [P, 2, HG, MI, PU])
    dst = sb("dstk", [P, UN, MI])
    ttr = sb("ttr", [P, NP, MI, PU])
    cst = sb("cstk", [P, UN, CH])
    tl = sb("tl", [P, MI, HG, MI])
    HD_DVE = 3
    tmpd = sb("tmpd", [P, HD_DVE, CH * (CH - 1)])
    lmask = sb("lmask", [P, CH, CH])
    usb, wsb = sb("usb", [P, 2, W]), sb("wsb", [P, 2, W])
    if has_q:
        qd, q8 = sb("qd", [P, 2, PU, CH]), sb("q8", [P, 2, PU, SUB])
        q0t = sb("q0t", [P, 2, RG, CH, RC])
        aq = sb("aq", [P, 2, RG, CH, RC])
        qmask, cmask = sb("qmask", [P, CH]), sb("cmask", [P, SUB])
        psQ = ctx.enter_context(nc.psum_tensor(f"{tag}_psQ", [P, 512], F32))
    psD = [ctx.enter_context(nc.psum_tensor(f"{tag}_psD{i}", [P, 512], F32)) for i in range(2)]
    psC = ctx.enter_context(nc.psum_tensor(f"{tag}_psC", [P, 512], F32))
    psL = [ctx.enter_context(nc.psum_tensor(f"{tag}_psL{i}", [P, 512], F32)) for i in range(2)]
    psW = [ctx.enter_context(nc.psum_tensor(f"{tag}_psW{i}", [P, 512], F32)) for i in range(2)]

    NL = 8 + 4 + 8
    NSRC = len(names)
    setup = sem("setup")
    x_in = [sem(f"pieces_in{b}") for b in range(2)]
    src_free = Count(sem("pieces_used"), NP)
    gm_ready = Count(sem("gm_ready"), NP)
    exps = Count(sem("exps_ready"), NP)
    rows_ready = Count(sem("rows_ready"), NP)
    bdr_in = [sem(f"bd_right_in{b}") for b in range(2)]
    prods = Count(sem("products_full"), NP)
    prods_free = Count(sem("products_free"), NP)
    aq_free = Count(sem("q_products_read"), NP)
    tm_ready = Count(sem("row_major_ready"), NP)
    store1 = [sem(f"stored_right{b}") for b in range(2)]
    ST1 = 16 * (4 if has_q else 2)
    lanes = Count(sem("lane_banks_full"), NL)
    lanes_free = Count(sem("lane_banks_free"), NL)
    mats = Count(sem("matrices_ready"), 1)
    solved = Count(sem("solved"), 2)
    tt_ready = Count(sem("inverse_ready"), 1)
    bdt_in = [sem(f"bd_left_in{b}") for b in range(2)]
    uw = Count(sem("uw_full"), 2 * NP)
    uw_free = Count(sem("uw_read"), 2 * NP)
    store2 = [sem(f"stored_uw{b}") for b in range(2)]
    act_self, dve_self, pool_self = sem("act_steps"), sem("dve_steps"), sem("pool_steps")
    turns = (q1 - q0) * NG
    it0 = q0 * NG

    SOLVE_STEPS = 2 * (MI - 2)
    tmpg = sb("tmpg", [P, HG - HD_DVE, CH * (CH - 1)])
    pool_setup, dve_setup = sem("pool_setup"), sem("dve_setup")
    dve_solve = sem("dve_solve")
    rows_l = Count(sem("left_rows_ready"), NP)

    def pair(i, p):
        return i * (NP // 2) + p // 2

    passed_sp, passed_dve, passed_pool = (sem(f"passed_{e}") for e in ("sp", "dve", "pool"))
    sems.prime(nc)

    with nc.Block() as block:
        def solve(eng, i, self_sem, tmp, h0, h1):
            ch = Chain(eng, self_sem, i, SOLVE_STEPS)
            eng.wait_ge(mats.sem, mats.at(i, 1) + 1)
            nh = h1 - h0
            tlh = tl[:].rearrange("p s h r -> p h s r")
            for r in range(1, MI - 1):
                below, left = MI - 1 - r, r
                col = tlh[:, h0:h1, r + 1:MI, r:r + 1].to_broadcast([P, nh, below, left])
                row = tlh[:, h0:h1, r:r + 1, 0:r].to_broadcast([P, nh, below, left])
                t = tmp[:, 0:nh, 0:below * left].rearrange("p h (b l) -> p h b l", l=left)
                ch.link(eng.tensor_tensor(t, col, row, ALU.mult))
                acc = tlh[:, h0:h1, r + 1:MI, 0:r]
                ch.link(eng.tensor_tensor(acc, acc, t, ALU.add))
            eng.sem_inc(solved.sem, 1)
            ch.end()

        @block.sync
        def _(sp):
            def load(i, p):
                j = i * NP + p
                sp.wait_ge(src_free.sem, j + 1)
                settle(sp, passed_sp)
                for m in names:
                    sp.dma_start(src[m][:, p % 2, :], scratch[m][bass.ds(i + it0, 1), :, p * PT:(p + 1) * PT]
                                 .rearrange("a p t -> p (a t)")).then_inc(x_in[p % 2], 16)

            def bd_right(i, p):
                j = i * NP + p
                sp.wait_ge(rows_l.sem, j + 1 + 1)
                settle(sp, passed_sp)
                sp.wait_ge(prods.sem, j + 1 + 1)
                settle(sp, passed_sp)
                if p < 2:
                    sp.wait_ge(uw.sem, 2 * NP * i + 2 + 1)
                settle(sp, passed_sp)
                for h in range(HG):
                    r = slice(h * HD, (h + 1) * HD)
                    sp.dma_start(bd1[r, p % 2, h], rd[r, p % 2]).then_inc(bdr_in[p % 2], 16)
                    sp.dma_start(bd2[r, p % 2, h, 0:CH], r8[r, p % 2]).then_inc(bdr_in[p % 2], 16)

            def out_right(i, p):
                j = i * NP + p
                sp.wait_ge(tm_ready.sem, j + 1 + 1)
                settle(sp, passed_sp)
                us = slice(p * PU, (p + 1) * PU)
                ug = slice(p * RG, (p + 1) * RG)
                sp.dma_start(scratch["R"][bass.ds(i + it0, 1), :, ug, :].rearrange("a p u c -> p (a u) c"),
                             ret[:, p % 2].rearrange("p u c r -> p u (c r)")).then_inc(store1[p % 2], 16)
                sp.dma_start(scratch["gam"][bass.ds(i + it0, 1), :, us].rearrange("a p u -> p (a u)"),
                             gam[:, p % 2]).then_inc(store1[p % 2], 16)
                if has_q:
                    sp.dma_start(scratch["q0"][bass.ds(i + it0, 1), :, ug, :].rearrange("a p u c -> p (a u) c"),
                                 q0t[:, p % 2].rearrange("p u c r -> p u (c r)")).then_inc(store1[p % 2], 16)
                    sp.wait_ge(aq_free.sem, j + 1 + 1)
                    settle(sp, passed_sp)
                    sp.dma_start(scratch["Aq"][bass.ds(i + it0, 1), :, ug, :].rearrange("a p u c -> p (a u) c"),
                                 aq[:, p % 2].rearrange("p u c r -> p u (c r)")).then_inc(store1[p % 2], 16)

            def bd_left(i, p):
                j = i * NP + p
                sp.wait_ge(uw.sem, 2 * j + 1)
                settle(sp, passed_sp)
                for h in range(HG):
                    r = slice(h * HD, (h + 1) * HD)
                    sp.dma_start(bd1[r, p % 2, h], ttr[r, p]).then_inc(bdt_in[p % 2], 16)
                    sp.dma_start(bd3[r, p % 2, h], l0t[r, p]).then_inc(bdt_in[p % 2], 16)

            def out_left(i, p):
                j = i * NP + p
                sp.wait_ge(uw_free.sem, 2 * j + 3 + 1)
                settle(sp, passed_sp)
                for m, buf, us in (("U", usb, slice(p * PU, (p + 1) * PU)), ("WT", wsb, slice(p * RG, (p + 1) * RG))):
                    sp.dma_start(scratch[m][bass.ds(i + it0, 1), :, us, :].rearrange("a p u c -> p (a u c)"),
                                 buf[:, p % 2]).then_inc(store2[p % 2], 16)

            sp.wait_ge(setup, 2 + 1)
            with sp.Fori(0, turns) as i:
                load(i, 0)
                for p in range(NP):
                    if p + 1 < NP:
                        load(i, p + 1)
                    bd_right(i, p)
                    if p:
                        out_right(i, p - 1)
                out_right(i, NP - 1)
                sp.wait_ge(tt_ready.sem, i + 1 + 1)
                settle(sp, passed_sp)
                for p in range(NP):
                    bd_left(i, p)
                    if p:
                        out_left(i, p - 1)
                out_left(i, NP - 1)
            for b in range(2):
                sp.wait_ge(store1[b], turns * (NP // 2) * ST1 + 1)
                sp.wait_ge(store2[b], turns * (NP // 2) * 32 + 1)

        @block.gpsimd
        def _(pool):
            tmpp = tmpg
            n = [0]

            def link(ins):
                n[0] += 1
                ins.then_inc(pool_setup, 1)
                pool.wait_ge(pool_setup, n[0] + 1)

            for t in (bd1, bd2, bd3):
                link(pool.memset(t[:], 0.0))
            link(pool.memset(keep[:], 1.0))
            link(pool.memset(keep[:, :, 0:1], 0.0))
            link(pool.memset(gm[:], 0.0))
            link(pool.memset(vm[:], 0.0))
            link(pool.memset(tl[:], 0.0))
            link(pool.affine_select(out=tl[:], in_=tl[:], compare_op=ALU.not_equal, fill=1.0, base=0,
                                    pattern=[[1, MI], [0, HG], [-1, MI]], channel_multiplier=0))
            link(pool.memset(lmask[:], 1.0))
            link(pool.affine_select(out=lmask[:], in_=lmask[:], compare_op=ALU.is_gt, fill=0.0, base=0,
                                    pattern=[[1, CH], [-1, CH]], channel_multiplier=0))
            if has_q:
                link(pool.memset(aq[:], 0.0))
                link(pool.memset(qmask[:], 1.0))
                link(pool.memset(cmask[:], 1.0))
                for h in range(HG):
                    r = slice(h * HD, (h + 1) * HD)
                    link(pool.affine_select(out=qmask[r], in_=qmask[r], compare_op=ALU.is_ge, fill=0.0, base=1,
                                            pattern=[[2, CH]], channel_multiplier=-1))
                    link(pool.affine_select(out=qmask[r, SUB:CH], in_=qmask[r, SUB:CH], compare_op=ALU.is_ge, fill=0.0,
                                            base=-CH, pattern=[[0, SUB]], channel_multiplier=1))
                    link(pool.affine_select(out=cmask[r], in_=cmask[r], compare_op=ALU.is_ge, fill=0.0,
                                            base=CH - 1, pattern=[[0, SUB]], channel_multiplier=-1))
            pool.sem_inc(setup, 1)
            with pool.Fori(0, turns) as i:
                solve(pool, i, pool_self, tmpp, HD_DVE, HG)

        @block.scalar
        def _(act):
            act.sem_inc(lanes_free.sem, 1)
            act.sem_inc(uw_free.sem, 1)
            with act.Fori(0, turns) as i:
                for p in range(NP):
                    j = i * NP + p
                    b = p % 2
                    act.wait_ge(gm_ready.sem, j + 1 + 1)
                    act.wait_ge(rows_ready.sem, j + 1)
                    act.activation(ep[:].rearrange("p t m -> p (t m)"), dm[:], ACT.Exp)
                    act.activation(en[:].rearrange("p t m -> p (t m)"), dm[:], ACT.Exp, scale=-1.0)
                    act.activation(ff[:], gm[:], ACT.Exp)
                    act.activation(hh[:].rearrange("p t m -> p (t m)"), he[:], ACT.Exp).then_inc(exps.sem, 1)
                    act.wait_ge(prods.sem, j + 3 + 1)
                    us = slice(p * PU, (p + 1) * PU)
                    act.activation(dst[:, us, :], psD[b][:].rearrange("p (u m) -> p u m", u=PU), ACT.Copy)
                    act.activation(cst[:, us, :], psC[:, b * 256:(b + 1) * 256].rearrange("p (u m) -> p u m", u=PU), ACT.Copy)\
                       .then_inc(prods_free.sem, 1)
                act.wait_ge(lanes_free.sem, lanes_free.at(i, 8 + 1) + 1)
                act.wait_ge(uw.sem, 2 * NP * i + 2 + 1)
                for c in range(8, NL):
                    act.wait_ge(lanes.sem, lanes.at(i, c + 1) + 1)
                    ps = psL[c % 2]
                    if c < 12:
                        s0 = CH + 4 * (c - 8)
                        act.activation(tl[:, s0:s0 + 4, :, 0:CH],
                                       ps[:].rearrange("p (s h r) -> p s h r", s=4, h=HG)[:, :, :, 0:CH], ACT.Copy)\
                           .then_inc(lanes_free.sem, 1)
                    else:
                        s0 = 4 * (c - 12)
                        act.activation(ttr[:, :, s0:s0 + 4, :].rearrange("p a s u -> p s a u"),
                                       ps[:].rearrange("p (s a u) -> p s a u", s=4, u=PU), ACT.Copy).then_inc(lanes_free.sem, 1)
                act.wait_ge(lanes_free.sem, lanes_free.at(i, NL + 1) + 1)
                act.sem_inc(tt_ready.sem, 1)
                for p in range(NP):
                    j = i * NP + p
                    act.wait_ge(store2[p % 2], pair(i, p) * 32 + 1)
                    for c, buf in ((0, usb), (1, wsb)):
                        act.wait_ge(uw.sem, 2 * j + c + 3 + 1)
                        act.activation(buf[:, p % 2], psW[c][:], ACT.Copy).then_inc(uw_free.sem, 1)

        @block.vector
        def _(dve):
            dve.wait_ge(setup, 1 + 1)
            dve.sem_inc(src_free.sem, 1)
            dve.sem_inc(prods.sem, 2)
            dve.sem_inc(uw.sem, 2)
            dve.sem_inc(prods_free.sem, 1)
            dve.sem_inc(setup, 1)
            npc = 9 + (3 if has_q else 0)
            with dve.Fori(0, turns) as i:
                for p in range(NP):
                    j = i * NP + p
                    b = p % 2
                    ch = Chain(dve, dve_self, j, npc)
                    gmv = gm[:].rearrange("p (n s) m -> p n s m", s=SUB)
                    g8v = g8[:].rearrange("p (n s) -> p n s", s=SUB)
                    dve.wait_ge(x_in[b], (pair(i, p) + 1) * (NSRC * 16) + 1)
                    ch.link(dve.tensor_tensor_scan(out=g8[:], data0=keep[:].rearrange("p n s -> p (n s)"),
                                                   data1=src["lf"][:, b, :], initial=0.0, op0=ALU.mult, op1=ALU.add))
                    dve.wait_ge(exps.sem, j + 1)
                    ch.tick(dve.tensor_copy(gm[:, :, 1], g8[:]))
                    ch.link(dve.tensor_copy(gmv[:, :, 1:SUB, 0], g8v[:, :, 0:SUB - 1]))
                    gmn = gm[:].rearrange("p (n s) m -> p n (s m)", s=SUB)
                    mid = g8v[:, :, SUB // 2 - 1:SUB // 2].to_broadcast([P, NS, 2 * SUB])
                    end = g8v[:, :, SUB - 1:SUB].to_broadcast([P, NS, 2 * SUB])
                    ch.tick(dve.tensor_tensor(dm[:].rearrange("p (n s) -> p n s", n=NS), gmn, mid, ALU.subtract))
                    ch.link(dve.tensor_tensor(he[:].rearrange("p (n s) -> p n s", n=NS), end, gmn, ALU.subtract))
                    dve.sem_inc(gm_ready.sem, 1)
                    ch.tick(dve.tensor_copy(vm[:, :, 1], src["v"][:, b, :]))
                    dve.wait_ge(exps.sem, j + 1 + 1)
                    dve.wait_ge(prods.sem, j + 1 + 1)
                    kk = src["k"][:, b, :].unsqueeze(2).to_broadcast([P, PT, 2])
                    aa = src["a"][:, b, :].unsqueeze(2).to_broadcast([P, PT, 2])

                    def half(t, c):
                        return t.rearrange("p (u c s) m -> p u c s m", u=PU, c=2)[:, :, c]

                    def v3(t):
                        return t.rearrange("p u (s m) -> p u s m", m=2)

                    def v3t(t):
                        return t.rearrange("p (s m) u -> p u s m", m=2)

                    def full(t):
                        return t.rearrange("p (u s) m -> p u s m", u=PU)

                    dve.tensor_tensor(v3t(rd[:, b]), full(kk), full(en[:]), ALU.mult)
                    dve.tensor_tensor(ld[:, b], aa, ep[:], ALU.mult)
                    dve.tensor_tensor(v3t(r8[:, b]), half(kk, 0), half(hh[:], 0), ALU.mult)
                    ch.link(dve.tensor_tensor(v3(l8[:, b]), half(aa, 1), half(ff[:], 1), ALU.mult))
                    gf = ff[:].rearrange("p (u t) m -> p u (t m)", u=PU)
                    gfirst, gsec = gf[:, :, CH - 1:CH], gf[:, :, MI - 1:MI]
                    if has_q:
                        qq = src["q"][:, b, :]
                        qv = qq.rearrange("p (u t) -> p u t", u=PU)
                        dve.tensor_tensor(qd[:, b], qv, ep[:, :, 1].rearrange("p (u t) -> p u t", u=PU), ALU.mult)
                        ffq = ff[:, :, 1].rearrange("p (u t) -> p u t", u=PU)
                        ch.link(dve.tensor_tensor(q8[:, b], qv[:, :, SUB:CH], ffq[:, :, SUB:CH], ALU.mult))
                    dve.sem_inc(rows_l.sem, 1)
                    dve.tensor_tensor(v3(l0[:, :, 0:CH]), half(aa, 0), half(ff[:], 0), ALU.mult)
                    dve.tensor_tensor(l0[:, :, CH:MI], l8[:, b], gfirst.to_broadcast([P, PU, CH]), ALU.mult)
                    dve.tensor_tensor(v3(re[:, :, CH:MI]), half(kk, 1), half(hh[:], 1), ALU.mult)
                    ch.link(dve.tensor_tensor(re[:, :, 0:CH], r8[:, b].rearrange("p m u -> p u m"), gsec.to_broadcast([P, PU, CH]), ALU.mult))
                    dve.wait_ge(store1[b], pair(i, p) * ST1 + 1)
                    if has_q:
                        def grouped(t):
                            return t.rearrange("p (a r) t -> p a r t", r=RC)

                        q0v = q0t[:, b].rearrange("p a t r -> p a r t")
                        dve.tensor_tensor(q0v[:, :, :, 0:SUB], grouped(qv[:, :, 0:SUB]), grouped(ffq[:, :, 0:SUB]), ALU.mult)
                        ch.tick(dve.tensor_tensor(q0v[:, :, :, SUB:CH], grouped(q8[:, b]),
                                                  grouped(gfirst.to_broadcast([P, PU, SUB])), ALU.mult))
                    dve.tensor_tensor(gam[:, b, :].unsqueeze(2), gfirst, gsec, ALU.mult)
                    if p == 0:
                        dve.wait_ge(uw.sem, 2 * NP * i + 2 + 1)
                    us = slice(p * PU, (p + 1) * PU)
                    dve.transpose(l0t[:, p].rearrange("p c u -> p u c"), l0[:])
                    dve.transpose(vtm[:, us, :].rearrange("p u c -> p (u c)"), vm[:].rearrange("p t m -> p (t m)"))
                    for a in range(RG):
                        last = dve.transpose(ret[:, b, a].rearrange("p c r -> p r c"), re[:, a * RC:(a + 1) * RC, :])
                    ch.link(last)
                    dve.sem_inc(tm_ready.sem, 1)
                    dve.sem_inc(rows_ready.sem, 1)
                    dve.sem_inc(src_free.sem, 1)
                    if has_q:
                        dve.wait_ge(prods.sem, j + 3 + 1)
                        pq = psQ[:, 0:PU * CH].rearrange("p (u t) -> p u t", u=PU)
                        pc = psQ[:, PU * CH:PU * (CH + SUB)].rearrange("p (u t) -> p u t", u=PU)
                        aqv = aq[:, b].rearrange("p a t r -> p a r t")
                        settle(dve, passed_dve)
                        ch.link(dve.copy_predicated(out=aqv, data=grouped(pq), mask=grouped(
                            qmask[:].bitcast(U32).unsqueeze(1).to_broadcast([P, PU, CH]))))
                        settle(dve, passed_dve)
                        dve.copy_predicated(out=aqv[:, :, :, SUB:CH], data=grouped(pc), mask=grouped(
                            cmask[:].bitcast(U32).unsqueeze(1).to_broadcast([P, PU, SUB])))\
                           .then_inc(aq_free.sem, 1)
                    ch.end()
                for c in range(8):
                    dve.wait_ge(lanes.sem, lanes.at(i, c + 1) + 1)
                    s0 = 4 * c
                    r0 = 0 if s0 < CH else CH
                    ps = psL[c % 2][:].rearrange("p (s h r) -> p s h r", s=4, h=HG)
                    settle(dve, passed_dve)
                    for h in range(HG):
                        last = dve.copy_predicated(
                            out=tl[:, s0:s0 + 4, h, r0:r0 + CH], data=ps[:, :, h, r0:r0 + CH],
                            mask=lmask[:, s0 - r0:s0 - r0 + 4, :].bitcast(U32))
                    last.then_inc(lanes_free.sem, 1)
                dve.wait_ge(lanes_free.sem, lanes_free.at(i, 12 + 1) + 1)
                dve.sem_inc(mats.sem, 1)
                solve(dve, i, dve_solve, tmpd, 0, HD_DVE)

        @block.tensor
        def _(pe):
            pe.wait_ge(setup, 2 + 1)
            with pe.Fori(0, turns) as i:
                for p in range(NP):
                    j = i * NP + p
                    b = p % 2
                    pe.wait_ge(rows_l.sem, j + 1 + 1)
                    pe.wait_ge(bdr_in[b], (pair(i, p) + 1) * (2 * HG * 16) + 1)
                    pe.wait_ge(prods_free.sem, j + 1)
                    if has_q:
                        pe.wait_ge(aq_free.sem, j + 1)
                    ldv = ld[:, b].rearrange("p (u s) m -> p u (s m)", u=PU)
                    for u in range(PU):
                        right = bd1[:, b, :, :, u].rearrange("p h m -> p (h m)")
                        across = bd2[:, b, :, :, u].rearrange("p h m -> p (h m)")
                        last = nc.tensor.matmul(psD[b][:, u * MI:(u + 1) * MI], right, ldv[:, u, :], start=True, stop=True)
                        if has_q:
                            last = nc.tensor.matmul(psQ[:, u * CH:(u + 1) * CH], right, qd[:, b, u, :], start=True, stop=True)
                        o = b * 256 + u * CH
                        last = nc.tensor.matmul(psC[:, o:o + CH], across, l8[:, b, u, :], start=True, stop=True)
                        if has_q:
                            o = PU * CH + u * SUB
                            last = nc.tensor.matmul(psQ[:, o:o + SUB], across, q8[:, b, u, :], start=True, stop=True)
                    last.then_inc(prods.sem, 1)
                pe.wait_ge(prods_free.sem, (i + 1) * NP + 1 + 1)
                bank = 0
                for buf, ns in ((dst, MI), (cst, CH)):
                    for s0 in range(0, ns, 4):
                        pe.wait_ge(lanes_free.sem, lanes_free.at(i, bank) + 1)
                        for s in range(4):
                            last = nc.tensor.transpose(psL[bank % 2][:, s * P:(s + 1) * P], buf[:, :, s0 + s], ident[:])
                        last.then_inc(lanes.sem, 1)
                        bank += 1
                pe.wait_ge(solved.sem, solved.at(i, 2) + 1)
                for s0 in range(0, MI, 4):
                    pe.wait_ge(lanes_free.sem, lanes_free.at(i, bank) + 1)
                    for s in range(4):
                        last = nc.tensor.transpose(psL[bank % 2][:, s * P:(s + 1) * P],
                                                   tl[:, s0 + s].rearrange("p h r -> p (h r)"), ident[:])
                    last.then_inc(lanes.sem, 1)
                    bank += 1
                assert bank == NL
                for p in range(NP):
                    j = i * NP + p
                    b = p % 2
                    pe.wait_ge(bdt_in[b], (pair(i, p) + 1) * (2 * HG * 16) + 1)
                    pe.wait_ge(uw_free.sem, 2 * j + 1)
                    for u in range(PU):
                        last = nc.tensor.matmul(psW[0][:, u * HD:(u + 1) * HD], bd1[:, b, :, :, u].rearrange("p h m -> p (h m)"),
                                                vtm[:, p * PU + u, :], start=True, stop=True)
                    last.then_inc(uw.sem, 1)
                    pe.wait_ge(uw_free.sem, 2 * j + 1 + 1)
                    wt = psW[1][:].rearrange("p (a m r) -> p a r m", a=RG, r=RC)
                    for u in range(PU):
                        last = nc.tensor.matmul(wt[:, u // RC, u % RC, :], bd3[:, b, :, :, u].rearrange("p h m -> p (h m)"),
                                                ttr[:, p, :, u], start=True, stop=True)
                    last.then_inc(uw.sem, 1)



def chain_states(nc, sems, ctx, scratch):
    def sb(name, shape, dt=F32):
        return ctx.enter_context(nc.sbuf_tensor(f"s_{name}", shape, dt))

    def sem(name):
        return sems.new(nc, f"s_{name}")

    bdw = sb("bdw", [P, 2, NG, HG, MI * RC])
    bdr = sb("bdr", [P, 2, NG, HG, HD * RC])
    bdq = sb("bdq", [P, 2, NG, HG, CH * RC])
    bda = sb("bda", [P, 2, NG, HG, CH * RC])
    u = sb("u", [P, 2, NG, RC, HD])
    gam = sb("gam", [P, 2, NG, RC])
    S = sb("S", [P, 2, NG, HD])
    X = sb("X", [P, 2, NG, HD])
    GS = sb("GS", [P, NG, HD])
    osb = sb("osb", [HG * CH, 2, RC, NG * HD])
    psX = ctx.enter_context(nc.psum_tensor("s_psX", [P, 512], F32))
    psS = ctx.enter_context(nc.psum_tensor("s_psS", [P, 512], F32))
    psO = [ctx.enter_context(nc.psum_tensor(f"s_psO{i}", [P, 512], F32)) for i in range(2)]
    zeroed = sem("zeroed")
    in_m, in_q = ([sem(f"{m}{b}") for b in range(2)] for m in ("chunk_operands_in", "output_operands_in"))
    used = sem("operands_used")
    x_full, x_done, s_full, s_done = sem("x_product"), sem("x_ready"), sem("s_product"), sem("s_ready")
    g_done = sem("decayed")
    o_full, o_read = sem("o_product"), sem("o_read")
    o_out = [sem(f"o_stored{b}") for b in range(2)]
    LM = (2 * HG + 2) * 16
    LQ = 2 * HG * 16

    GQ = UN // RC
    cut = (QCH0 - 2 * UN) // RC
    segments = [(0, 0, GQ, False), (1, 0, GQ, False), (2, 0, cut, False), (2, cut, GQ, True), (3, 0, GQ, True)]

    def groups(eng, body):
        n0, o0 = 0, 0
        for q, a, b, out in segments:
            assert (b - a) % 2 == 0
            with eng.Fori(0, (b - a) // 2) as i:
                for par in range(2):
                    body(q, i * 2 + (a + par), i + n0 // 2, i + o0 // 2, par, out)
            n0 += b - a
            o0 += (b - a) if out else 0
        return n0, o0

    def groups_act(eng, body):
        n0, o0 = 0, 0
        for q, a, b, out in segments:
            if out:
                with eng.Fori(0, (b - a) // 2) as i:
                    for par in range(2):
                        body(q, i * 2 + (a + par), i + n0 // 2, i + o0 // 2, par, out)
            n0 += b - a
            o0 += (b - a) if out else 0
        return n0, o0

    def chunk(t, c):
        return t.rearrange("p h (m r) -> p (h m) r", r=RC)[:, :, c]

    passed_sp, passed_dve, passed_pool = (sem(f"passed_{e}") for e in ("sp", "dve", "pool"))
    sems.prime(nc)

    with nc.Block() as block:
        @block.gpsimd
        def _(pool):
            for t in (bdw, bdr, bdq, bda, S):
                pool.memset(t[:], 0.0).then_inc(zeroed, 1)

        @block.sync
        def _(sp):
            sp.wait_ge(zeroed, 5 + 1)

            def body(q, g0, n2, no2, par, out):
                n, no = n2 * 2 + par, no2 * 2 + par
                c0 = g0 * RC
                sp.wait_ge(used, n + 1)
                settle(sp, passed_sp)
                us = bass.ds(c0, RC)
                ug = bass.ds(g0, 1)
                gs = slice(q * NG, (q + 1) * NG)
                for h in range(HG):
                    r = slice(h * HD, (h + 1) * HD)
                    sp.dma_start(bdw[r, par, :, h], scratch["WT"][gs, r, ug, :].rearrange("g p u c -> p g (u c)")).then_inc(in_m[par], 16)
                    sp.dma_start(bdr[r, par, :, h], scratch["R"][gs, r, ug, :].rearrange("g p u c -> p g (u c)")).then_inc(in_m[par], 16)
                sp.dma_start(u[:, par], scratch["U"][gs, :, us, :].rearrange("g p u c -> p g u c")).then_inc(in_m[par], 16)
                sp.dma_start(gam[:, par], scratch["gam"][gs, :, us].rearrange("g p u -> p g u")).then_inc(in_m[par], 16)
                if out:
                    for h in range(HG):
                        r = slice(h * HD, (h + 1) * HD)
                        sp.dma_start(bdq[r, par, :, h], scratch["q0"][gs, r, ug, :].rearrange("g p u c -> p g (u c)")).then_inc(in_q[par], 16)
                        sp.dma_start(bda[r, par, :, h], scratch["Aq"][gs, r, ug, :].rearrange("g p u c -> p g (u c)")).then_inc(in_q[par], 16)

            groups(sp, body)

        @block.scalar
        def _(act):
            act.sem_inc(o_read, 1)

            def body(q, g0, n2, no2, par, out):
                n, no = n2 * 2 + par, no2 * 2 + par
                c0 = g0 * RC
                if not out:
                    return
                act.wait_ge(o_out[par], no2 * (HG * 16) + 1)
                for c in range(RC):
                    act.wait_ge(o_full, no * RC + c + 1 + 1)
                    act.activation(osb[:, par, c, :], psO[c % 2][0:HG * CH, 0:NG * HD], ACT.Copy).then_inc(o_read, 1)
                act.wait_ge(o_read, no * RC + RC + 1 + 1)
                t0 = c0 * CH + q * QT
                for h in range(HG):
                    dst = scratch["o"][h, bass.ds(t0, RC * CH), :].rearrange("(c t) x -> t c x", t=CH)
                    act.dma_start(dst, osb[h * CH:(h + 1) * CH, par])\
                       .then_inc(o_out[par], 16)

            _, no = groups_act(act, body)
            for par in range(2):
                act.wait_ge(o_out[par], no // 2 * HG * 16 + 1)

        @block.vector
        def _(dve):
            dve.wait_ge(zeroed, 5 + 1)
            dve.sem_inc(used, 1)
            dve.sem_inc(s_done, 1)

            def body(q, g0, n2, no2, par, out):
                n, no = n2 * 2 + par, no2 * 2 + par
                c0 = g0 * RC
                dve.wait_ge(in_m[par], n2 * LM + LM + 1)
                for c in range(RC):
                    m = n * RC + c
                    a, b = c % 2, (c + 1) % 2
                    dve.wait_ge(s_done, m + 1 + 1)
                    if out:
                        dve.wait_ge(o_full, no * RC + c - 1 + 1) if c else dve.wait_ge(o_read, no * RC + 1)
                    dve.tensor_tensor(GS[:], S[:, a], gam[:, par, :, c:c + 1].to_broadcast([P, NG, HD]), ALU.mult)\
                       .then_inc(g_done, 1)
                    dve.wait_ge(x_full, m + 1 + 1)
                    dve.tensor_tensor(X[:, a], u[:, par, :, c, :], psX[:, 0:P].rearrange("p (g v) -> p g v", g=NG),
                                      ALU.add).then_inc(x_done, 1)
                    dve.wait_ge(g_done, m + 1 + 1)
                    dve.wait_ge(s_full, m + 1 + 1)
                    dve.tensor_tensor(S[:, b], GS[:], psS[:, 0:P].rearrange("p (g v) -> p g v", g=NG),
                                      ALU.add).then_inc(s_done, 1)
                if out:
                    dve.wait_ge(o_full, no * RC + RC + 1)
                dve.wait_ge(s_done, n * RC + RC + 1 + 1)
                dve.sem_inc(used, 1)

            groups(dve, body)

        @block.tensor
        def _(pe):
            pe.wait_ge(zeroed, 5 + 1)

            def body(q, g0, n2, no2, par, out):
                n, no = n2 * 2 + par, no2 * 2 + par
                c0 = g0 * RC
                pe.wait_ge(in_m[par], n2 * LM + LM + 1)
                if out:
                    pe.wait_ge(in_q[par], no2 * LQ + LQ + 1)
                for c in range(RC):
                    m = n * RC + c
                    a = c % 2
                    pe.wait_ge(s_done, m + 1 + 1)
                    for g in range(NG):
                        last = nc.tensor.matmul(psX[:, g * HD:(g + 1) * HD], chunk(bdw[:, par, g], c), S[:, a, g, :],
                                                start=True, stop=True)
                    last.then_inc(x_full, 1)
                    pe.wait_ge(x_done, m + 1 + 1)
                    for g in range(NG):
                        last = nc.tensor.matmul(psS[:, g * HD:(g + 1) * HD], chunk(bdr[:, par, g], c), X[:, a, g, :],
                                                start=True, stop=True)
                    last.then_inc(s_full, 1)
                    if out:
                        pe.wait_ge(o_read, no * RC + c + 1)
                        for g in range(NG):
                            ps = psO[c % 2][0:HG * CH, g * HD:(g + 1) * HD]
                            nc.tensor.matmul(ps, chunk(bdq[:, par, g], c), S[:, a, g, :], start=True, stop=False)
                            last = nc.tensor.matmul(ps, chunk(bda[:, par, g], c), X[:, a, g, :], start=False, stop=True)
                        last.then_inc(o_full, 1)

            groups(pe, body)


def finish(nc, sems, ctx, consts, scratch, x_r, out_r, Wo1_d, Wo2_d, lnw_d, Wout_d):
    def sb(name, shape, dt=F32):
        return ctx.enter_context(nc.sbuf_tensor(f"f_{name}", shape, dt))

    def sem(name):
        return sems.new(nc, f"f_{name}")

    ident = consts["ident"]
    wout, wo1, wo2 = sb("wout", [P, KD, D]), sb("wo1", [P, KD, HD]), sb("wo2", [HD, D])
    lnw = sb("lnw", [P, D])
    o, x, r = sb("o", [P, 2, D]), sb("x", [P, 2, D]), sb("r", [P, 2, D])
    xn, xnT, yn, ynT = sb("xn", [P, D]), sb("xnT", [P, KD, P]), sb("yn", [P, D]), sb("ynT", [P, KD, P])
    g1, gate, res = sb("g1", [HD, P]), sb("gate", [P, D]), sb("res", [P, 2, D])
    st, mv, ve, lnv, rs, nt = (sb(m, [P, c]) for m, c in
                               (("st", 6), ("mv", 2), ("ve", 1), ("lnv", 1), ("rs", 1), ("nt", 1)))
    psT, psG1, psG, psY, psO = (ctx.enter_context(nc.psum_tensor(f"f_ps{m}", [P, 512], F32))
                                for m in ("T", "G1", "G", "Y", "O"))
    loaded, rows_in, stored = (sem("weights_loaded"), [sem(f"rows_in{b}") for b in range(2)],
                               [sem(f"rows_stored{b}") for b in range(2)])
    var_r, rs_r = sem("var_ready"), sem("rs_ready")
    xn_r, xT_f, xT_r, g1_f, g1_r, g_f, g_r = (sem(m) for m in ("xn", "xT_full", "xT", "g1_full", "g1", "gate_full", "gate"))
    yn_r, yT_f, yT_r, o_f, res_r = (sem(m) for m in ("yn", "yT_full", "yT", "o_full", "res"))
    dve_self, act_self = sem("dve_steps"), sem("act_steps")
    full, tail = divmod(NOUT, P)
    assert full % 2 == 1

    def tiles(eng, body):
        with eng.Fori(0, full // 2) as i:
            for par in range(2):
                body(i, (i * 2 + par) * P, par, P)
        body(full // 2, (full - 1) * P, 0, P)
        body(full // 2, full * P, 1, tail)

    passed_sp, passed_dve, passed_pool = (sem(f"passed_{e}") for e in ("sp", "dve", "pool"))
    sems.prime(nc)

    with nc.Block() as block:
        @block.sync
        def _(sp):
            sp.dma_start(wo1[:], Wo1_d.rearrange("(k p) n -> p k n", p=P)).then_inc(loaded, 16)
            for g in range(NG):
                sp.dma_start(wout[g * HD:(g + 1) * HD], Wout_d[g * P:(g + 1) * P, :].rearrange("(h v) n -> v h n", h=HG)).then_inc(loaded, 16)
            for h in range(HG):
                sp.dma_start(wo2[:, h * P:(h + 1) * P].rearrange("r (g v) -> r g v", g=NG),
                             Wo2_d.rearrange("r (g h v) -> r h g v", g=NG, h=HG)[:, h]).then_inc(loaded, 16)
                sp.dma_start(lnw[:, h * P:(h + 1) * P].rearrange("p (g v) -> p g v", g=NG),
                             lnw_d.rearrange("(a g h v) -> a h g v", a=1, g=NG, h=HG)[:, h].to_broadcast([P, NG, HD])).then_inc(loaded, 16)

            def body(n2, i0, par, rows):
                n = n2 * 2 + par
                sp.wait_ge(res_r, n + 1)
                settle(sp, passed_sp)
                sp.dma_start(o[0:rows, par].rearrange("p (h x) -> p h x", h=HG),
                             scratch["o"][:, bass.ds(i0 + OUT0, rows), :].rearrange("h t x -> t h x")).then_inc(rows_in[par], 16)
                for dst, src in ((x, x_r), (r, out_r)):
                    sp.dma_start(dst[0:rows, par], src[bass.ds(i0 * 3 + 1, 3 * rows - 2), :][0:3 * rows - 2:3, :])\
                      .then_inc(rows_in[par], 16)

            tiles(sp, body)

        @block.scalar
        def _(act):
            def rsqrt(k, rows):
                act.wait_ge(var_r, k + 1 + 1)
                act.activation(lnv[0:rows], ve[0:rows], ACT.Ln).then_inc(act_self, 1)
                act.wait_ge(act_self, k + 1 + 1)
                act.activation(rs[0:rows], lnv[0:rows], ACT.Exp, scale=-0.5).then_inc(rs_r, 1)

            def body(n2, i0, par, rows):
                n = n2 * 2 + par
                rsqrt(n * 2, rows)
                act.wait_ge(xT_f, n + 1 + 1)
                act.activation(xnT[:, :, 0:rows], psT[:].rearrange("p (k t) -> p k t", k=KD)[:, :, 0:rows], ACT.Copy).then_inc(xT_r, 1)
                act.wait_ge(g1_f, n + 1 + 1)
                act.activation(g1[:, 0:rows], psG1[0:HD, 0:rows], ACT.Copy).then_inc(g1_r, 1)
                act.wait_ge(g_f, n + 1 + 1)
                act.activation(gate[0:rows], psG[0:rows], ACT.Sigmoid).then_inc(g_r, 1)
                rsqrt(n * 2 + 1, rows)
                act.wait_ge(yT_f, n + 1 + 1)
                act.activation(ynT[:, :, 0:rows], psY[:].rearrange("p (k t) -> p k t", k=KD)[:, :, 0:rows], ACT.Copy).then_inc(yT_r, 1)
                act.wait_ge(res_r, n + 2 + 1)
                act.dma_start(out_r[bass.ds(i0 * 3 + 1, 3 * rows - 2), :][0:3 * rows - 2:3, :], res[0:rows, par])\
                   .then_inc(stored[par], 16)

            tiles(act, body)
            for par in range(2):
                act.wait_ge(stored[par], (full + 1) // 2 * 16 + 1)

        @block.vector
        def _(dve):
            dve.wait_ge(loaded, (1 + NG + 2 * HG) * 16 + 1)
            dve.sem_inc(res_r, 1)

            def norm(ch, k, src, dst, rows, done):
                ch.link(dve.bn_stats(st[0:rows], src))
                settle(dve, passed_dve)
                ch.link(dve.bn_aggr(mv[0:rows], st[0:rows]))
                ch.link(dve.tensor_scalar(ve[0:rows], mv[0:rows, 1:2], LN_EPS, None, ALU.add))
                dve.sem_inc(var_r, 1)
                dve.wait_ge(rs_r, k + 1 + 1)
                ch.link(dve.tensor_tensor(nt[0:rows], rs[0:rows], rs[0:rows], ALU.mult))
                ch.link(dve.tensor_tensor(nt[0:rows], nt[0:rows], ve[0:rows], ALU.mult))
                ch.link(dve.tensor_scalar(nt[0:rows], nt[0:rows], -0.5, 1.5, ALU.mult, ALU.add))
                ch.link(dve.tensor_tensor(rs[0:rows], nt[0:rows], rs[0:rows], ALU.mult))
                return dve.tensor_scalar(dst, src, mv[0:rows, 0:1], rs[0:rows], ALU.subtract, ALU.mult)

            def body(n2, i0, par, rows):
                n = n2 * 2 + par
                ch = Chain(dve, dve_self, n, 7 + 1 + 7 + 1)
                dve.wait_ge(rows_in[par], n2 * 48 + 48 + 1)
                norm(ch, n * 2, x[0:rows, par], xn[0:rows], rows, xn_r).then_inc(xn_r, 1)
                dve.wait_ge(g_r, n + 1 + 1)
                ch.link(dve.tensor_tensor(o[0:rows, par], o[0:rows, par], gate[0:rows], ALU.mult))
                ch.link(norm(ch, n * 2 + 1, o[0:rows, par], yn[0:rows], rows, None))
                dve.tensor_tensor(yn[0:rows], yn[0:rows], lnw[0:rows], ALU.mult).then_inc(yn_r, 1)
                dve.wait_ge(o_f, n + 1 + 1)
                dve.wait_ge(stored[par], n2 * 16 + 1)
                dve.tensor_tensor(res[0:rows, par], psO[0:rows], r[0:rows, par], ALU.add).then_inc(res_r, 1)
                ch.end()

            tiles(dve, body)

        @block.tensor
        def _(pe):
            pe.wait_ge(loaded, (1 + NG + 2 * HG) * 16 + 1)

            def body(n2, i0, par, rows):
                n = n2 * 2 + par
                pe.wait_ge(xn_r, n + 1 + 1)
                for kd in range(KD):
                    last = nc.tensor.transpose(psT[:, kd * P:kd * P + rows], xn[0:rows, kd * P:(kd + 1) * P], ident[0:rows, 0:rows])
                last.then_inc(xT_f, 1)
                pe.wait_ge(xT_r, n + 1 + 1)
                for kd in range(KD):
                    last = nc.tensor.matmul(psG1[0:HD, 0:rows], wo1[:, kd, :], xnT[:, kd, 0:rows], start=(kd == 0), stop=(kd == KD - 1))
                last.then_inc(g1_f, 1)
                pe.wait_ge(g1_r, n + 1 + 1)
                nc.tensor.matmul(psG[0:rows], g1[:, 0:rows], wo2[:], start=True, stop=True).then_inc(g_f, 1)
                pe.wait_ge(yn_r, n + 1 + 1)
                for kd in range(KD):
                    last = nc.tensor.transpose(psY[:, kd * P:kd * P + rows], yn[0:rows, kd * P:(kd + 1) * P], ident[0:rows, 0:rows])
                last.then_inc(yT_f, 1)
                pe.wait_ge(yT_r, n + 1 + 1)
                for kd in range(KD):
                    last = nc.tensor.matmul(psO[0:rows], ynT[:, kd, 0:rows], wout[:, kd, :], start=(kd == 0), stop=(kd == KD - 1))
                last.then_inc(o_f, 1)

            tiles(pe, body)


_INS = ["L0_attn_x", "L0_attn_Wq", "L0_attn_Wk", "L0_attn_Wv", "L0_attn_Wf1", "L0_attn_Wf2", "L0_attn_Wg",
        "L0_attn_Wo1", "L0_attn_Wo2", "L0_attn_ln_w", "L0_attn_Wout", "L0_ffn_kernel", "L0_ffn_input_scale",
        "L0_ffn_kernel_scale", "L0_ffn_bias"]


def kernel(**inputs):
    import numpy as _np
    import concourse.bacc as _bacc
    from concourse import mybir as _mybir
    from concourse.bass_utils import run_bass_kernel_spmd as _run

    nc = _bacc.Bacc("TRN2", target_bir_lowering=False, num_devices=1)
    arrays, args = {}, []
    for name in _INS:
        a = _np.ascontiguousarray(inputs[name])
        arrays[f"in_{name}"] = a
        args.append(nc.dram_tensor(f"in_{name}", a.shape, _mybir.dt.from_np(a.dtype), kind="ExternalInput").ap())
    out = nc.dram_tensor("out", (1, T, D), F32, kind="ExternalOutput").ap()
    program(nc, *args, out)
    r = _run(nc, [arrays], core_ids=[0])
    return r.results[0]["out"]
```

```python
import concourse.bass as bass
from concourse import mybir
from contextlib import ExitStack

F32 = mybir.dt.float32
BF16 = mybir.dt.bfloat16
U32 = mybir.dt.uint32
ALU = mybir.AluOpType
ACT = mybir.ActivationFunctionType

P = 128
T = 8192
D = 512
KD = D // P
HD = 32
H = D // HD
NG = D // P
HG = H // NG
CH = 16
SUB = CH // 2
MI = 2 * CH
NCH = T // CH
BT = 512
QT = 2048
NQ = T // QT
UN = QT // CH
PT = 256
PU = PT // CH
NP = QT // PT
RC = 8
OUT0 = (2 * T) // 3
NOUT = T - OUT0
QCH0 = (OUT0 // (CH * RC)) * RC
OT0 = QCH0 * CH
NSRC = 5
RGAM = HD * RC
RQ0 = RGAM + RC
RAQ = RQ0 + CH * RC
RW = RAQ + CH * RC
LN_EPS = 1e-5
NORM_EPS = 1e-12
ZMIN = -21.0
assert UN == P and (2 * T + 1) % 3 == 2


class Count:

    def __init__(self, sem, per):
        self.sem, self.per = sem, per

    def at(self, n, c):
        return n * self.per + c


class Chain:

    def __init__(self, eng, sem, n, per):
        self.eng, self.sem, self.n, self.per, self.c = eng, sem, n, per, 0

    def tick(self, ins):
        self.c += 1
        ins.then_inc(self.sem, 1)
        return self.c

    def wait(self, c=None):
        self.eng.wait_ge(self.sem, self.n * self.per + (self.c if c is None else c) + 1)

    def link(self, ins):
        self.tick(ins)
        self.wait()

    def end(self):
        assert self.c == self.per, (self.c, self.per)


class Semaphores(list):

    def new(self, nc, name):
        self.append(nc.alloc_semaphore(name=name))
        return self[-1]

    def prime(self, nc):
        with nc.Block() as block:
            @block.gpsimd
            def _(pool):
                for s in self:
                    pool.sem_inc(s, 1)

    def clear(self, nc):
        nc.clear_and_free_semaphores(self)
        nc.all_engine_barrier()


def settle(eng, passed):
    eng.sem_inc(passed, 1)


def program(nc, x_d, Wq_d, Wk_d, Wv_d, Wf1_d, Wf2_d, Wg_d, Wo1_d, Wo2_d, lnw_d, Wout_d,
            kern_d, sin_d, sk_d, bias_d, out_d):
    x_r = x_d.rearrange("a t d -> (a t) d")
    out_r = out_d.rearrange("a t d -> (a t) d")
    scratch = {m: nc.dram_tensor(f"{m}_scr", shape, F32).ap() for m, shape in dict(
        src=(NQ * NG, P, NSRC, QT),
        rec=(NQ * NG, P, UN // RC, RW),
        lv=(NQ * NG, P, NP, 2 * PU * MI),
        uw=(NQ * NG, P, UN // RC, 2 * HD * RC),
        o=(HG, T, NG * HD),
    ).items()}
    with ExitStack() as top:
        consts = make_constants(nc, top)

        def phase(run, *args):
            sems = Semaphores()
            with ExitStack() as ctx:
                run(nc, sems, ctx, *args)
            sems.clear(nc)

        for has_q, q0, q1 in ((False, 0, 2), (True, 2, NQ)):
            phase(project, consts, scratch, x_r, out_r, Wq_d, Wk_d, Wv_d, Wf1_d, Wf2_d, Wg_d,
                  kern_d, sin_d, sk_d, bias_d, has_q, q0, q1)
        phase(chunks, consts, scratch)
        phase(chain_states, scratch)
        phase(finish, consts, scratch, x_r, out_r, Wo1_d, Wo2_d, lnw_d, Wout_d)


def make_constants(nc, top):
    ident = top.enter_context(nc.sbuf_tensor("ident", [P, P], F32))
    ones_bd = top.enter_context(nc.sbuf_tensor("ones_bd", [P, HG, HD], F32))
    spread = top.enter_context(nc.sbuf_tensor("spread", [H, NG, HG, HD], F32))
    made = top.enter_context(nc.semaphore("consts_made"))
    with nc.Block() as block:
        @block.gpsimd
        def _(pool):
            pool.memset(ident[:], 0.0).then_inc(made, 1)
            pool.memset(ones_bd[:], 1.0).then_inc(made, 1)
            pool.memset(spread[:], 0.0).then_inc(made, 1)
            pool.wait_ge(made, 3)
            pool.affine_select(out=ident[:], in_=ident[:], compare_op=ALU.not_equal, fill=1.0,
                               base=0, pattern=[[-1, P]], channel_multiplier=1).then_inc(made, 1)
            pool.affine_select(out=ones_bd[:], in_=ones_bd[:], compare_op=ALU.is_ge, fill=0.0,
                               base=0, pattern=[[-HD, HG], [0, HD]], channel_multiplier=1).then_inc(made, 1)
            pool.affine_select(out=spread[:], in_=spread[:], compare_op=ALU.not_equal, fill=-1.0,
                               base=0, pattern=[[-HG, NG], [-1, HG], [0, HD]],
                               channel_multiplier=1).then_inc(made, 1)
            pool.wait_ge(made, 6)
            pool.affine_select(out=ones_bd[:], in_=ones_bd[:], compare_op=ALU.is_ge, fill=0.0,
                               base=HD - 1, pattern=[[HD, HG], [0, HD]], channel_multiplier=-1).then_inc(made, 1)
            pool.wait_ge(made, 7)
    return dict(ident=ident, ones_bd=ones_bd, spread=spread)


EXP_BITS = 0x7F800000
FP8_MIN = 2.0 ** -6
FP8_MAGIC = 1.5 * 2.0 ** 20


def project(nc, sems, ctx, consts, scratch, x_r, out_r, Wq_d, Wk_d, Wv_d, Wf1_d, Wf2_d, Wg_d,
            kern_d, sin_d, sk_d, bias_d, has_q, q0, q1):
    tag = "pq" if has_q else "p"

    def sb(name, shape, dt=F32):
        return ctx.enter_context(nc.sbuf_tensor(f"{tag}_{name}", shape, dt))

    def sem(name):
        return sems.new(nc, f"{tag}_{name}")

    NT = BT // P
    NB = QT // BT
    ident, ones_bd, spread = consts["ident"], consts["ones_bd"], consts["spread"]
    wk, wv = sb("wk", [P, KD, D]), sb("wv", [P, KD, D])
    wq = sb("wq", [P, KD, D]) if has_q else None
    wf1, wf2, wg = sb("wf1", [P, KD, HD]), sb("wf2", [HD, D]), sb("wg", [P, KD, H])
    kraw, kq = sb("kraw", [P, KD, D], BF16), sb("kq", [P, KD, D], BF16)
    bias = sb("bias", [P, D], BF16)
    scal = sb("scal", [P, 4])
    rsc = sb("rsc", [P, 2])
    osc = sb("osc", [P, 1])
    x = sb("x", [P, 2, NT, D])
    xn = sb("xn", [P, NT, D])
    xnT = sb("xnT", [P, 2, KD, BT])
    st, mv = sb("st", [P, NT, 6]), sb("mv", [P, NT, 2])
    ve, lnv, rs, nt = sb("ve", [P, NT]), sb("lnv", [P, NT]), sb("rs", [P, NT]), sb("nt", [P, NT])
    vq, cq = sb("vq", [P, KD, BT]), sb("cq", [P, KD, BT])
    xb, xq = sb("xb", [P, KD, BT], BF16), sb("xq", [P, KD, BT], BF16)
    f1 = sb("f1", [HD, BT])
    yg, bg, beta = sb("yg", [H, BT]), sb("bg", [H, BT]), sb("beta", [H, BT])
    kr, k2, kn, av = (sb(n, [P, NG, BT]) for n in ("kr", "k2", "kn", "av"))
    vt, z, lz = (sb(n, [P, NG, BT]) for n in ("vt", "z", "lz"))
    qt = sb("qt", [P, NG, BT]) if has_q else None
    kss = sb("kss", [P, NG, BT])
    yb = sb("yb", [P, NT, D], BF16)
    yo = sb("yo", [P, NT, D])
    nscale = sb("nscale", [P, 1])
    psA = [ctx.enter_context(nc.psum_tensor(f"{tag}_psA{i}", [P, 512], F32)) for i in range(4)]
    psD = [ctx.enter_context(nc.psum_tensor(f"{tag}_psD{i}", [P, 512], F32)) for i in range(4)]

    JA = 4 + 2 + 4 + 4 + (4 if has_q else 0) + 4
    JD = 12
    NLOAD = 11 if has_q else 10
    loaded = sem("weights_loaded")
    x_in = [sem(f"x_in{b}") for b in range(2)]
    setup = sem("setup")
    kern_ready = sem("kern_ready")
    act_psum = Count(sem("act_psum_full"), JA)
    act_free = Count(sem("act_psum_free"), JA)
    dve_psum = Count(sem("dve_psum_full"), JD)
    dve_free = Count(sem("dve_psum_free"), JD)
    var_ready = Count(sem("var_ready"), 1)
    rs_raw = Count(sem("rs_raw"), 1)
    xn_ready = Count(sem("xn_ready"), NT)
    xnT_ready = Count(sem("xnT_ready"), 1)
    v_scaled = Count(sem("v_scaled"), 1)
    cq_ready = Count(sem("magic_ready"), 1)
    xq_ready = Count(sem("xq_ready"), 1)
    k_sq = Count(sem("k_squared"), 1)
    kss_ready = Count(sem("k_sumsq_ready"), 1)
    rn_ready = Count(sem("k_rnorm_ready"), 1)
    kn_ready = Count(sem("kn_ready"), 1)
    z_ready = Count(sem("z_ready"), 1)
    lz_ready = Count(sem("log_z_ready"), 1)
    lf_ready = Count(sem("lf_ready"), 1)
    bln_ready = Count(sem("beta_log_ready"), 1)
    blm_ready = Count(sem("beta_arg_ready"), 1)
    beta_ready = Count(sem("beta_ready"), 1)
    a_ready = Count(sem("a_ready"), 1)
    silu_k = Count(sem("silu_k_ready"), 1)
    silu_v = Count(sem("silu_v_ready"), 1)
    silu_q = Count(sem("silu_q_ready"), 1)
    yb_ready = Count(sem("ffn_ready"), NT)
    yo_ready = Count(sem("rows_ready"), NT)
    stored_y = sem("stored_rows")
    stored_k, stored_a, stored_v, stored_lf, stored_q = (sem(f"stored_{n}") for n in ("k", "a", "v", "lf", "q"))
    act_self, dve_self, pool_self = sem("act_steps"), sem("dve_steps"), sem("pool_steps")
    kern_steps = sem("kernel_steps")
    turns = q1 - q0

    passed_sp, passed_dve, passed_pool = (sem(f"passed_{e}") for e in ("sp", "dve", "pool"))
    sems.prime(nc)

    with nc.Block() as block:
        def store_block(sp, i, s):
            n = i * NB + s
            it = (i + q0) * NG
            cols = slice(s * BT, (s + 1) * BT)
            sp.wait_ge(silu_v.sem, silu_v.at(n, 1) + 1)
            settle(sp, passed_sp)
            sp.dma_start(scratch["src"][bass.ds(it, NG), :, 2, cols].rearrange("g p t -> p g t"), vt[:]).then_inc(stored_v, 16)
            if has_q:
                sp.wait_ge(silu_q.sem, silu_q.at(n, 1) + 1)
                settle(sp, passed_sp)
                sp.dma_start(scratch["src"][bass.ds(it, NG), :, 4, cols].rearrange("g p t -> p g t"), qt[:]).then_inc(stored_q, 16)
            sp.wait_ge(lf_ready.sem, lf_ready.at(n, 1) + 1)
            settle(sp, passed_sp)
            sp.dma_start(scratch["src"][bass.ds(it, NG), :, 3, cols].rearrange("g p t -> p g t"), z[:]).then_inc(stored_lf, 16)
            sp.wait_ge(kn_ready.sem, kn_ready.at(n, 1) + 1)
            settle(sp, passed_sp)
            sp.dma_start(scratch["src"][bass.ds(it, NG), :, 0, cols].rearrange("g p t -> p g t"), kn[:]).then_inc(stored_k, 16)
            sp.wait_ge(a_ready.sem, a_ready.at(n, 1) + 1)
            settle(sp, passed_sp)
            sp.dma_start(scratch["src"][bass.ds(it, NG), :, 1, cols].rearrange("g p t -> p g t"), av[:]).then_inc(stored_a, 16)
            sp.wait_ge(yo_ready.sem, yo_ready.at(n, 2 * NT) + 1)
            settle(sp, passed_sp)
            row = (i * NB + (q0 * NB + s)) * BT
            sp.dma_start(out_r[bass.ds(row, BT), :].rearrange("(j p) d -> p j d", p=P), yo[:]).then_inc(stored_y, 16)

        @block.sync
        def _(sp):
            for dst, src in ((wk, Wk_d), (wv, Wv_d), (wf1, Wf1_d), (wg, Wg_d), (kraw, kern_d)) \
                    + (((wq, Wq_d),) if has_q else ()):
                sp.dma_start(dst[:], src.rearrange("(k p) n -> p k n", p=P)).then_inc(loaded, 16)
            sp.dma_start(wf2[:], Wf2_d).then_inc(loaded, 16)
            sp.dma_start(bias[:], bias_d.rearrange("(a n) -> a n", a=1).to_broadcast([P, D])).then_inc(loaded, 16)
            for c, s in ((0, sin_d), (1, sk_d)):
                sp.dma_start(scal[:, c:c + 1], s.rearrange("(a n) -> a n", a=1).to_broadcast([P, 1])).then_inc(loaded, 16)
            sp.dma_start(scal[:, 2:3], sin_d.rearrange("(a n) -> a n", a=1).to_broadcast([P, 1])).then_inc(loaded, 16)
            with sp.Fori(0, turns) as i:
                for s in range(NB):
                    n = i * NB + s
                    sp.wait_ge(yo_ready.sem, n * NT + 1)
                    settle(sp, passed_sp)
                    row = (i * NB + (q0 * NB + s)) * BT
                    sp.dma_start(x[:, s % 2, :, :],
                                 x_r[bass.ds(row, BT), :].rearrange("(j p) d -> p j d", p=P)).then_inc(x_in[s % 2], 16)
                    if s > 0:
                        store_block(sp, i, s - 1)
                store_block(sp, i, NB - 1)
            for sm in (stored_y, stored_k, stored_a, stored_v, stored_lf) + ((stored_q,) if has_q else ()):
                sp.wait_ge(sm, 16 * turns * NB + 1)

        @block.gpsimd
        def _(pool):
            pool.sem_inc(yo_ready.sem, NT)
            with pool.Fori(0, turns) as i:
                for s in range(NB):
                    n = i * NB + s
                    b = s % 2
                    ch = Chain(pool, pool_self, n, 2 + NT)
                    pool.wait_ge(xnT_ready.sem, xnT_ready.at(n, 1) + 1)
                    if s == 0:
                        pool.wait_ge(kern_ready, 1 + 1)
                    pool.wait_ge(yb_ready.sem, n * NT + 1)
                    settle(pool, passed_pool)
                    ch.link(pool.tensor_copy(xb[:], xnT[:, b]))
                    settle(pool, passed_pool)
                    pool.tensor_scalar(vq[:], xb[:], rsc[:, 0:1], None, ALU.mult).then_inc(v_scaled.sem, 1)
                    pool.wait_ge(cq_ready.sem, cq_ready.at(n, 1) + 1)
                    ch.link(pool.tensor_tensor(vq[:], vq[:], cq[:], ALU.add))
                    pool.tensor_tensor(xq[:], vq[:], cq[:], ALU.subtract).then_inc(xq_ready.sem, 1)
                    pool.wait_ge(silu_k.sem, silu_k.at(n, 1) + 1)
                    pool.tensor_tensor(k2[:], kr[:], kr[:], ALU.mult).then_inc(k_sq.sem, 1)
                    pool.wait_ge(rn_ready.sem, rn_ready.at(n, 1) + 1)
                    pool.wait_ge(stored_k, n * 16 + 1)
                    pool.wait_ge(a_ready.sem, n + 1)
                    pool.tensor_tensor(kn[:], kr[:], kss[:], ALU.mult).then_inc(kn_ready.sem, 1)
                    pool.wait_ge(stored_y, n * 16 + 1)
                    for j in range(NT):
                        pool.wait_ge(yb_ready.sem, yb_ready.at(n, j + 1) + 1)
                        ch.link(pool.tensor_tensor(yb[:, j], yb[:, j], bias[:], ALU.add))
                        pool.tensor_tensor(yo[:, j], yb[:, j], x[:, b, j], ALU.add).then_inc(yo_ready.sem, 1)
                    ch.end()

        @block.scalar
        def _(act):
            act.sem_inc(act_free.sem, 3)
            act.wait_ge(setup, 1 + 1)
            with act.Fori(0, turns) as i:
                for s in range(NB):
                    n = i * NB + s
                    b = s % 2
                    job = [0]
                    ch = Chain(act, act_self, n, 1 + 2 + 2 + 1)

                    def take(out, func, done=None, scale=1.0, rows=P):
                        act.wait_ge(act_psum.sem, act_psum.at(n, job[0] + 1) + 1)
                        act.activation(out, psA[(s * JA + job[0]) % 4][0:rows, :], func, scale=scale)\
                           .then_inc(act_free.sem, 1)
                        job[0] += 1

                    act.wait_ge(var_ready.sem, var_ready.at(n, 1) + 1)
                    act.wait_ge(xn_ready.sem, n * NT + 1)
                    ch.link(act.activation(lnv[:], ve[:], ACT.Ln))
                    act.activation(rs[:], lnv[:], ACT.Exp, scale=-0.5).then_inc(rs_raw.sem, 1)
                    act.wait_ge(xq_ready.sem, n + 1)
                    for kd in range(KD):
                        take(xnT[:, b, kd, :], ACT.Copy)
                    act.wait_ge(act_free.sem, act_free.at(n, job[0] + 3) + 1)
                    act.sem_inc(xnT_ready.sem, 1)
                    act.wait_ge(dve_psum.sem, dve_psum.at(n, 0) + 1)
                    take(f1[:], ACT.Copy, rows=HD)
                    take(yg[:], ACT.Copy, rows=H)
                    act.wait_ge(a_ready.sem, n + 1)
                    act.wait_ge(kn_ready.sem, n + 1)
                    for g in range(NG):
                        take(kr[:, g, :], ACT.Silu)
                    act.wait_ge(act_free.sem, act_free.at(n, job[0] + 3) + 1)
                    act.sem_inc(silu_k.sem, 1)
                    act.wait_ge(stored_v, n * 16 + 1)
                    for g in range(NG):
                        take(vt[:, g, :], ACT.Silu)
                    act.wait_ge(act_free.sem, act_free.at(n, job[0] + 3) + 1)
                    act.sem_inc(silu_v.sem, 1)
                    if has_q:
                        act.wait_ge(stored_q, n * 16 + 1)
                        for g in range(NG):
                            take(qt[:, g, :], ACT.Silu)
                        act.wait_ge(act_free.sem, act_free.at(n, job[0] + 3) + 1)
                        act.sem_inc(silu_q.sem, 1)
                    ch.link(act.activation(bg[:], yg[:], ACT.Abs))
                    ch.link(act.activation(bg[:], bg[:], ACT.Exp, scale=-1.0))
                    act.activation(bg[:], bg[:], ACT.Ln, bias=1.0).then_inc(bln_ready.sem, 1)
                    act.wait_ge(z_ready.sem, z_ready.at(n, 1) + 1)
                    act.wait_ge(lf_ready.sem, n + 1)
                    ch.link(act.activation(lz[:], z[:], ACT.Abs))
                    ch.link(act.activation(lz[:], lz[:], ACT.Exp, scale=-1.0))
                    act.activation(lz[:], lz[:], ACT.Ln, bias=1.0).then_inc(lz_ready.sem, 1)
                    act.wait_ge(blm_ready.sem, blm_ready.at(n, 1) + 1)
                    act.activation(beta[:], yg[:], ACT.Exp).then_inc(beta_ready.sem, 1)
                    act.wait_ge(kss_ready.sem, kss_ready.at(n, 1) + 1)
                    ch.link(act.activation(kss[:], kss[:], ACT.Ln, scale=NSC))
                    act.activation(kss[:], kss[:], ACT.Exp, scale=-0.5, bias=nscale[:]).then_inc(rn_ready.sem, 1)
                    act.wait_ge(yo_ready.sem, n * NT + NT + 1)
                    for j in range(NT):
                        act.wait_ge(act_psum.sem, act_psum.at(n, job[0] + 1) + 1)
                        act.activation(yb[:, j, :], psA[(s * JA + job[0]) % 4][:], ACT.Identity, scale=osc[:])\
                           .then_inc(act_free.sem, 1)
                        job[0] += 1
                        act.wait_ge(act_free.sem, act_free.at(n, job[0] + 3) + 1)
                        act.sem_inc(yb_ready.sem, 1)
                    assert job[0] == JA
                    ch.end()

        @block.vector
        def _(dve):
            ns = [0]

            def slink(ins):
                ns[0] += 1
                ins.then_inc(kern_steps, 1)
                dve.wait_ge(kern_steps, ns[0] + 1)

            dve.sem_inc(dve_free.sem, 3)
            dve.wait_ge(loaded, NLOAD * 16 + 1)
            slink(dve.memset(nscale[:], NBIAS))
            slink(dve.reciprocal(rsc[:, 0:1], scal[:, 0:1]))
            slink(dve.reciprocal(rsc[:, 1:2], scal[:, 1:2]))
            slink(dve.tensor_tensor(osc[:], scal[:, 0:1], scal[:, 1:2], ALU.mult))
            dve.sem_inc(setup, 1)
            wtmp = vq[:]
            slink(dve.tensor_scalar(wtmp, kraw[:], rsc[:, 1:2], None, ALU.mult))
            slink(dve.tensor_scalar(cq[:].bitcast(U32), wtmp.bitcast(U32), EXP_BITS, None, ALU.bitwise_and))
            slink(dve.tensor_scalar(cq[:], cq[:], FP8_MIN, FP8_MAGIC, ALU.max, ALU.mult))
            slink(dve.tensor_tensor(wtmp, wtmp, cq[:], ALU.add))
            slink(dve.tensor_tensor(kq[:], wtmp, cq[:], ALU.subtract))
            dve.sem_inc(kern_ready, 1)
            with dve.Fori(0, turns) as i:
                for s in range(NB):
                    n = i * NB + s
                    b = s % 2
                    ch = Chain(dve, dve_self, n, NT + NT + 1 + 4 + 1)
                    job = [0]

                    def bank():
                        dve.wait_ge(dve_psum.sem, dve_psum.at(n, job[0] + 1) + 1)
                        job[0] += 1
                        return psD[(s * JD + job[0] - 1) % 4]

                    dve.wait_ge(x_in[b], (i * (NB // 2) + s // 2) * 16 + 16 + 1)
                    for j in range(NT):
                        ch.tick(dve.bn_stats(st[:, j, :], x[:, b, j, :]))
                    ch.wait()
                    settle(dve, passed_dve)
                    for j in range(NT):
                        ch.tick(dve.bn_aggr(mv[:, j, :], st[:, j, :]))
                    ch.wait()
                    ch.tick(dve.tensor_scalar(ve[:], mv[:, :, 1], LN_EPS, None, ALU.add))
                    ch.wait()
                    dve.sem_inc(var_ready.sem, 1)
                    dve.wait_ge(rs_raw.sem, rs_raw.at(n, 1) + 1)
                    ch.link(dve.tensor_tensor(nt[:], rs[:], rs[:], ALU.mult))
                    ch.link(dve.tensor_tensor(nt[:], nt[:], ve[:], ALU.mult))
                    ch.link(dve.tensor_scalar(nt[:], nt[:], -0.5, 1.5, ALU.mult, ALU.add))
                    ch.link(dve.tensor_tensor(rs[:], nt[:], rs[:], ALU.mult))
                    dve.wait_ge(xnT_ready.sem, n + 1)
                    for j in range(NT):
                        dve.tensor_scalar(xn[:, j, :], x[:, b, j, :], mv[:, j, 0:1], rs[:, j:j + 1],
                                          ALU.subtract, ALU.mult).then_inc(xn_ready.sem, 1)
                    dve.wait_ge(v_scaled.sem, v_scaled.at(n, 1) + 1)
                    dve.wait_ge(xq_ready.sem, n + 1)
                    ch.link(dve.tensor_scalar(cq[:].bitcast(U32), vq[:].bitcast(U32), EXP_BITS, None, ALU.bitwise_and))
                    dve.tensor_scalar(cq[:], cq[:], FP8_MIN, FP8_MAGIC, ALU.max, ALU.mult).then_inc(cq_ready.sem, 1)
                    dve.wait_ge(stored_lf, n * 16 + 1)
                    for g in range(NG):
                        dve.tensor_scalar(z[:, g, :], bank()[:], ZMIN, None, ALU.max).then_inc(dve_free.sem, 1)
                    dve.wait_ge(dve_free.sem, dve_free.at(n, 4 + 3) + 1)
                    dve.sem_inc(z_ready.sem, 1)
                    dve.wait_ge(bln_ready.sem, bln_ready.at(n, 1) + 1)
                    dve.scalar_tensor_tensor(out=yg[:], in0=yg[:], scalar=0.0, in1=bg[:], op0=ALU.min,
                                             op1=ALU.subtract).then_inc(blm_ready.sem, 1)
                    dve.wait_ge(lz_ready.sem, lz_ready.at(n, 1) + 1)
                    dve.scalar_tensor_tensor(out=z[:], in0=z[:], scalar=0.0, in1=lz[:], op0=ALU.min,
                                             op1=ALU.subtract).then_inc(lf_ready.sem, 1)
                    dve.wait_ge(kn_ready.sem, n + 1)
                    for g in range(NG):
                        dve.tensor_scalar(kss[:, g, :], bank()[:], NORM_EPS ** 2, None, ALU.max).then_inc(dve_free.sem, 1)
                    dve.wait_ge(dve_free.sem, dve_free.at(n, 8 + 3) + 1)
                    dve.sem_inc(kss_ready.sem, 1)
                    dve.wait_ge(kn_ready.sem, kn_ready.at(n, 1) + 1)
                    dve.wait_ge(stored_a, n * 16 + 1)
                    for g in range(NG):
                        dve.tensor_tensor(av[:, g, :], bank()[:], kn[:, g, :], ALU.mult).then_inc(dve_free.sem, 1)
                    dve.wait_ge(dve_free.sem, dve_free.at(n, 12 + 3) + 1)
                    dve.sem_inc(a_ready.sem, 1)
                    ch.end()

        @block.tensor
        def _(pe):
            pe.wait_ge(loaded, NLOAD * 16 + 1)
            pe.wait_ge(kern_ready, 1 + 1)
            with pe.Fori(0, turns) as i:
                for s in range(NB):
                    n = i * NB + s
                    b = s % 2
                    ja, jd = [0], [0]

                    def bank_a():
                        pe.wait_ge(act_free.sem, act_free.at(n, ja[0]) + 1)
                        ja[0] += 1
                        return psA[(s * JA + ja[0] - 1) % 4]

                    def bank_d():
                        pe.wait_ge(dve_free.sem, dve_free.at(n, jd[0]) + 1)
                        jd[0] += 1
                        return psD[(s * JD + jd[0] - 1) % 4]

                    pe.wait_ge(xn_ready.sem, xn_ready.at(n, NT) + 1)
                    for kd in range(KD):
                        ps = bank_a()
                        for j in range(NT):
                            last = nc.tensor.transpose(ps[:, j * P:(j + 1) * P], xn[:, j, kd * P:(kd + 1) * P], ident[:])
                        last.then_inc(act_psum.sem, 1)
                    pe.wait_ge(xnT_ready.sem, xnT_ready.at(n, 1) + 1)

                    def product(ps, w, rows):
                        for kd in range(KD):
                            last = nc.tensor.matmul(ps[0:rows, :], w(kd), xnT[:, b, kd, :],
                                                    start=(kd == 0), stop=(kd == KD - 1))
                        return last

                    product(bank_a(), lambda kd: wf1[:, kd, :], HD).then_inc(act_psum.sem, 1)
                    product(bank_a(), lambda kd: wg[:, kd, :], H).then_inc(act_psum.sem, 1)
                    for w in (wk, wv) + ((wq,) if has_q else ()):
                        for g in range(NG):
                            product(bank_a(), lambda kd: w[:, kd, g * P:(g + 1) * P], P).then_inc(act_psum.sem, 1)
                    for g in range(NG):
                        ps = bank_d()
                        nc.tensor.matmul(ps[:], wf2[:, g * P:(g + 1) * P], f1[:], start=True, stop=True)\
                          .then_inc(dve_psum.sem, 1)
                    pe.wait_ge(k_sq.sem, k_sq.at(n, 1) + 1)
                    for g in range(NG):
                        ps = bank_d()
                        nc.tensor.matmul(ps[:], ones_bd[:].rearrange("p h c -> p (h c)"), k2[:, g, :],
                                         start=True, stop=True).then_inc(dve_psum.sem, 1)
                    pe.wait_ge(beta_ready.sem, beta_ready.at(n, 1) + 1)
                    for g in range(NG):
                        ps = bank_d()
                        nc.tensor.matmul(ps[:], spread[:, g].rearrange("p h c -> p (h c)"), beta[:],
                                         start=True, stop=True).then_inc(dve_psum.sem, 1)
                    pe.wait_ge(xq_ready.sem, xq_ready.at(n, 1) + 1)
                    for j in range(NT):
                        ps = bank_a()
                        for kd in range(KD):
                            last = nc.tensor.matmul(ps[:], xq[:, kd, j * P:(j + 1) * P], kq[:, kd, :],
                                                    start=(kd == 0), stop=(kd == KD - 1))
                        last.then_inc(act_psum.sem, 1)
                    assert ja[0] == JA and jd[0] == JD


NSC = 2.0 ** 20
NBIAS = 10.0 * 0.6931471805599453


def chunks(nc, sems, ctx, consts, scratch):
    def sb(name, shape, dt=F32):
        return ctx.enter_context(nc.sbuf_tensor(f"c_{name}", shape, dt))

    def sem(name):
        return sems.new(nc, f"c_{name}")

    ident = consts["ident"]
    RG = PU // RC
    NS = PT // SUB
    W = PU * MI
    src = sb("src", [P, 2, NSRC, PT])
    keep = sb("keep", [P, NS, SUB])
    g8 = sb("g8", [P, PT])
    gm = sb("gm", [P, 2, PT, 2])
    dm, he = sb("dm", [P, 2, W]), sb("he", [P, 2, W])
    en, ff = sb("en", [P, PT, 2]), sb("ff", [P, PT, 2])
    LQ = MI + CH
    LQS = LQ + CH + SUB
    NMOV = 96
    lqx = sb("lqx", [P, 2, (PU + 1) * LQS])
    lqv = lqx[:].rearrange("p b (u x) -> p b u x", x=LQS)[:, :, 0:PU]
    lq, lq8 = lqv[:, :, :, 0:LQ], lqv[:, :, :, LQ:LQS]
    rr = sb("rr", [P, 2, MI, 2, PU])
    l0, re = sb("l0", [P, PU, MI]), sb("re", [P, PU, MI])
    vm = sb("vm", [P, PT, 2])
    rec = sb("rec", [P, 2, RG, RW])
    lv = sb("lv", [P, 2, PU, 2, HD])
    lvc = sb("lvc", [P, 2, PU, 2 * HD])
    bda = sb("bda", [P, 2, HG, MI, 2, PU])
    bdt = sb("bdt", [P, 2, HG, MI, PU])
    dst = sb("dstk", [P, UN, MI])
    cst = sb("cstk", [P, UN, CH])
    ttr = sb("ttr", [P, NP, MI, PU])
    tl = sb("tl", [P, MI, HG, MI])
    lmask = sb("lmask", [P, CH, CH])
    wsb = sb("wsb", [P, 2, PU, HD])
    uwsb = sb("uwsb", [P, 2, RG, 2 * HD * RC])
    qmask, cmask = sb("qmask", [P, CH]), sb("cmask", [P, SUB])
    HD_DVE = 2
    tmpd = sb("tmpd", [P, HD_DVE, CH * (CH - 1)])
    tmpg = sb("tmpg", [P, HG - HD_DVE, CH * (CH - 1)])

    def ps(name, banks):
        return ctx.enter_context(nc.psum_tensor(f"c_{name}", [P, banks * 512], F32))

    psD, psC = ([ps(f"{m}{i}", n) for i in range(2)] for m, n in (("psD", 2), ("psC", 1)))
    psL = psC
    psW = ps("psW", 2)
    dslot = [t[:].rearrange("p (a x) -> p a x", a=RG)[:, :, 0:RC * LQ].rearrange("p a (r x) -> p a r x", r=RC) for t in psD]
    cslot = [t[:, 0:PU * (CH + SUB)].rearrange("p (u x) -> p u x", u=PU) for t in psC]
    wslot = psW[:].rearrange("p (u x) -> p u x", x=2 * HD)

    ITEMS = NQ * NG
    NOQ = (OT0 // QT) * NG
    NB_BACK, NB_IN, NB_X = 8, 8, 4
    NL = NB_BACK + NB_IN + NB_X
    x_in, bdr_in, bdt_in, store1, store2 = ([sem(f"{m}{b}") for b in range(2)] for m in
                                            ("pieces_in", "bd_right_in", "bd_left_in", "stored_right", "stored_uw"))
    src_free = sem("pieces_used")
    gm_ready, vm_ready = sem("gm_ready"), sem("vm_ready")
    exps = sem("exps_ready")
    rows_l, rows_ready, tm_ready = sem("left_rows_ready"), sem("rows_ready"), sem("row_major_ready")
    prods = sem("products_full")
    prods_free = sem("products_free")
    aq_free = sem("q_products_read")
    lanes, lanes_free = sem("lane_banks_full"), sem("lane_banks_free")
    mats, solved, tt_ready = sem("matrices_ready"), sem("solved"), sem("inverse_ready")
    uw, uw_free = sem("uw_full"), sem("uw_read")
    wt_ready = sem("w_transposed")
    setup, pool_setup = sem("setup"), sem("pool_setup")
    front_steps, back_steps, q_steps = sem("dve_front_steps"), sem("dve_back_steps"), sem("dve_q_steps")
    dve_solve, pool_solve = sem("dve_solve_steps"), sem("pool_solve_steps")
    passed_sp, passed_dve = sem("passed_sp"), sem("passed_dve")
    sems.prime(nc)
    SOLVE_STEPS = 2 * (MI - 2)

    def pair(i, p):
        return i * (NP // 2) + p // 2

    def turns(body):
        for i in range(2):
            body(i, False, True, i > 0, False)
        return [(2, NOQ, False), (NOQ, ITEMS, True)]

    def run(eng, body):
        for a, b, has_q in turns(body):
            with eng.Fori(a, b) as i:
                body(i, has_q, True, True, True)
        body(ITEMS, True, False, True, True)
        body(ITEMS + 1, True, False, False, True)

    def solve_item(eng, c, steps, tmp, h0, h1, between=None):
        ch = Chain(eng, steps, c, SOLVE_STEPS)
        eng.wait_ge(mats, c + 2)
        nh = h1 - h0
        tlh = tl[:].rearrange("p s h r -> p h s r")
        for r in range(1, MI - 1):
            below, left = MI - 1 - r, r
            col = tlh[:, h0:h1, r + 1:MI, r:r + 1].to_broadcast([P, nh, below, left])
            row = tlh[:, h0:h1, r:r + 1, 0:r].to_broadcast([P, nh, below, left])
            t = tmp[:, 0:nh, 0:below * left].rearrange("p h (b l) -> p h b l", l=left)
            ch.link(eng.tensor_tensor(t, col, row, ALU.mult))
            acc = tlh[:, h0:h1, r + 1:MI, 0:r]
            ch.link(eng.tensor_tensor(acc, acc, t, ALU.add))
            if between:
                between(r)
        eng.sem_inc(solved, 1)
        ch.end()

    with nc.Block() as block:
        @block.sync
        def _(sp):
            def load(i, p, has_q):
                sp.wait_ge(src_free, i * NP + p + 1)
                settle(sp, passed_sp)
                ns = NSRC if has_q else NSRC - 1
                sp.dma_start(src[:, p % 2, 0:ns, :], scratch["src"][bass.ds(i, 1), :, 0:ns, p * PT:(p + 1) * PT]
                             .rearrange("a p m t -> p (a m) t")).then_inc(x_in[p % 2], 16)

            def bd_right(i, p):
                j = i * NP + p
                sp.wait_ge(rows_l, j + 1 + 1)
                settle(sp, passed_sp)
                sp.wait_ge(prods, j + 1 + 1)
                settle(sp, passed_sp)
                for h in range(HG):
                    r = slice(h * HD, (h + 1) * HD)
                    sp.dma_start(bda[r, p % 2, h], rr[r, p % 2]).then_inc(bdr_in[p % 2], 16)

            def out_right(i, p, has_q):
                j = i * NP + p
                sp.wait_ge(tm_ready, j + 1 + 1)
                settle(sp, passed_sp)
                sp.dma_start(scratch["lv"][bass.ds(i, 1), :, p, :].rearrange("a p x -> p (a x)"),
                             lv[:, p % 2].rearrange("p u m d -> p (u m d)")).then_inc(store1[p % 2], 16)
                if has_q:
                    sp.wait_ge(aq_free, (i - NOQ) * NP + p + 2 + 1)
                    settle(sp, passed_sp)
                rw = RW if has_q else RQ0
                sp.dma_start(scratch["rec"][bass.ds(i, 1), :, p * RG:(p + 1) * RG, 0:rw].rearrange("a p u c -> p (a u) c"),
                             rec[:, p % 2, :, 0:rw]).then_inc(store1[p % 2], 16)

            def bd_left(c, p):
                j = c * NP + p
                sp.wait_ge(uw, 2 * j + 1)
                settle(sp, passed_sp)
                for h in range(HG):
                    r = slice(h * HD, (h + 1) * HD)
                    sp.dma_start(bdt[r, p % 2, h], ttr[r, p]).then_inc(bdt_in[p % 2], 16)
                sp.dma_start(lvc[:, p % 2].rearrange("p u x -> p (u x)"), scratch["lv"][bass.ds(c, 1), :, p, :]
                             .rearrange("a p x -> p (a x)")).then_inc(bdt_in[p % 2], 16)

            def out_left(c, p):
                sp.wait_ge(wt_ready, c * NP + p + 1 + 1)
                settle(sp, passed_sp)
                sp.dma_start(scratch["uw"][bass.ds(c, 1), :, p * RG:(p + 1) * RG, :].rearrange("a p u c -> p (a u) c"),
                             uwsb[:, p % 2]).then_inc(store2[p % 2], 16)

            def body(i, has_q, make, solve, out):
                if make:
                    load(i, 0, has_q)
                    load(i, 1, has_q)
                if out:
                    c = i - 2
                    sp.wait_ge(tt_ready, c + 1 + 1)
                    settle(sp, passed_sp)
                    for b in range(2):
                        sp.wait_ge(store1[b], (c + 1) * (NP // 2 * 32) + 1)
                        settle(sp, passed_sp)
                    for p in range(NP):
                        bd_left(c, p)
                        if p:
                            out_left(c, p - 1)
                    out_left(c, NP - 1)
                if make:
                    for p in range(NP):
                        bd_right(i, p)
                        if p + 2 < NP:
                            load(i, p + 2, has_q)
                        if p:
                            out_right(i, p - 1, has_q)
                    out_right(i, NP - 1, has_q)

            sp.wait_ge(setup, 2 + 1)
            run(sp, body)
            for b in range(2):
                sp.wait_ge(store1[b], ITEMS * (NP // 2) * 32 + 1)
                sp.wait_ge(store2[b], ITEMS * (NP // 2) * 16 + 1)

        @block.gpsimd
        def _(pool):
            n = [0]

            def link(ins):
                n[0] += 1
                ins.then_inc(pool_setup, 1)
                pool.wait_ge(pool_setup, n[0] + 1)

            for t in (bda, bdt, lqx, rr, gm, vm, tl, rec):
                link(pool.memset(t[:], 0.0))
            for t in (keep, lmask, qmask, cmask):
                link(pool.memset(t[:], 1.0))
            link(pool.memset(keep[:, :, 0:1], 0.0))
            link(pool.affine_select(out=tl[:], in_=tl[:], compare_op=ALU.not_equal, fill=1.0, base=0,
                                    pattern=[[1, MI], [0, HG], [-1, MI]], channel_multiplier=0))
            link(pool.affine_select(out=lmask[:], in_=lmask[:], compare_op=ALU.is_gt, fill=0.0, base=0,
                                    pattern=[[1, CH], [-1, CH]], channel_multiplier=0))
            for h in range(HG):
                r = slice(h * HD, (h + 1) * HD)
                link(pool.affine_select(out=qmask[r], in_=qmask[r], compare_op=ALU.is_ge, fill=0.0, base=1,
                                        pattern=[[2, CH]], channel_multiplier=-1))
                link(pool.affine_select(out=qmask[r, SUB:CH], in_=qmask[r, SUB:CH], compare_op=ALU.is_ge, fill=0.0,
                                        base=-CH, pattern=[[0, SUB]], channel_multiplier=1))
                link(pool.affine_select(out=cmask[r], in_=cmask[r], compare_op=ALU.is_ge, fill=0.0,
                                        base=CH - 1, pattern=[[0, SUB]], channel_multiplier=-1))
            pool.sem_inc(setup, 1)

            def body(i, has_q, make, solve, out):
                if solve:
                    solve_item(pool, i - 1, pool_solve, tmpg, HD_DVE, HG)

            run(pool, body)

        @block.scalar
        def _(act):
            def body(i, has_q, make, solve, out):
                if out:
                    for p in range(NP):
                        j = (i - 2) * NP + p
                        act.wait_ge(store2[p % 2], pair(i - 2, p) * 16 + 1)
                        for c in range(2):
                            act.wait_ge(uw, 2 * j + c + 3 + 1)
                            us = slice(c * RC, (c + 1) * RC)
                            act.activation(wsb[:, p % 2, us, :], wslot[:, us, 0:HD], ACT.Copy)
                            act.activation(uwsb[:, p % 2, c, 0:HD * RC].rearrange("p (r v) -> p r v", r=RC),
                                           wslot[:, us, HD:2 * HD], ACT.Copy).then_inc(uw_free, 1)

                def read_products(p):
                    us = slice(p * PU, (p + 1) * PU)
                    act.wait_ge(prods, i * NP + p + 3 + 1)
                    act.activation(dst[:, us, :].rearrange("p (a r) m -> p a r m", r=RC), dslot[p % 2][:, :, :, 0:MI], ACT.Copy)
                    act.activation(cst[:, us, :], cslot[p % 2][:, :, 0:CH], ACT.Copy).then_inc(prods_free, 1)

                if make:
                    for p in range(NP):
                        j = i * NP + p
                        b = p % 2
                        act.wait_ge(gm_ready, j + 1 + 1)
                        act.wait_ge(rows_ready, j + 1)
                        act.activation(en[:].rearrange("p t m -> p (t m)"), dm[:, b], ACT.Exp, scale=-1.0)
                        act.activation(dm[:, b], dm[:, b], ACT.Exp)
                        act.activation(ff[:], gm[:, b], ACT.Exp)
                        act.activation(he[:, b], he[:, b], ACT.Exp).then_inc(exps, 1)
                        act.activation(vm[:, :, 1], src[:, b, 2, :], ACT.Copy).then_inc(vm_ready, 1)
                        if p:
                            read_products(p - 1)
                    read_products(NP - 1)
                if solve:
                    act.wait_ge(uw, 2 * NP * (i - 1) + 2 + 1)
                    for k in range(NB_BACK):
                        act.wait_ge(lanes, i * NL - NB_BACK + k + 1 + 1)
                        act.activation(ttr[:, :, 4 * k:4 * k + 4, :].rearrange("p a s u -> p s a u"),
                                       psL[k % 2][:].rearrange("p (s a u) -> p s a u", s=4, u=PU), ACT.Copy).then_inc(lanes_free, 1)
                    act.wait_ge(lanes_free, i * NL + 1 + 1)
                    act.sem_inc(tt_ready, 1)
                if make:
                    act.wait_ge(lanes_free, i * NL + NB_IN + 1 + 1)
                    for k in range(NB_X):
                        act.wait_ge(lanes, i * NL + NB_IN + k + 1 + 1)
                        s0 = CH + 4 * k
                        act.activation(tl[:, s0:s0 + 4, :, 0:CH],
                                       psL[k % 2][:].rearrange("p (s h r) -> p s h r", s=4, h=HG)[:, :, :, 0:CH], ACT.Copy)\
                           .then_inc(lanes_free, 1)
                    act.wait_ge(lanes_free, i * NL + NB_IN + NB_X + 1 + 1)
                    act.sem_inc(mats, 1)

            act.wait_ge(setup, 2 + 1)
            run(act, body)

        @block.vector
        def _(dve):
            dve.wait_ge(setup, 1 + 1)
            for s, credit in ((src_free, 1), (exps, 1), (prods, 2), (prods_free, 1), (lanes_free, 1), (aq_free, 1), (uw, 2), (uw_free, 1)):
                dve.sem_inc(s, credit)
            dve.sem_inc(setup, 1)

            def front(i, p):
                j = i * NP + p
                b = p % 2
                ch = Chain(dve, front_steps, j, 5)
                gmv = gm[:, b].rearrange("p (n s) m -> p n s m", s=SUB)
                g8v = g8[:].rearrange("p (n s) -> p n s", s=SUB)
                dve.wait_ge(x_in[b], (pair(i, p) + 1) * 16 + 1)
                ch.link(dve.tensor_tensor_scan(out=g8[:], data0=keep[:].rearrange("p n s -> p (n s)"),
                                               data1=src[:, b, 3, :], initial=0.0, op0=ALU.mult, op1=ALU.add))
                dve.wait_ge(exps, j + 1)
                ch.tick(dve.tensor_copy(gm[:, b, :, 1], g8[:]))
                ch.link(dve.tensor_copy(gmv[:, :, 1:SUB, 0], g8v[:, :, 0:SUB - 1]))
                gmn = gm[:, b].rearrange("p (n s) m -> p n (s m)", s=SUB)
                mid = g8v[:, :, SUB // 2 - 1:SUB // 2].to_broadcast([P, NS, 2 * SUB])
                end = g8v[:, :, SUB - 1:SUB].to_broadcast([P, NS, 2 * SUB])
                ch.tick(dve.tensor_tensor(dm[:, b].rearrange("p (n s) -> p n s", n=NS), gmn, mid, ALU.subtract))
                ch.link(dve.tensor_tensor(he[:, b].rearrange("p (n s) -> p n s", n=NS), end, gmn, ALU.subtract))
                dve.sem_inc(gm_ready, 1)
                ch.end()

            def grouped(t):
                return t.rearrange("p (a r) t -> p a r t", r=RC)

            def back(i, p, has_q):
                j = i * NP + p
                b = p % 2
                ch = Chain(dve, back_steps, j, 3)
                dve.wait_ge(exps, j + 2 + 1)
                dve.wait_ge(prods, j + 1 + 1)
                ep, hh = (t[:, b].rearrange("p (t m) -> p t m", m=2) for t in (dm, he))
                kk = src[:, b, 0, :].unsqueeze(2).to_broadcast([P, PT, 2])
                aa = src[:, b, 1, :].unsqueeze(2).to_broadcast([P, PT, 2])

                def half(t, c):
                    return t.rearrange("p (u c s) m -> p u c s m", u=PU, c=2)[:, :, c]

                def v3(t):
                    return t.rearrange("p u (s m) -> p u s m", m=2)

                def v3t(t):
                    return t.rearrange("p (s m) u -> p u s m", m=2)

                def full(t):
                    return t.rearrange("p (u s) m -> p u s m", u=PU)

                rd, r8 = rr[:, b, :, 0, :], rr[:, b, 0:CH, 1, :]
                dve.tensor_tensor(v3t(rd), full(kk), full(en[:]), ALU.mult)
                dve.tensor_tensor(v3t(r8), half(kk, 0), half(hh, 0), ALU.mult)
                dve.tensor_tensor(v3(lq[:, b, :, 0:MI]), full(aa), full(ep), ALU.mult)
                gf = ff[:].rearrange("p (u t) m -> p u (t m)", u=PU)
                gfirst, gsec = gf[:, :, CH - 1:CH], gf[:, :, MI - 1:MI]
                if has_q:
                    qv = src[:, b, 4, :].rearrange("p (u t) -> p u t", u=PU)
                    dve.tensor_tensor(lq[:, b, :, MI:MI + CH], qv, ep[:, :, 1].rearrange("p (u t) -> p u t", u=PU), ALU.mult)
                    ffq = ff[:, :, 1].rearrange("p (u t) -> p u t", u=PU)
                    dve.tensor_tensor(lq8[:, b, :, CH:CH + SUB], qv[:, :, SUB:CH], ffq[:, :, SUB:CH], ALU.mult)
                ch.link(dve.tensor_tensor(v3(lq8[:, b, :, 0:CH]), half(aa, 1), half(ff[:], 1), ALU.mult))
                dve.sem_inc(rows_l, 1)
                dve.tensor_tensor(v3(l0[:, :, 0:CH]), half(aa, 0), half(ff[:], 0), ALU.mult)
                dve.tensor_tensor(l0[:, :, CH:MI], lq8[:, b, :, 0:CH], gfirst.to_broadcast([P, PU, CH]), ALU.mult)
                dve.tensor_tensor(v3(re[:, :, CH:MI]), half(kk, 1), half(hh, 1), ALU.mult)
                ch.link(dve.tensor_tensor(re[:, :, 0:CH], r8.rearrange("p m u -> p u m"), gsec.to_broadcast([P, PU, CH]), ALU.mult))
                dve.wait_ge(store1[b], pair(i, p) * 32 + 1)
                if has_q:
                    q0v = rec[:, b, :, RQ0:RAQ].rearrange("p a (t r) -> p a r t", r=RC)
                    dve.tensor_tensor(q0v[:, :, :, 0:SUB], grouped(qv[:, :, 0:SUB]), grouped(ffq[:, :, 0:SUB]), ALU.mult)
                    dve.tensor_tensor(q0v[:, :, :, SUB:CH], grouped(lq8[:, b, :, CH:CH + SUB]),
                                      grouped(gfirst.to_broadcast([P, PU, SUB])), ALU.mult)
                dve.tensor_tensor(rec[:, b, :, RGAM:RQ0].unsqueeze(3), grouped(gfirst), grouped(gsec), ALU.mult)
                dve.wait_ge(vm_ready, j + 1 + 1)
                dve.transpose(lv[:, b, :, 0, :], l0[:])
                dve.transpose(lv[:, b, :, 1, :], vm[:].rearrange("p (u t) m -> p u (t m)", u=PU))
                for a in range(RG):
                    last = dve.transpose(rec[:, b, a, 0:RGAM].rearrange("p (c r) -> p r c", r=RC), re[:, a * RC:(a + 1) * RC, :])
                ch.link(last)
                for s in (tm_ready, rows_ready, src_free):
                    dve.sem_inc(s, 1)
                ch.end()

            W_FIRST, W_STEP = 7, 3

            def w_turned(c, p):
                j = c * NP + p
                dve.wait_ge(uw_free, 2 * j + 3 + 1)
                for a in range(RG):
                    last = dve.transpose(uwsb[:, p % 2, a, HD * RC:].rearrange("p (m r) -> p r m", r=RC),
                                         wsb[:, p % 2, a * RC:(a + 1) * RC, :])
                last.then_inc(wt_ready, 1)

            def read_q(i, p):
                jq = (i - NOQ) * NP + p
                b = p % 2
                ch = Chain(dve, q_steps, jq, 1)
                dve.wait_ge(prods_free, i * NP + p + 2 + 1)
                pq, pc = dslot[b][:, :, :, MI:LQ], cslot[b][:, :, CH:CH + SUB]
                aqv = rec[:, b, :, RAQ:RW].rearrange("p a (t r) -> p a r t", r=RC)
                settle(dve, passed_dve)
                ch.link(dve.copy_predicated(out=aqv, data=pq, mask=grouped(
                    qmask[:].bitcast(U32).unsqueeze(1).to_broadcast([P, PU, CH]))))
                settle(dve, passed_dve)
                dve.copy_predicated(out=aqv[:, :, :, SUB:CH], data=grouped(pc), mask=grouped(
                    cmask[:].bitcast(U32).unsqueeze(1).to_broadcast([P, PU, SUB]))).then_inc(aq_free, 1)
                ch.end()

            def body(i, has_q, make, solve, out):
                if make:
                    front(i, 0)
                if solve:
                    solve_item(dve, i - 1, dve_solve, tmpd, 0, HD_DVE,
                               (lambda r: w_turned(i - 2, (r - W_FIRST) // W_STEP)
                                if r >= W_FIRST and (r - W_FIRST) % W_STEP == 0 and (r - W_FIRST) // W_STEP < NP
                                else None) if out else None)
                elif out:
                    for p in range(NP):
                        w_turned(i - 2, p)
                if not make:
                    return
                for p in range(NP):
                    if p + 1 < NP:
                        front(i, p + 1)
                    back(i, p, has_q)
                    if has_q and p:
                        read_q(i, p - 1)
                if has_q:
                    read_q(i, NP - 1)
                dve.wait_ge(lanes_free, i * NL + 1 + 1)
                for k in range(NB_IN):
                    dve.wait_ge(lanes, i * NL + k + 1 + 1)
                    s0 = 4 * k
                    r0 = 0 if s0 < CH else CH
                    bank = psL[k % 2][:].rearrange("p (s h r) -> p s h r", s=4, h=HG)
                    settle(dve, passed_dve)
                    for h in range(HG):
                        last = dve.copy_predicated(out=tl[:, s0:s0 + 4, h, r0:r0 + CH], data=bank[:, :, h, r0:r0 + CH],
                                                   mask=lmask[:, s0 - r0:s0 - r0 + 4, :].bitcast(U32))
                    last.then_inc(lanes_free, 1)

            run(dve, body)

        @block.tensor
        def _(pe):
            def left(t):
                return t.rearrange("p h m -> p (h m)")

            def body(i, has_q, make, solve, out):
                if out:
                    pe.wait_ge(tt_ready, i - 1 + 1)
                    for p in range(NP):
                        j = (i - 2) * NP + p
                        b = p % 2
                        pe.wait_ge(bdt_in[b], (pair(i - 2, p) + 1) * ((HG + 1) * 16) + 1)
                        for c in range(RG):
                            pe.wait_ge(uw_free, 2 * j + c + 1)
                            for u in range(c * RC, (c + 1) * RC):
                                last = nc.tensor.matmul(wslot[:, u, :], left(bdt[:, b, :, :, u]), lvc[:, b, u, :],
                                                        start=True, stop=True)
                            last.then_inc(uw, 1)
                if make:
                    if solve:
                        pe.wait_ge(lanes_free, i * NL - NB_BACK + 1 + 1)
                    for p in range(NP):
                        j = i * NP + p
                        b = p % 2
                        pe.wait_ge(rows_l, j + 1 + 1)
                        pe.wait_ge(bdr_in[b], (pair(i, p) + 1) * (HG * 16) + 1)
                        pe.wait_ge(prods_free, j + 1)
                        if has_q:
                            pe.wait_ge(aq_free, (i - NOQ) * NP + p + 1)
                        for u in range(PU):
                            for ps, o, k, x in ((psD[b], u // RC * 512 + u % RC * LQ, 0, 0), (psC[b], u * (CH + SUB), 1, LQ)):
                                o2 = u * LQS + x
                                last = nc.tensor.matmul(ps[:, o:o + NMOV], left(bda[:, b, :, :, k, u]), lqx[:, b, o2:o2 + NMOV],
                                                        start=True, stop=True)
                        last.then_inc(prods, 1)

                def lane_transposes(buf, ns, first):
                    for k in range(ns // 4):
                        pe.wait_ge(lanes_free, i * NL + first + k + 1)
                        for s in range(4):
                            last = nc.tensor.transpose(psL[k % 2][:, s * P:(s + 1) * P], buf(4 * k + s), ident[:])
                        last.then_inc(lanes, 1)

                if make:
                    pe.wait_ge(prods_free, (i + 1) * NP + 1 + 1)
                    if has_q:
                        pe.wait_ge(aq_free, (i + 1 - NOQ) * NP + 1 + 1)
                if solve:
                    pe.wait_ge(solved, 2 * i + 1)
                    lane_transposes(lambda s: tl[:, s].rearrange("p h r -> p (h r)"), MI, -NB_BACK)
                if make:
                    lane_transposes(lambda s: dst[:, :, s], MI, 0)
                    lane_transposes(lambda s: cst[:, :, s], CH, NB_IN)

            pe.wait_ge(setup, 2 + 1)
            run(pe, body)


def chain_states(nc, sems, ctx, scratch):
    def sb(name, shape, dt=F32):
        return ctx.enter_context(nc.sbuf_tensor(f"s_{name}", shape, dt))

    def sem(name):
        return sems.new(nc, f"s_{name}")

    bdw = sb("bdw", [P, 2, NG, HG, MI * RC])
    bdr = sb("bdr", [P, 2, NG, HG, HD * RC])
    bdq = sb("bdq", [P, 2, NG, HG, CH * RC])
    bda = sb("bda", [P, 2, NG, HG, CH * RC])
    u = sb("u", [P, 2, NG, RC, HD])
    gam = sb("gam", [P, 2, NG, RC])
    NF, SPARE = NG // 2, 2
    NMOV = (1 + SPARE) * HD
    S = sb("S", [P, 2, 2, NF + SPARE, HD])
    X = sb("X", [P, 2, 2, NF + SPARE, HD])
    GS = sb("GS", [P, NG, HD])
    osb = sb("osb", [HG * CH, 2, RC, NG * HD])
    psX, psS = ([ctx.enter_context(nc.psum_tensor(f"s_ps{m}{i}", [P, 512], F32)) for i in range(2)] for m in "XS")
    psO = [ctx.enter_context(nc.psum_tensor(f"s_psO{i}", [P, 512], F32)) for i in range(2)]
    zeroed = sem("zeroed")
    in_m, in_q = ([sem(f"{m}{b}") for b in range(2)] for m in ("chunk_operands_in", "output_operands_in"))
    used = sem("operands_used")
    x_full, x_done, s_full, s_done, g_done = ([sem(f"{m}{f}") for f in range(2)] for m in
                                              ("x_product", "x_ready", "s_product", "s_ready", "decayed"))
    halves = [slice(f * NG // 2, (f + 1) * NG // 2) for f in range(2)]
    o_full, o_read = sem("o_product"), sem("o_read")
    o_out = [sem(f"o_stored{b}") for b in range(2)]
    LM = (2 * HG + 2) * 16
    LQ = 2 * HG * 16

    GQ = UN // RC
    cut = (QCH0 - 2 * UN) // RC
    segments = [(0, 0, GQ, False), (1, 0, GQ, False), (2, 0, cut, False), (2, cut, GQ, True), (3, 0, GQ, True)]

    def groups(eng, body):
        n0, o0 = 0, 0
        for q, a, b, out in segments:
            assert (b - a) % 2 == 0
            with eng.Fori(0, (b - a) // 2) as i:
                for par in range(2):
                    body(q, i * 2 + (a + par), i + n0 // 2, i + o0 // 2, par, out)
            n0 += b - a
            o0 += (b - a) if out else 0
        return n0, o0

    def groups_act(eng, body):
        n0, o0 = 0, 0
        for q, a, b, out in segments:
            if out:
                with eng.Fori(0, (b - a) // 2) as i:
                    for par in range(2):
                        body(q, i * 2 + (a + par), i + n0 // 2, i + o0 // 2, par, out)
            n0 += b - a
            o0 += (b - a) if out else 0
        return n0, o0

    def streamed(t, a, g):
        return t[:, a, g // NF, g % NF:g % NF + 1 + SPARE, :].rearrange("p k v -> p (k v)")

    def chunk(t, c):
        return t.rearrange("p h (m r) -> p (h m) r", r=RC)[:, :, c]

    passed_sp, passed_dve, passed_pool = (sem(f"passed_{e}") for e in ("sp", "dve", "pool"))
    sems.prime(nc)

    with nc.Block() as block:
        @block.gpsimd
        def _(pool):
            for t in (bdw, bdr, bdq, bda, S, X):
                pool.memset(t[:], 0.0).then_inc(zeroed, 1)
            pool.wait_ge(zeroed, 6 + 1)

            def body(q, g0, n2, no2, par, out):
                n = n2 * 2 + par
                pool.wait_ge(in_m[par], n2 * LM + LM + 1)
                for c in range(RC):
                    m = n * RC + c
                    for f, gs in enumerate(halves):
                        pool.wait_ge(s_done[f], m + 1 + 1)
                        pool.tensor_tensor(GS[:, gs], S[:, c % 2, f, 0:NF], gam[:, par, gs, c:c + 1].to_broadcast([P, NG // 2, HD]),
                                           ALU.mult).then_inc(g_done[f], 1)

            groups(pool, body)

        @block.sync
        def _(sp):
            sp.wait_ge(zeroed, 6 + 1)

            def body(q, g0, n2, no2, par, out):
                n, no = n2 * 2 + par, no2 * 2 + par
                c0 = g0 * RC
                sp.wait_ge(used, n + 1)
                settle(sp, passed_sp)
                ug = bass.ds(g0, 1)
                gs = slice(q * NG, (q + 1) * NG)
                for h in range(HG):
                    r = slice(h * HD, (h + 1) * HD)
                    sp.dma_start(bdw[r, par, :, h], scratch["uw"][gs, r, ug, HD * RC:].rearrange("g p u c -> p g (u c)")).then_inc(in_m[par], 16)
                    sp.dma_start(bdr[r, par, :, h], scratch["rec"][gs, r, ug, 0:RGAM].rearrange("g p u c -> p g (u c)")).then_inc(in_m[par], 16)
                sp.dma_start(u[:, par].rearrange("p g r c -> p g (r c)"), scratch["uw"][gs, :, ug, 0:HD * RC].rearrange("g p u c -> p g (u c)")).then_inc(in_m[par], 16)
                sp.dma_start(gam[:, par], scratch["rec"][gs, :, ug, RGAM:RQ0].rearrange("g p u c -> p g (u c)")).then_inc(in_m[par], 16)
                if out:
                    for h in range(HG):
                        r = slice(h * HD, (h + 1) * HD)
                        sp.dma_start(bdq[r, par, :, h], scratch["rec"][gs, r, ug, RQ0:RAQ].rearrange("g p u c -> p g (u c)")).then_inc(in_q[par], 16)
                        sp.dma_start(bda[r, par, :, h], scratch["rec"][gs, r, ug, RAQ:RW].rearrange("g p u c -> p g (u c)")).then_inc(in_q[par], 16)

            groups(sp, body)

        @block.scalar
        def _(act):
            act.sem_inc(o_read, 1)

            def body(q, g0, n2, no2, par, out):
                n, no = n2 * 2 + par, no2 * 2 + par
                c0 = g0 * RC
                if not out:
                    return
                act.wait_ge(o_out[par], no2 * (HG * 16) + 1)
                for c in range(RC):
                    act.wait_ge(o_full, no * RC + c + 1 + 1)
                    act.activation(osb[:, par, c, :], psO[c % 2][0:HG * CH, 0:NG * HD], ACT.Copy).then_inc(o_read, 1)
                act.wait_ge(o_read, no * RC + RC + 1 + 1)
                t0 = c0 * CH + q * QT
                for h in range(HG):
                    dst = scratch["o"][h, bass.ds(t0, RC * CH), :].rearrange("(c t) x -> t c x", t=CH)
                    act.dma_start(dst, osb[h * CH:(h + 1) * CH, par])\
                       .then_inc(o_out[par], 16)

            _, no = groups_act(act, body)
            for par in range(2):
                act.wait_ge(o_out[par], no // 2 * HG * 16 + 1)

        @block.vector
        def _(dve):
            dve.wait_ge(zeroed, 6 + 1)
            dve.sem_inc(used, 1)
            for f in range(2):
                dve.sem_inc(s_done[f], 1)

            def body(q, g0, n2, no2, par, out):
                n, no = n2 * 2 + par, no2 * 2 + par
                dve.wait_ge(in_m[par], n2 * LM + LM + 1)
                for c in range(RC):
                    m = n * RC + c
                    a, b = c % 2, (c + 1) % 2
                    if out:
                        dve.wait_ge(o_full, no * RC + c - 1 + 1) if c else dve.wait_ge(o_read, no * RC + 1)
                    for f, gs in enumerate(halves):
                        dve.wait_ge(x_full[f], m + 1 + 1)
                        dve.tensor_tensor(X[:, a, f, 0:NF], u[:, par, gs, c, :],
                                          psX[f][:, 0:P // 2].rearrange("p (g v) -> p g v", v=HD), ALU.add).then_inc(x_done[f], 1)
                    for f, gs in enumerate(halves):
                        dve.wait_ge(g_done[f], m + 1 + 1)
                        dve.wait_ge(s_full[f], m + 1 + 1)
                        dve.tensor_tensor(S[:, b, f, 0:NF], GS[:, gs],
                                          psS[f][:, 0:P // 2].rearrange("p (g v) -> p g v", v=HD), ALU.add).then_inc(s_done[f], 1)
                if out:
                    dve.wait_ge(o_full, no * RC + RC + 1)
                for f in range(2):
                    dve.wait_ge(s_done[f], n * RC + RC + 1 + 1)
                dve.sem_inc(used, 1)

            groups(dve, body)

        @block.tensor
        def _(pe):
            pe.wait_ge(zeroed, 6 + 1)

            def body(q, g0, n2, no2, par, out):
                n, no = n2 * 2 + par, no2 * 2 + par
                pe.wait_ge(in_m[par], n2 * LM + LM + 1)
                if out:
                    pe.wait_ge(in_q[par], no2 * LQ + LQ + 1)
                for c in range(RC):
                    m = n * RC + c
                    a = c % 2
                    for ps, w, rhs, ready, done in ((psX, bdw, S, s_done, x_full), (psS, bdr, X, x_done, s_full)):
                        for f in range(2):
                            pe.wait_ge(ready[f], m + 1 + 1)
                            for k in range(NG // 2):
                                g = f * NG // 2 + k
                                last = nc.tensor.matmul(ps[f][:, k * HD:k * HD + NMOV], chunk(w[:, par, g], c), streamed(rhs, a, g),
                                                        start=True, stop=True)
                            last.then_inc(done[f], 1)
                    if out:
                        pe.wait_ge(o_read, no * RC + c + 1)
                        for g in range(NG):
                            ps = psO[c % 2][0:HG * CH, g * HD:g * HD + NMOV]
                            nc.tensor.matmul(ps, chunk(bdq[:, par, g], c), streamed(S, a, g), start=True, stop=False)
                            last = nc.tensor.matmul(ps, chunk(bda[:, par, g], c), streamed(X, a, g), start=False, stop=True)
                        last.then_inc(o_full, 1)

            groups(pe, body)


def finish(nc, sems, ctx, consts, scratch, x_r, out_r, Wo1_d, Wo2_d, lnw_d, Wout_d):
    def sb(name, shape, dt=F32):
        return ctx.enter_context(nc.sbuf_tensor(f"f_{name}", shape, dt))

    def sem(name):
        return sems.new(nc, f"f_{name}")

    ident = consts["ident"]
    wout, wo1, wo2 = sb("wout", [P, KD, D]), sb("wo1", [P, KD, HD]), sb("wo2", [HD, D])
    lnw = sb("lnw", [P, D])
    o, x, r = sb("o", [P, 2, D]), sb("x", [P, 2, D]), sb("r", [P, 2, D])
    xn, xnT, yn, ynT = sb("xn", [P, D]), sb("xnT", [P, KD, P]), sb("yn", [P, D]), sb("ynT", [P, KD, P])
    g1, gate, res = sb("g1", [HD, P]), sb("gate", [P, D]), sb("res", [P, 2, D])
    st, mv, ve, lnv, rs, nt = (sb(m, [P, c]) for m, c in
                               (("st", 6), ("mv", 2), ("ve", 1), ("lnv", 1), ("rs", 1), ("nt", 1)))
    psT, psG1, psG, psY, psO = (ctx.enter_context(nc.psum_tensor(f"f_ps{m}", [P, 512], F32))
                                for m in ("T", "G1", "G", "Y", "O"))
    loaded, rows_in, stored = (sem("weights_loaded"), [sem(f"rows_in{b}") for b in range(2)],
                               [sem(f"rows_stored{b}") for b in range(2)])
    var_r, rs_r = sem("var_ready"), sem("rs_ready")
    xn_r, xT_f, xT_r, g1_f, g1_r, g_f, g_r = (sem(m) for m in ("xn", "xT_full", "xT", "g1_full", "g1", "gate_full", "gate"))
    yn_r, yT_f, yT_r, o_f, res_r = (sem(m) for m in ("yn", "yT_full", "yT", "o_full", "res"))
    dve_self, act_self = sem("dve_steps"), sem("act_steps")
    full, tail = divmod(NOUT, P)
    assert full % 2 == 1

    def tiles(eng, body):
        with eng.Fori(0, full // 2) as i:
            for par in range(2):
                body(i, (i * 2 + par) * P, par, P)
        body(full // 2, (full - 1) * P, 0, P)
        body(full // 2, full * P, 1, tail)

    passed_sp, passed_dve, passed_pool = (sem(f"passed_{e}") for e in ("sp", "dve", "pool"))
    sems.prime(nc)

    with nc.Block() as block:
        @block.sync
        def _(sp):
            sp.dma_start(wo1[:], Wo1_d.rearrange("(k p) n -> p k n", p=P)).then_inc(loaded, 16)
            for g in range(NG):
                sp.dma_start(wout[g * HD:(g + 1) * HD], Wout_d[g * P:(g + 1) * P, :].rearrange("(h v) n -> v h n", h=HG)).then_inc(loaded, 16)
            for h in range(HG):
                sp.dma_start(wo2[:, h * P:(h + 1) * P].rearrange("r (g v) -> r g v", g=NG),
                             Wo2_d.rearrange("r (g h v) -> r h g v", g=NG, h=HG)[:, h]).then_inc(loaded, 16)
                sp.dma_start(lnw[:, h * P:(h + 1) * P].rearrange("p (g v) -> p g v", g=NG),
                             lnw_d.rearrange("(a g h v) -> a h g v", a=1, g=NG, h=HG)[:, h].to_broadcast([P, NG, HD])).then_inc(loaded, 16)

            def body(n2, i0, par, rows):
                n = n2 * 2 + par
                sp.wait_ge(res_r, n + 1)
                settle(sp, passed_sp)
                sp.dma_start(o[0:rows, par].rearrange("p (h x) -> p h x", h=HG),
                             scratch["o"][:, bass.ds(i0 + OUT0, rows), :].rearrange("h t x -> t h x")).then_inc(rows_in[par], 16)
                for dst, src in ((x, x_r), (r, out_r)):
                    sp.dma_start(dst[0:rows, par], src[bass.ds(i0 * 3 + 1, 3 * rows - 2), :][0:3 * rows - 2:3, :])\
                      .then_inc(rows_in[par], 16)

            tiles(sp, body)

        @block.scalar
        def _(act):
            def rsqrt(k, rows):
                act.wait_ge(var_r, k + 1 + 1)
                act.activation(lnv[0:rows], ve[0:rows], ACT.Ln).then_inc(act_self, 1)
                act.wait_ge(act_self, k + 1 + 1)
                act.activation(rs[0:rows], lnv[0:rows], ACT.Exp, scale=-0.5).then_inc(rs_r, 1)

            def body(n2, i0, par, rows):
                n = n2 * 2 + par
                rsqrt(n * 2, rows)
                act.wait_ge(xT_f, n + 1 + 1)
                act.activation(xnT[:, :, 0:rows], psT[:].rearrange("p (k t) -> p k t", k=KD)[:, :, 0:rows], ACT.Copy).then_inc(xT_r, 1)
                act.wait_ge(g1_f, n + 1 + 1)
                act.activation(g1[:, 0:rows], psG1[0:HD, 0:rows], ACT.Copy).then_inc(g1_r, 1)
                act.wait_ge(g_f, n + 1 + 1)
                act.activation(gate[0:rows], psG[0:rows], ACT.Sigmoid).then_inc(g_r, 1)
                rsqrt(n * 2 + 1, rows)
                act.wait_ge(yT_f, n + 1 + 1)
                act.activation(ynT[:, :, 0:rows], psY[:].rearrange("p (k t) -> p k t", k=KD)[:, :, 0:rows], ACT.Copy).then_inc(yT_r, 1)
                act.wait_ge(res_r, n + 2 + 1)
                act.dma_start(out_r[bass.ds(i0 * 3 + 1, 3 * rows - 2), :][0:3 * rows - 2:3, :], res[0:rows, par])\
                   .then_inc(stored[par], 16)

            tiles(act, body)
            for par in range(2):
                act.wait_ge(stored[par], (full + 1) // 2 * 16 + 1)

        @block.vector
        def _(dve):
            dve.wait_ge(loaded, (1 + NG + 2 * HG) * 16 + 1)
            dve.sem_inc(res_r, 1)

            def norm(ch, k, src, dst, rows, done):
                ch.link(dve.bn_stats(st[0:rows], src))
                settle(dve, passed_dve)
                ch.link(dve.bn_aggr(mv[0:rows], st[0:rows]))
                ch.link(dve.tensor_scalar(ve[0:rows], mv[0:rows, 1:2], LN_EPS, None, ALU.add))
                dve.sem_inc(var_r, 1)
                dve.wait_ge(rs_r, k + 1 + 1)
                ch.link(dve.tensor_tensor(nt[0:rows], rs[0:rows], rs[0:rows], ALU.mult))
                ch.link(dve.tensor_tensor(nt[0:rows], nt[0:rows], ve[0:rows], ALU.mult))
                ch.link(dve.tensor_scalar(nt[0:rows], nt[0:rows], -0.5, 1.5, ALU.mult, ALU.add))
                ch.link(dve.tensor_tensor(rs[0:rows], nt[0:rows], rs[0:rows], ALU.mult))
                return dve.tensor_scalar(dst, src, mv[0:rows, 0:1], rs[0:rows], ALU.subtract, ALU.mult)

            def body(n2, i0, par, rows):
                n = n2 * 2 + par
                ch = Chain(dve, dve_self, n, 7 + 1 + 7 + 1)
                dve.wait_ge(rows_in[par], n2 * 48 + 48 + 1)
                norm(ch, n * 2, x[0:rows, par], xn[0:rows], rows, xn_r).then_inc(xn_r, 1)
                dve.wait_ge(g_r, n + 1 + 1)
                ch.link(dve.tensor_tensor(o[0:rows, par], o[0:rows, par], gate[0:rows], ALU.mult))
                ch.link(norm(ch, n * 2 + 1, o[0:rows, par], yn[0:rows], rows, None))
                dve.tensor_tensor(yn[0:rows], yn[0:rows], lnw[0:rows], ALU.mult).then_inc(yn_r, 1)
                dve.wait_ge(o_f, n + 1 + 1)
                dve.wait_ge(stored[par], n2 * 16 + 1)
                dve.tensor_tensor(res[0:rows, par], psO[0:rows], r[0:rows, par], ALU.add).then_inc(res_r, 1)
                ch.end()

            tiles(dve, body)

        @block.tensor
        def _(pe):
            pe.wait_ge(loaded, (1 + NG + 2 * HG) * 16 + 1)

            def body(n2, i0, par, rows):
                n = n2 * 2 + par
                pe.wait_ge(xn_r, n + 1 + 1)
                for kd in range(KD):
                    last = nc.tensor.transpose(psT[:, kd * P:kd * P + rows], xn[0:rows, kd * P:(kd + 1) * P], ident[0:rows, 0:rows])
                last.then_inc(xT_f, 1)
                pe.wait_ge(xT_r, n + 1 + 1)
                for kd in range(KD):
                    last = nc.tensor.matmul(psG1[0:HD, 0:rows], wo1[:, kd, :], xnT[:, kd, 0:rows], start=(kd == 0), stop=(kd == KD - 1))
                last.then_inc(g1_f, 1)
                pe.wait_ge(g1_r, n + 1 + 1)
                nc.tensor.matmul(psG[0:rows], g1[:, 0:rows], wo2[:], start=True, stop=True).then_inc(g_f, 1)
                pe.wait_ge(yn_r, n + 1 + 1)
                for kd in range(KD):
                    last = nc.tensor.transpose(psY[:, kd * P:kd * P + rows], yn[0:rows, kd * P:(kd + 1) * P], ident[0:rows, 0:rows])
                last.then_inc(yT_f, 1)
                pe.wait_ge(yT_r, n + 1 + 1)
                for kd in range(KD):
                    last = nc.tensor.matmul(psO[0:rows], ynT[:, kd, 0:rows], wout[:, kd, :], start=(kd == 0), stop=(kd == KD - 1))
                last.then_inc(o_f, 1)

            tiles(pe, body)


_INS = ["L0_attn_x", "L0_attn_Wq", "L0_attn_Wk", "L0_attn_Wv", "L0_attn_Wf1", "L0_attn_Wf2", "L0_attn_Wg",
        "L0_attn_Wo1", "L0_attn_Wo2", "L0_attn_ln_w", "L0_attn_Wout", "L0_ffn_kernel", "L0_ffn_input_scale",
        "L0_ffn_kernel_scale", "L0_ffn_bias"]


def kernel(**inputs):
    import numpy as _np
    import concourse.bacc as _bacc
    from concourse import mybir as _mybir
    from concourse.bass_utils import run_bass_kernel_spmd as _run

    nc = _bacc.Bacc("TRN2", target_bir_lowering=False, num_devices=1)
    arrays, args = {}, []
    for name in _INS:
        a = _np.ascontiguousarray(inputs[name])
        arrays[f"in_{name}"] = a
        args.append(nc.dram_tensor(f"in_{name}", a.shape, _mybir.dt.from_np(a.dtype), kind="ExternalInput").ap())
    out = nc.dram_tensor("out", (1, T, D), F32, kind="ExternalOutput").ap()
    program(nc, *args, out)
    r = _run(nc, [arrays], core_ids=[0])
    return r.results[0]["out"]
```

```python
import concourse.bass as bass
from concourse import mybir
from contextlib import ExitStack

F32 = mybir.dt.float32
BF16 = mybir.dt.bfloat16
U32 = mybir.dt.uint32
ALU = mybir.AluOpType
ACT = mybir.ActivationFunctionType

P = 128
T = 8192
D = 512
KD = D // P
HD = 32
H = D // HD
NG = D // P
HG = H // NG
CH = 16
SUB = CH // 2
MI = 2 * CH
NCH = T // CH
BT = 512
QT = 2048
NQ = T // QT
UN = QT // CH
PT = 256
PU = PT // CH
NP = QT // PT
RC = 8
OUT0 = (2 * T) // 3
NOUT = T - OUT0
QCH0 = (OUT0 // (CH * RC)) * RC
OT0 = QCH0 * CH
NSRC = 5
RGAM = HD * RC
RQ0 = RGAM + RC
RAQ = RQ0 + CH * RC
RW = RAQ + CH * RC
LN_EPS = 1e-5
NORM_EPS = 1e-12
ZMIN = -21.0
assert UN == P and (2 * T + 1) % 3 == 2


class Count:

    def __init__(self, sem, per):
        self.sem, self.per = sem, per

    def at(self, n, c):
        return n * self.per + c


class Chain:

    def __init__(self, eng, sem, n, per):
        self.eng, self.sem, self.n, self.per, self.c = eng, sem, n, per, 0

    def tick(self, ins):
        self.c += 1
        ins.then_inc(self.sem, 1)
        return self.c

    def wait(self, c=None):
        self.eng.wait_ge(self.sem, self.n * self.per + (self.c if c is None else c) + 1)

    def link(self, ins):
        self.tick(ins)
        self.wait()

    def end(self):
        assert self.c == self.per, (self.c, self.per)


class Semaphores(list):

    def new(self, nc, name):
        self.append(nc.alloc_semaphore(name=name))
        return self[-1]

    def prime(self, nc):
        with nc.Block() as block:
            @block.gpsimd
            def _(pool):
                for s in self:
                    pool.sem_inc(s, 1)

    def clear(self, nc):
        nc.clear_and_free_semaphores(self)
        nc.all_engine_barrier()


def settle(eng, passed):
    eng.sem_inc(passed, 1)


def program(nc, x_d, Wq_d, Wk_d, Wv_d, Wf1_d, Wf2_d, Wg_d, Wo1_d, Wo2_d, lnw_d, Wout_d,
            kern_d, sin_d, sk_d, bias_d, out_d):
    x_r = x_d.rearrange("a t d -> (a t) d")
    out_r = out_d.rearrange("a t d -> (a t) d")
    scratch = {m: nc.dram_tensor(f"{m}_scr", shape, F32).ap() for m, shape in dict(
        src=(NQ * NG, P, NSRC, QT),
        rec=(NQ * NG, P, UN // RC, RW),
        lv=(NQ * NG, P, NP, 2 * PU * MI),
        uw=(NQ * NG, P, UN // RC, 2 * HD * RC),
        o=(HG, T, NG * HD),
    ).items()}
    with ExitStack() as top:
        consts = make_constants(nc, top)

        def phase(run, *args):
            sems = Semaphores()
            with ExitStack() as ctx:
                run(nc, sems, ctx, *args)
            sems.clear(nc)

        for has_q, q0, q1 in ((False, 0, 2), (True, 2, NQ)):
            phase(project, consts, scratch, x_r, out_r, Wq_d, Wk_d, Wv_d, Wf1_d, Wf2_d, Wg_d,
                  kern_d, sin_d, sk_d, bias_d, has_q, q0, q1)
        phase(chunks, consts, scratch)
        phase(chain_states, scratch)
        phase(finish, consts, scratch, x_r, out_r, Wo1_d, Wo2_d, lnw_d, Wout_d)


def make_constants(nc, top):
    ident = top.enter_context(nc.sbuf_tensor("ident", [P, P], F32))
    ones_bd = top.enter_context(nc.sbuf_tensor("ones_bd", [P, HG, HD], F32))
    spread = top.enter_context(nc.sbuf_tensor("spread", [H, NG, HG, HD], F32))
    made = top.enter_context(nc.semaphore("consts_made"))
    with nc.Block() as block:
        @block.gpsimd
        def _(pool):
            pool.memset(ident[:], 0.0).then_inc(made, 1)
            pool.memset(ones_bd[:], 1.0).then_inc(made, 1)
            pool.memset(spread[:], 0.0).then_inc(made, 1)
            pool.wait_ge(made, 3)
            pool.affine_select(out=ident[:], in_=ident[:], compare_op=ALU.not_equal, fill=1.0,
                               base=0, pattern=[[-1, P]], channel_multiplier=1).then_inc(made, 1)
            pool.affine_select(out=ones_bd[:], in_=ones_bd[:], compare_op=ALU.is_ge, fill=0.0,
                               base=0, pattern=[[-HD, HG], [0, HD]], channel_multiplier=1).then_inc(made, 1)
            pool.affine_select(out=spread[:], in_=spread[:], compare_op=ALU.not_equal, fill=-1.0,
                               base=0, pattern=[[-HG, NG], [-1, HG], [0, HD]],
                               channel_multiplier=1).then_inc(made, 1)
            pool.wait_ge(made, 6)
            pool.affine_select(out=ones_bd[:], in_=ones_bd[:], compare_op=ALU.is_ge, fill=0.0,
                               base=HD - 1, pattern=[[HD, HG], [0, HD]], channel_multiplier=-1).then_inc(made, 1)
            pool.wait_ge(made, 7)
    return dict(ident=ident, ones_bd=ones_bd, spread=spread)


EXP_BITS = 0x7F800000
FP8_MIN = 2.0 ** -6
FP8_MAGIC = 1.5 * 2.0 ** 20


def project(nc, sems, ctx, consts, scratch, x_r, out_r, Wq_d, Wk_d, Wv_d, Wf1_d, Wf2_d, Wg_d,
            kern_d, sin_d, sk_d, bias_d, has_q, q0, q1):
    tag = "pq" if has_q else "p"

    def sb(name, shape, dt=F32):
        return ctx.enter_context(nc.sbuf_tensor(f"{tag}_{name}", shape, dt))

    def sem(name):
        return sems.new(nc, f"{tag}_{name}")

    NT = BT // P
    NB = QT // BT
    ident, ones_bd, spread = consts["ident"], consts["ones_bd"], consts["spread"]
    wk, wv = sb("wk", [P, KD, D]), sb("wv", [P, KD, D])
    wq = sb("wq", [P, KD, D]) if has_q else None
    wf1, wf2, wg = sb("wf1", [P, KD, HD]), sb("wf2", [HD, D]), sb("wg", [P, KD, H])
    kraw, kq = sb("kraw", [P, KD, D], BF16), sb("kq", [P, KD, D], BF16)
    bias = sb("bias", [P, D], BF16)
    scal = sb("scal", [P, 4])
    rsc = sb("rsc", [P, 2])
    osc = sb("osc", [P, 1])
    x = sb("x", [P, 2, NT, D])
    xn = sb("xn", [P, NT, D])
    xnT = sb("xnT", [P, 2, KD, BT])
    st, mv = sb("st", [P, NT, 6]), sb("mv", [P, NT, 2])
    ve, lnv, rs, nt = sb("ve", [P, NT]), sb("lnv", [P, NT]), sb("rs", [P, NT]), sb("nt", [P, NT])
    vq, cq = sb("vq", [P, KD, BT]), sb("cq", [P, KD, BT])
    xb, xq = sb("xb", [P, KD, BT], BF16), sb("xq", [P, KD, BT], BF16)
    f1 = sb("f1", [HD, BT])
    yg, bg, beta = sb("yg", [H, BT]), sb("bg", [H, BT]), sb("beta", [H, BT])
    kr, k2, kn, av = (sb(n, [P, NG, BT]) for n in ("kr", "k2", "kn", "av"))
    vt, z, lz = (sb(n, [P, NG, BT]) for n in ("vt", "z", "lz"))
    qt = sb("qt", [P, NG, BT]) if has_q else None
    kss = sb("kss", [P, NG, BT])
    yb = sb("yb", [P, NT, D], BF16)
    yo = sb("yo", [P, NT, D])
    nscale = sb("nscale", [P, 1])
    psA = [ctx.enter_context(nc.psum_tensor(f"{tag}_psA{i}", [P, 512], F32)) for i in range(4)]
    psD = [ctx.enter_context(nc.psum_tensor(f"{tag}_psD{i}", [P, 512], F32)) for i in range(4)]

    JA = 4 + 2 + 4 + 4 + (4 if has_q else 0) + 4
    JD = 12
    NLOAD = 11 if has_q else 10
    loaded = sem("weights_loaded")
    x_in = [sem(f"x_in{b}") for b in range(2)]
    setup = sem("setup")
    kern_ready = sem("kern_ready")
    act_psum = Count(sem("act_psum_full"), JA)
    act_free = Count(sem("act_psum_free"), JA)
    dve_psum = Count(sem("dve_psum_full"), JD)
    dve_free = Count(sem("dve_psum_free"), JD)
    var_ready = Count(sem("var_ready"), 1)
    rs_raw = Count(sem("rs_raw"), 1)
    xn_ready = Count(sem("xn_ready"), NT)
    xnT_ready = Count(sem("xnT_ready"), 1)
    v_scaled = Count(sem("v_scaled"), 1)
    cq_ready = Count(sem("magic_ready"), 1)
    xq_ready = Count(sem("xq_ready"), 1)
    k_sq = Count(sem("k_squared"), 1)
    kss_ready = Count(sem("k_sumsq_ready"), 1)
    rn_ready = Count(sem("k_rnorm_ready"), 1)
    kn_ready = Count(sem("kn_ready"), 1)
    z_ready = Count(sem("z_ready"), 1)
    lz_ready = Count(sem("log_z_ready"), 1)
    lf_ready = Count(sem("lf_ready"), 1)
    bln_ready = Count(sem("beta_log_ready"), 1)
    blm_ready = Count(sem("beta_arg_ready"), 1)
    beta_ready = Count(sem("beta_ready"), 1)
    a_ready = Count(sem("a_ready"), 1)
    silu_k = Count(sem("silu_k_ready"), 1)
    silu_v = Count(sem("silu_v_ready"), 1)
    silu_q = Count(sem("silu_q_ready"), 1)
    yb_ready = Count(sem("ffn_ready"), NT)
    yo_ready = Count(sem("rows_ready"), NT)
    stored_y = sem("stored_rows")
    stored_k, stored_a, stored_v, stored_lf, stored_q = (sem(f"stored_{n}") for n in ("k", "a", "v", "lf", "q"))
    act_self, pool_self = sem("act_steps"), sem("pool_steps")
    dve_steps = sem("dve_steps")
    act_norm, dve_norm = sem("act_norm_steps"), sem("dve_norm_steps")
    kern_steps = sem("kernel_steps")
    turns = q1 - q0

    def in_turns(eng, turn):
        with eng.Fori(0, turns - 1) as i:
            turn(i, False)
        turn(turns - 1, True)

    passed_sp, passed_dve, passed_pool = (sem(f"passed_{e}") for e in ("sp", "dve", "pool"))
    sems.prime(nc)

    with nc.Block() as block:
        def store_block(sp, i, s):
            n = i * NB + s
            it = (i + q0) * NG
            cols = slice(s * BT, (s + 1) * BT)
            sp.wait_ge(silu_v.sem, silu_v.at(n, 1) + 1)
            settle(sp, passed_sp)
            sp.dma_start(scratch["src"][bass.ds(it, NG), :, 2, cols].rearrange("g p t -> p g t"), vt[:]).then_inc(stored_v, 16)
            if has_q:
                sp.wait_ge(silu_q.sem, silu_q.at(n, 1) + 1)
                settle(sp, passed_sp)
                sp.dma_start(scratch["src"][bass.ds(it, NG), :, 4, cols].rearrange("g p t -> p g t"), qt[:]).then_inc(stored_q, 16)
            sp.wait_ge(lf_ready.sem, lf_ready.at(n, 1) + 1)
            settle(sp, passed_sp)
            sp.dma_start(scratch["src"][bass.ds(it, NG), :, 3, cols].rearrange("g p t -> p g t"), z[:]).then_inc(stored_lf, 16)
            sp.wait_ge(kn_ready.sem, kn_ready.at(n, 1) + 1)
            settle(sp, passed_sp)
            sp.dma_start(scratch["src"][bass.ds(it, NG), :, 0, cols].rearrange("g p t -> p g t"), kn[:]).then_inc(stored_k, 16)
            sp.wait_ge(a_ready.sem, a_ready.at(n, 1) + 1)
            settle(sp, passed_sp)
            sp.dma_start(scratch["src"][bass.ds(it, NG), :, 1, cols].rearrange("g p t -> p g t"), av[:]).then_inc(stored_a, 16)
            sp.wait_ge(yo_ready.sem, yo_ready.at(n, 2 * NT) + 1)
            settle(sp, passed_sp)
            row = (i * NB + (q0 * NB + s)) * BT
            sp.dma_start(out_r[bass.ds(row, BT), :].rearrange("(j p) d -> p j d", p=P), yo[:]).then_inc(stored_y, 16)

        @block.sync
        def _(sp):
            for dst, src in ((wk, Wk_d), (wv, Wv_d), (wf1, Wf1_d), (wg, Wg_d), (kraw, kern_d)) \
                    + (((wq, Wq_d),) if has_q else ()):
                sp.dma_start(dst[:], src.rearrange("(k p) n -> p k n", p=P)).then_inc(loaded, 16)
            sp.dma_start(wf2[:], Wf2_d).then_inc(loaded, 16)
            sp.dma_start(bias[:], bias_d.rearrange("(a n) -> a n", a=1).to_broadcast([P, D])).then_inc(loaded, 16)
            for c, s in ((0, sin_d), (1, sk_d)):
                sp.dma_start(scal[:, c:c + 1], s.rearrange("(a n) -> a n", a=1).to_broadcast([P, 1])).then_inc(loaded, 16)
            sp.dma_start(scal[:, 2:3], sin_d.rearrange("(a n) -> a n", a=1).to_broadcast([P, 1])).then_inc(loaded, 16)
            def load_block(i, s):
                n = i * NB + s
                sp.wait_ge(yo_ready.sem, n * NT + 1)
                settle(sp, passed_sp)
                row = (i * NB + (q0 * NB + s)) * BT
                sp.dma_start(x[:, s % 2, :, :],
                             x_r[bass.ds(row, BT), :].rearrange("(j p) d -> p j d", p=P)).then_inc(x_in[s % 2], 16)

            def turn(i, last):
                for s in range(NB):
                    if s + 1 < NB:
                        load_block(i, s + 1)
                    elif not last:
                        load_block(i + 1, 0)
                    store_block(sp, i, s)

            load_block(0, 0)
            in_turns(sp, turn)
            for sm in (stored_y, stored_k, stored_a, stored_v, stored_lf) + ((stored_q,) if has_q else ()):
                sp.wait_ge(sm, 16 * turns * NB + 1)

        @block.gpsimd
        def _(pool):
            pool.sem_inc(yo_ready.sem, NT)
            with pool.Fori(0, turns) as i:
                for s in range(NB):
                    n = i * NB + s
                    b = s % 2
                    ch = Chain(pool, pool_self, n, 2 + NT)
                    pool.wait_ge(xnT_ready.sem, xnT_ready.at(n, 1) + 1)
                    if s == 0:
                        pool.wait_ge(kern_ready, 1 + 1)
                    pool.wait_ge(yb_ready.sem, n * NT + 1)
                    settle(pool, passed_pool)
                    ch.link(pool.tensor_copy(xb[:], xnT[:, b]))
                    settle(pool, passed_pool)
                    pool.tensor_scalar(vq[:], xb[:], rsc[:, 0:1], None, ALU.mult).then_inc(v_scaled.sem, 1)
                    pool.wait_ge(cq_ready.sem, cq_ready.at(n, 1) + 1)
                    ch.link(pool.tensor_tensor(vq[:], vq[:], cq[:], ALU.add))
                    pool.tensor_tensor(xq[:], vq[:], cq[:], ALU.subtract).then_inc(xq_ready.sem, 1)
                    pool.wait_ge(silu_k.sem, silu_k.at(n, 1) + 1)
                    pool.tensor_tensor(k2[:], kr[:], kr[:], ALU.mult).then_inc(k_sq.sem, 1)
                    pool.wait_ge(rn_ready.sem, rn_ready.at(n, 1) + 1)
                    pool.wait_ge(stored_k, n * 16 + 1)
                    pool.wait_ge(a_ready.sem, n + 1)
                    pool.tensor_tensor(kn[:], kr[:], kss[:], ALU.mult).then_inc(kn_ready.sem, 1)
                    pool.wait_ge(stored_y, n * 16 + 1)
                    for j in range(NT):
                        pool.wait_ge(yb_ready.sem, yb_ready.at(n, j + 1) + 1)
                        ch.link(pool.tensor_tensor(yb[:, j], yb[:, j], bias[:], ALU.add))
                        pool.tensor_tensor(yo[:, j], yb[:, j], x[:, b, j], ALU.add).then_inc(yo_ready.sem, 1)
                    ch.end()

        @block.scalar
        def _(act):
            act.sem_inc(act_free.sem, 3)
            act.wait_ge(setup, 1 + 1)

            def rsqrt(n):
                ch = Chain(act, act_norm, n, 1)
                act.wait_ge(var_ready.sem, var_ready.at(n, 1) + 1)
                act.wait_ge(xn_ready.sem, n * NT + 1)
                ch.link(act.activation(lnv[:], ve[:], ACT.Ln))
                act.activation(rs[:], lnv[:], ACT.Exp, scale=-0.5).then_inc(rs_raw.sem, 1)
                ch.end()

            def turn(i, last):
                for s in range(NB):
                    n = i * NB + s
                    b = s % 2
                    job = [0]
                    ch = Chain(act, act_self, n, 2 + 2 + 1)

                    def take(out, func, done=None, scale=1.0, rows=P):
                        act.wait_ge(act_psum.sem, act_psum.at(n, job[0] + 1) + 1)
                        act.activation(out, psA[(s * JA + job[0]) % 4][0:rows, :], func, scale=scale)\
                           .then_inc(act_free.sem, 1)
                        job[0] += 1

                    act.wait_ge(xq_ready.sem, n + 1)
                    for kd in range(KD):
                        take(xnT[:, b, kd, :], ACT.Copy)
                    act.wait_ge(act_free.sem, act_free.at(n, job[0] + 3) + 1)
                    act.sem_inc(xnT_ready.sem, 1)
                    act.wait_ge(dve_psum.sem, dve_psum.at(n, 0) + 1)
                    take(f1[:], ACT.Copy, rows=HD)
                    take(yg[:], ACT.Copy, rows=H)
                    act.wait_ge(act_free.sem, act_free.at(n, job[0] + 3) + 1)
                    ch.link(act.activation(bg[:], yg[:], ACT.Abs))
                    ch.link(act.activation(bg[:], bg[:], ACT.Exp, scale=-1.0))
                    act.activation(bg[:], bg[:], ACT.Ln, bias=1.0).then_inc(bln_ready.sem, 1)
                    act.wait_ge(z_ready.sem, z_ready.at(n, 1) + 1)
                    act.wait_ge(lf_ready.sem, n + 1)
                    ch.link(act.activation(lz[:], z[:], ACT.Abs))
                    ch.link(act.activation(lz[:], lz[:], ACT.Exp, scale=-1.0))
                    act.activation(lz[:], lz[:], ACT.Ln, bias=1.0).then_inc(lz_ready.sem, 1)
                    act.wait_ge(blm_ready.sem, blm_ready.at(n, 1) + 1)
                    act.activation(beta[:], yg[:], ACT.Exp).then_inc(beta_ready.sem, 1)
                    act.wait_ge(a_ready.sem, n + 1)
                    act.wait_ge(kn_ready.sem, n + 1)
                    for g in range(NG):
                        take(kr[:, g, :], ACT.Silu)
                    act.wait_ge(act_free.sem, act_free.at(n, job[0] + 3) + 1)
                    act.sem_inc(silu_k.sem, 1)
                    act.wait_ge(stored_v, n * 16 + 1)
                    for g in range(NG):
                        take(vt[:, g, :], ACT.Silu)
                    act.wait_ge(act_free.sem, act_free.at(n, job[0] + 3) + 1)
                    act.sem_inc(silu_v.sem, 1)
                    if has_q:
                        act.wait_ge(stored_q, n * 16 + 1)
                        for g in range(NG):
                            take(qt[:, g, :], ACT.Silu)
                        act.wait_ge(act_free.sem, act_free.at(n, job[0] + 3) + 1)
                        act.sem_inc(silu_q.sem, 1)
                    if s + 1 < NB or not last:
                        rsqrt(n + 1)
                    act.wait_ge(kss_ready.sem, kss_ready.at(n, 1) + 1)
                    ch.link(act.activation(kss[:], kss[:], ACT.Ln, scale=NSC))
                    act.activation(kss[:], kss[:], ACT.Exp, scale=-0.5, bias=nscale[:]).then_inc(rn_ready.sem, 1)
                    act.wait_ge(yo_ready.sem, n * NT + NT + 1)
                    for j in range(NT):
                        act.wait_ge(act_psum.sem, act_psum.at(n, job[0] + 1) + 1)
                        act.activation(yb[:, j, :], psA[(s * JA + job[0]) % 4][:], ACT.Identity, scale=osc[:])\
                           .then_inc(act_free.sem, 1)
                        job[0] += 1
                        act.wait_ge(act_free.sem, act_free.at(n, job[0] + 3) + 1)
                        act.sem_inc(yb_ready.sem, 1)
                    assert job[0] == JA
                    ch.end()

            rsqrt(0)
            in_turns(act, turn)

        @block.vector
        def _(dve):
            ns = [0]

            def slink(ins):
                ns[0] += 1
                ins.then_inc(kern_steps, 1)
                dve.wait_ge(kern_steps, ns[0] + 1)

            dve.sem_inc(dve_free.sem, 3)
            dve.wait_ge(loaded, NLOAD * 16 + 1)
            slink(dve.memset(nscale[:], NBIAS))
            slink(dve.reciprocal(rsc[:, 0:1], scal[:, 0:1]))
            slink(dve.reciprocal(rsc[:, 1:2], scal[:, 1:2]))
            slink(dve.tensor_tensor(osc[:], scal[:, 0:1], scal[:, 1:2], ALU.mult))
            dve.sem_inc(setup, 1)
            wtmp = vq[:]
            slink(dve.tensor_scalar(wtmp, kraw[:], rsc[:, 1:2], None, ALU.mult))
            slink(dve.tensor_scalar(cq[:].bitcast(U32), wtmp.bitcast(U32), EXP_BITS, None, ALU.bitwise_and))
            slink(dve.tensor_scalar(cq[:], cq[:], FP8_MIN, FP8_MAGIC, ALU.max, ALU.mult))
            slink(dve.tensor_tensor(wtmp, wtmp, cq[:], ALU.add))
            slink(dve.tensor_tensor(kq[:], wtmp, cq[:], ALU.subtract))
            dve.sem_inc(kern_ready, 1)

            def statistics(n, i, s):
                ch = Chain(dve, dve_norm, n, NT + NT + 1 + 4)
                b = s % 2
                dve.wait_ge(x_in[b], (i * (NB // 2) + s // 2) * 16 + 16 + 1)
                for j in range(NT):
                    ch.tick(dve.bn_stats(st[:, j, :], x[:, b, j, :]))
                ch.wait()
                settle(dve, passed_dve)
                for j in range(NT):
                    ch.tick(dve.bn_aggr(mv[:, j, :], st[:, j, :]))
                ch.wait()
                ch.link(dve.tensor_scalar(ve[:], mv[:, :, 1], LN_EPS, None, ALU.add))
                dve.sem_inc(var_ready.sem, 1)
                return ch

            def rows(n, b, ch):
                dve.wait_ge(rs_raw.sem, rs_raw.at(n, 1) + 1)
                ch.link(dve.tensor_tensor(nt[:], rs[:], rs[:], ALU.mult))
                ch.link(dve.tensor_tensor(nt[:], nt[:], ve[:], ALU.mult))
                ch.link(dve.tensor_scalar(nt[:], nt[:], -0.5, 1.5, ALU.mult, ALU.add))
                ch.link(dve.tensor_tensor(rs[:], nt[:], rs[:], ALU.mult))
                ch.end()
                dve.wait_ge(xnT_ready.sem, n + 1)
                for j in range(NT):
                    dve.tensor_scalar(xn[:, j, :], x[:, b, j, :], mv[:, j, 0:1], rs[:, j:j + 1],
                                      ALU.subtract, ALU.mult).then_inc(xn_ready.sem, 1)

            def turn(i, last):
                for s in range(NB):
                    n = i * NB + s
                    b = s % 2
                    ch = Chain(dve, dve_steps, n, 1)
                    job = [0]

                    def bank():
                        dve.wait_ge(dve_psum.sem, dve_psum.at(n, job[0] + 1) + 1)
                        job[0] += 1
                        return psD[(s * JD + job[0] - 1) % 4]

                    dve.wait_ge(stored_lf, n * 16 + 1)
                    for g in range(NG):
                        dve.tensor_scalar(z[:, g, :], bank()[:], ZMIN, None, ALU.max).then_inc(dve_free.sem, 1)
                    dve.wait_ge(dve_free.sem, dve_free.at(n, 4 + 3) + 1)
                    dve.sem_inc(z_ready.sem, 1)
                    dve.wait_ge(bln_ready.sem, bln_ready.at(n, 1) + 1)
                    dve.scalar_tensor_tensor(out=yg[:], in0=yg[:], scalar=0.0, in1=bg[:], op0=ALU.min,
                                             op1=ALU.subtract).then_inc(blm_ready.sem, 1)
                    dve.wait_ge(lz_ready.sem, lz_ready.at(n, 1) + 1)
                    dve.scalar_tensor_tensor(out=z[:], in0=z[:], scalar=0.0, in1=lz[:], op0=ALU.min,
                                             op1=ALU.subtract).then_inc(lf_ready.sem, 1)
                    dve.wait_ge(v_scaled.sem, v_scaled.at(n, 1) + 1)
                    dve.wait_ge(xq_ready.sem, n + 1)
                    ch.link(dve.tensor_scalar(cq[:].bitcast(U32), vq[:].bitcast(U32), EXP_BITS, None, ALU.bitwise_and))
                    dve.tensor_scalar(cq[:], cq[:], FP8_MIN, FP8_MAGIC, ALU.max, ALU.mult).then_inc(cq_ready.sem, 1)
                    following = s + 1 < NB or not last
                    if following:
                        norm = statistics(n + 1, *((i, s + 1) if s + 1 < NB else (i + 1, 0)))
                    dve.wait_ge(kn_ready.sem, n + 1)
                    for g in range(NG):
                        dve.tensor_scalar(kss[:, g, :], bank()[:], NORM_EPS ** 2, None, ALU.max).then_inc(dve_free.sem, 1)
                    dve.wait_ge(dve_free.sem, dve_free.at(n, 8 + 3) + 1)
                    dve.sem_inc(kss_ready.sem, 1)
                    if following:
                        rows(n + 1, 1 - b, norm)
                    dve.wait_ge(kn_ready.sem, kn_ready.at(n, 1) + 1)
                    dve.wait_ge(stored_a, n * 16 + 1)
                    for g in range(NG):
                        dve.tensor_tensor(av[:, g, :], bank()[:], kn[:, g, :], ALU.mult).then_inc(dve_free.sem, 1)
                    dve.wait_ge(dve_free.sem, dve_free.at(n, 12 + 3) + 1)
                    dve.sem_inc(a_ready.sem, 1)
                    ch.end()

            rows(0, 0, statistics(0, 0, 0))
            in_turns(dve, turn)

        @block.tensor
        def _(pe):
            pe.wait_ge(loaded, NLOAD * 16 + 1)
            pe.wait_ge(kern_ready, 1 + 1)
            with pe.Fori(0, turns) as i:
                for s in range(NB):
                    n = i * NB + s
                    b = s % 2
                    ja, jd = [0], [0]

                    def bank_a():
                        pe.wait_ge(act_free.sem, act_free.at(n, ja[0]) + 1)
                        ja[0] += 1
                        return psA[(s * JA + ja[0] - 1) % 4]

                    def bank_d():
                        pe.wait_ge(dve_free.sem, dve_free.at(n, jd[0]) + 1)
                        jd[0] += 1
                        return psD[(s * JD + jd[0] - 1) % 4]

                    pe.wait_ge(xn_ready.sem, xn_ready.at(n, NT) + 1)
                    for kd in range(KD):
                        ps = bank_a()
                        for j in range(NT):
                            last = nc.tensor.transpose(ps[:, j * P:(j + 1) * P], xn[:, j, kd * P:(kd + 1) * P], ident[:])
                        last.then_inc(act_psum.sem, 1)
                    pe.wait_ge(xnT_ready.sem, xnT_ready.at(n, 1) + 1)

                    def product(ps, w, rows):
                        for kd in range(KD):
                            last = nc.tensor.matmul(ps[0:rows, :], w(kd), xnT[:, b, kd, :],
                                                    start=(kd == 0), stop=(kd == KD - 1))
                        return last

                    product(bank_a(), lambda kd: wf1[:, kd, :], HD).then_inc(act_psum.sem, 1)
                    product(bank_a(), lambda kd: wg[:, kd, :], H).then_inc(act_psum.sem, 1)
                    pe.wait_ge(act_free.sem, act_free.at(n, KD + 1 + 3) + 1)
                    for g in range(NG):
                        ps = bank_d()
                        nc.tensor.matmul(ps[:], wf2[:, g * P:(g + 1) * P], f1[:], start=True, stop=True)\
                          .then_inc(dve_psum.sem, 1)
                    for w in (wk, wv) + ((wq,) if has_q else ()):
                        for g in range(NG):
                            product(bank_a(), lambda kd: w[:, kd, g * P:(g + 1) * P], P).then_inc(act_psum.sem, 1)
                    pe.wait_ge(k_sq.sem, k_sq.at(n, 1) + 1)
                    for g in range(NG):
                        ps = bank_d()
                        nc.tensor.matmul(ps[:], ones_bd[:].rearrange("p h c -> p (h c)"), k2[:, g, :],
                                         start=True, stop=True).then_inc(dve_psum.sem, 1)
                    pe.wait_ge(xq_ready.sem, xq_ready.at(n, 1) + 1)
                    for j in range(NT):
                        ps = bank_a()
                        for kd in range(KD):
                            last = nc.tensor.matmul(ps[:], xq[:, kd, j * P:(j + 1) * P], kq[:, kd, :],
                                                    start=(kd == 0), stop=(kd == KD - 1))
                        last.then_inc(act_psum.sem, 1)
                    pe.wait_ge(beta_ready.sem, beta_ready.at(n, 1) + 1)
                    for g in range(NG):
                        ps = bank_d()
                        nc.tensor.matmul(ps[:], spread[:, g].rearrange("p h c -> p (h c)"), beta[:],
                                         start=True, stop=True).then_inc(dve_psum.sem, 1)
                    assert ja[0] == JA and jd[0] == JD


NSC = 2.0 ** 20
NBIAS = 10.0 * 0.6931471805599453


def chunks(nc, sems, ctx, consts, scratch):
    def sb(name, shape, dt=F32):
        return ctx.enter_context(nc.sbuf_tensor(f"c_{name}", shape, dt))

    def sem(name):
        return sems.new(nc, f"c_{name}")

    ident = consts["ident"]
    RG = PU // RC
    NS = PT // SUB
    W = PU * MI
    NB = 3
    src = sb("src", [P, NB, NSRC, PT])
    keep = sb("keep", [P, NS, SUB])
    g8 = sb("g8", [P, PT])
    gm = sb("gm", [P, 2, PT, 2])
    dm, he = sb("dm", [P, 2, W]), sb("he", [P, 2, W])
    en, ff = sb("en", [P, PT, 2]), sb("ff", [P, PT, 2])
    LQ = MI + CH
    LQS = LQ + CH + SUB
    NMOV = 96
    lqx = sb("lqx", [P, 2, (PU + 1) * LQS])
    lqv = lqx[:].rearrange("p b (u x) -> p b u x", x=LQS)[:, :, 0:PU]
    lq, lq8 = lqv[:, :, :, 0:LQ], lqv[:, :, :, LQ:LQS]
    rr = sb("rr", [P, 2, MI, 2, PU])
    l0, re = sb("l0", [P, PU, MI]), sb("re", [P, PU, MI])
    vm = sb("vm", [P, PT, 2])
    rec = sb("rec", [P, 2, RG, RW])
    lv = sb("lv", [P, 2, PU, 2, HD])
    lvc = sb("lvc", [P, 2, PU * 2 * HD])
    bda = sb("bda", [P, 2, HG, MI, 2, PU])
    bdt = sb("bdt", [P, 2, HG, MI, PU])
    dst = sb("dstk", [P, UN, MI])
    cst = sb("cstk", [P, UN, CH])
    ttr = sb("ttr", [P, NP, MI, PU])
    tl = sb("tl", [P, MI, HG, MI])
    lmask = sb("lmask", [P, CH, CH])
    wsb = sb("wsb", [P, 2, PU, HD])
    uwsb = sb("uwsb", [P, 2, RG, 2 * HD * RC])
    qmask, cmask = sb("qmask", [P, CH]), sb("cmask", [P, SUB])
    HD_DVE = 1
    tmpd = sb("tmpd", [P, HD_DVE, CH * (CH - 1)])
    tmpg = sb("tmpg", [P, HG - HD_DVE, CH * (CH - 1)])

    def ps(name, banks):
        return ctx.enter_context(nc.psum_tensor(f"c_{name}", [P, banks * 512], F32))

    psD, psC = ([ps(f"{m}{i}", n) for i in range(2)] for m, n in (("psD", 2), ("psC", 1)))
    psL = [psC[0], psC[1], psD[0], psD[1]]
    psW = ps("psW", 2)
    dslot = [t[:].rearrange("p (a x) -> p a x", a=RG)[:, :, 0:RC * LQ].rearrange("p a (r x) -> p a r x", r=RC) for t in psD]
    cslot = [t[:, 0:PU * (CH + SUB)].rearrange("p (u x) -> p u x", u=PU) for t in psC]
    wslot = psW[:].rearrange("p (u x) -> p u x", x=2 * HD)

    ITEMS = NQ * NG
    NOQ = (OT0 // QT) * NG
    NB_BACK, NB_IN, NB_X = 8, 8, 4
    NL = NB_BACK + NB_IN + NB_X
    bdr_in, bdt_in, store1, store2 = ([sem(f"{m}{b}") for b in range(2)] for m in
                                      ("bd_right_in", "bd_left_in", "stored_right", "stored_uw"))
    x_in = [sem(f"pieces_in{b}") for b in range(NB)]
    src_free = sem("pieces_used")
    gm_ready, vm_ready = sem("gm_ready"), sem("vm_ready")
    exps = sem("exps_ready")
    rows_l, rows_ready, tm_ready = sem("left_rows_ready"), sem("rows_ready"), sem("row_major_ready")
    prods = sem("products_full")
    prods_free = sem("products_free")
    aq_free = sem("q_products_read")
    lanes, lanes_free = sem("lane_banks_full"), sem("lane_banks_free")
    mats, solved, tt_ready = sem("matrices_ready"), sem("solved"), sem("inverse_ready")
    uw, uw_free = sem("uw_full"), sem("uw_read")
    wt_ready = sem("w_transposed")
    setup, pool_setup, dve_setup = sem("setup"), sem("pool_setup"), sem("dve_setup")
    front_steps, back_steps, q_steps = sem("dve_front_steps"), sem("dve_back_steps"), sem("dve_q_steps")
    dve_solve, pool_solve = sem("dve_solve_steps"), sem("pool_solve_steps")
    passed_sp, passed_dve = sem("passed_sp"), sem("passed_dve")
    sems.prime(nc)
    SOLVE_STEPS = 2 * (MI - 2)
    ROUNDS = [1 + (MI - 2) * p // NP for p in range(NP + 1)]

    def pair(i, p):
        return i * (NP // 2) + p // 2

    def turns(body):
        for i in range(2):
            body(i, False, True, i > 0, False)
        return [(2, NOQ, False), (NOQ, ITEMS, True)]

    def run(eng, body):
        for a, b, has_q in turns(body):
            with eng.Fori(a, b) as i:
                body(i, has_q, True, True, True)
        body(ITEMS, True, False, True, True)
        body(ITEMS + 1, True, False, False, True)

    def loads(i, p):
        b = p % NB
        return i * len(range(b, NP, NB)) + p // NB + 1

    def freed(i, p):
        return i * NP + (p - NB + 1 if p >= NB else max(range(p, NP, NB)) - NP + 1)

    def solve_rounds(eng, ch, tmp, h0, h1, first, last):
        nh = h1 - h0
        tlh = tl[:].rearrange("p s h r -> p h s r")
        for r in range(first, last):
            below, left = MI - 1 - r, r
            col = tlh[:, h0:h1, r + 1:MI, r:r + 1].to_broadcast([P, nh, below, left])
            row = tlh[:, h0:h1, r:r + 1, 0:r].to_broadcast([P, nh, below, left])
            t = tmp[:, 0:nh, 0:below * left].rearrange("p h (b l) -> p h b l", l=left)
            ch.link(eng.tensor_tensor(t, col, row, ALU.mult))
            acc = tlh[:, h0:h1, r + 1:MI, 0:r]
            ch.link(eng.tensor_tensor(acc, acc, t, ALU.add))

    with nc.Block() as block:
        @block.sync
        def _(sp):
            def load(i, p, has_q):
                sp.wait_ge(src_free, freed(i, p) + 2 + 1)
                settle(sp, passed_sp)
                ns = NSRC if has_q else NSRC - 1
                sp.dma_start(src[:, p % NB, 0:ns, :], scratch["src"][bass.ds(i, 1), :, 0:ns, p * PT:(p + 1) * PT]
                             .rearrange("a p m t -> p (a m) t")).then_inc(x_in[p % NB], 16)

            def bd_right(i, p):
                j = i * NP + p
                sp.wait_ge(rows_l, j + 1 + 1)
                settle(sp, passed_sp)
                sp.wait_ge(prods, j + 1 + 1)
                settle(sp, passed_sp)
                for h in range(HG):
                    r = slice(h * HD, (h + 1) * HD)
                    sp.dma_start(bda[r, p % 2, h], rr[r, p % 2]).then_inc(bdr_in[p % 2], 16)

            def out_right(i, p, has_q):
                j = i * NP + p
                sp.wait_ge(tm_ready, j + 1 + 1)
                settle(sp, passed_sp)
                sp.dma_start(scratch["lv"][bass.ds(i, 1), :, p, :].rearrange("a p x -> p (a x)"),
                             lv[:, p % 2].rearrange("p u m d -> p (u m d)")).then_inc(store1[p % 2], 16)
                if has_q:
                    sp.wait_ge(aq_free, (i - NOQ) * NP + p + 2 + 1)
                    settle(sp, passed_sp)
                rw = RW if has_q else RQ0
                sp.dma_start(scratch["rec"][bass.ds(i, 1), :, p * RG:(p + 1) * RG, 0:rw].rearrange("a p u c -> p (a u) c"),
                             rec[:, p % 2, :, 0:rw]).then_inc(store1[p % 2], 16)

            def bd_left(c, p):
                j = c * NP + p
                sp.wait_ge(uw, 2 * j + 1)
                settle(sp, passed_sp)
                for h in range(HG):
                    r = slice(h * HD, (h + 1) * HD)
                    sp.dma_start(bdt[r, p % 2, h], ttr[r, p]).then_inc(bdt_in[p % 2], 16)
                sp.dma_start(lvc[:, p % 2], scratch["lv"][bass.ds(c, 1), :, p, :]
                             .rearrange("a p x -> p (a x)")).then_inc(bdt_in[p % 2], 16)

            def out_left(c, p):
                sp.wait_ge(wt_ready, c * NP + p + 1 + 1)
                settle(sp, passed_sp)
                sp.dma_start(scratch["uw"][bass.ds(c, 1), :, p * RG:(p + 1) * RG, :].rearrange("a p u c -> p (a u) c"),
                             uwsb[:, p % 2]).then_inc(store2[p % 2], 16)

            def body(i, has_q, make, solve, out):
                if make:
                    load(i, 0, has_q)
                    load(i, 1, has_q)
                if out:
                    sp.wait_ge(tt_ready, i - 2 + 1 + 1)
                    settle(sp, passed_sp)
                    for b in range(2):
                        sp.wait_ge(store1[b], (i - 2 + 1) * (NP // 2 * 32) + 1)
                        settle(sp, passed_sp)
                    bd_left(i - 2, 0)
                for p in range(NP):
                    if make:
                        if p + 2 < NP:
                            load(i, p + 2, has_q)
                        bd_right(i, p)
                        if p:
                            out_right(i, p - 1, has_q)
                    if out:
                        if p + 1 < NP:
                            bd_left(i - 2, p + 1)
                        if p:
                            out_left(i - 2, p - 1)
                if make:
                    out_right(i, NP - 1, has_q)
                if out:
                    out_left(i - 2, NP - 1)

            sp.wait_ge(setup, 2 + 1)
            run(sp, body)
            for b in range(2):
                sp.wait_ge(store1[b], ITEMS * (NP // 2) * 32 + 1)
                sp.wait_ge(store2[b], ITEMS * (NP // 2) * 16 + 1)

        @block.gpsimd
        def _(pool):
            n = [0]

            def link(ins):
                n[0] += 1
                ins.then_inc(pool_setup, 1)
                pool.wait_ge(pool_setup, n[0] + 1)

            for t in (bdt, lqx, lvc, rr, gm, vm, tl, rec):
                link(pool.memset(t[:], 0.0))
            for t in (keep, lmask, qmask, cmask):
                link(pool.memset(t[:], 1.0))
            link(pool.memset(keep[:, :, 0:1], 0.0))
            link(pool.affine_select(out=tl[:], in_=tl[:], compare_op=ALU.not_equal, fill=1.0, base=0,
                                    pattern=[[1, MI], [0, HG], [-1, MI]], channel_multiplier=0))
            link(pool.affine_select(out=lmask[:], in_=lmask[:], compare_op=ALU.is_gt, fill=0.0, base=0,
                                    pattern=[[1, CH], [-1, CH]], channel_multiplier=0))
            for h in range(HG):
                r = slice(h * HD, (h + 1) * HD)
                link(pool.affine_select(out=qmask[r], in_=qmask[r], compare_op=ALU.is_ge, fill=0.0, base=1,
                                        pattern=[[2, CH]], channel_multiplier=-1))
                link(pool.affine_select(out=qmask[r, SUB:CH], in_=qmask[r, SUB:CH], compare_op=ALU.is_ge, fill=0.0,
                                        base=-CH, pattern=[[0, SUB]], channel_multiplier=1))
                link(pool.affine_select(out=cmask[r], in_=cmask[r], compare_op=ALU.is_ge, fill=0.0,
                                        base=CH - 1, pattern=[[0, SUB]], channel_multiplier=-1))
            pool.sem_inc(setup, 1)

            def body(i, has_q, make, solve, out):
                if solve:
                    ch = Chain(pool, pool_solve, i - 1, SOLVE_STEPS)
                    pool.wait_ge(mats, i - 1 + 2)
                    solve_rounds(pool, ch, tmpg, HD_DVE, HG, 1, MI - 1)
                    pool.sem_inc(solved, 1)
                    ch.end()

            run(pool, body)

        @block.scalar
        def _(act):
            def body(i, has_q, make, solve, out):
                def read_uw(p):
                    j = (i - 2) * NP + p
                    act.wait_ge(store2[p % 2], pair(i - 2, p) * 16 + 1)
                    for c in range(RG):
                        act.wait_ge(uw, 2 * j + c + 3 + 1)
                        us = slice(c * RC, (c + 1) * RC)
                        act.activation(wsb[:, p % 2, us, :], wslot[:, us, 0:HD], ACT.Copy)
                        act.activation(uwsb[:, p % 2, c, 0:HD * RC].rearrange("p (r v) -> p r v", r=RC),
                                       wslot[:, us, HD:2 * HD], ACT.Copy).then_inc(uw_free, 1)

                def read_products(p):
                    us = slice(p * PU, (p + 1) * PU)
                    act.wait_ge(prods, i * NP + p + 3 + 1)
                    act.activation(dst[:, us, :].rearrange("p (a r) m -> p a r m", r=RC), dslot[p % 2][:, :, :, 0:MI], ACT.Copy)
                    act.activation(cst[:, us, :], cslot[p % 2][:, :, 0:CH], ACT.Copy).then_inc(prods_free, 1)

                for p in range(NP):
                    if make:
                        j = i * NP + p
                        b = p % 2
                        act.wait_ge(gm_ready, j + 1 + 1)
                        act.wait_ge(rows_ready, j + 1)
                        act.activation(en[:].rearrange("p t m -> p (t m)"), dm[:, b], ACT.Exp, scale=-1.0)
                        act.activation(dm[:, b], dm[:, b], ACT.Exp)
                        act.activation(ff[:], gm[:, b], ACT.Exp)
                        act.activation(he[:, b], he[:, b], ACT.Exp).then_inc(exps, 1)
                        act.activation(vm[:, :, 1], src[:, p % NB, 2, :], ACT.Copy).then_inc(vm_ready, 1)
                        if p:
                            read_products(p - 1)
                    if out and p + 1 < NP:
                        read_uw(p)
                if make:
                    read_products(NP - 1)
                if out:
                    read_uw(NP - 1)
                if solve:
                    act.wait_ge(uw, 2 * NP * (i - 1) + 2 + 1)
                    for k in range(NB_BACK):
                        act.wait_ge(lanes, i * NL - NB_BACK + k + 1 + 1)
                        act.activation(ttr[:, :, 4 * k:4 * k + 4, :].rearrange("p a s u -> p s a u"),
                                       psL[k % 4][:, 0:512].rearrange("p (s a u) -> p s a u", s=4, u=PU), ACT.Copy).then_inc(lanes_free, 1)
                    act.wait_ge(lanes_free, i * NL + 3 + 1)
                    act.sem_inc(tt_ready, 1)
                if make:
                    act.wait_ge(lanes_free, i * NL + NB_IN + 3 + 1)
                    for k in range(NB_X):
                        act.wait_ge(lanes, i * NL + NB_IN + k + 1 + 1)
                        s0 = CH + 4 * k
                        act.activation(tl[:, s0:s0 + 4, :, 0:CH],
                                       psL[k % 4][:, 0:512].rearrange("p (s h r) -> p s h r", s=4, h=HG)[:, :, :, 0:CH], ACT.Copy)\
                           .then_inc(lanes_free, 1)
                    act.wait_ge(lanes_free, i * NL + NB_IN + NB_X + 3 + 1)
                    act.sem_inc(mats, 1)

            act.wait_ge(setup, 2 + 1)
            run(act, body)

        @block.vector
        def _(dve):
            dve.memset(bda[:], 0.0).then_inc(dve_setup, 1)
            dve.wait_ge(dve_setup, 1 + 1)
            dve.wait_ge(setup, 1 + 1)
            for s, credit in ((src_free, 2), (exps, 1), (prods, 2), (prods_free, 1), (lanes_free, 3), (aq_free, 1), (uw, 2), (uw_free, 1)):
                dve.sem_inc(s, credit)
            dve.sem_inc(setup, 1)

            def front(i, p):
                j = i * NP + p
                b = p % 2
                ch = Chain(dve, front_steps, j, 5)
                gmv = gm[:, b].rearrange("p (n s) m -> p n s m", s=SUB)
                g8v = g8[:].rearrange("p (n s) -> p n s", s=SUB)
                dve.wait_ge(x_in[p % NB], loads(i, p) * 16 + 1)
                ch.link(dve.tensor_tensor_scan(out=g8[:], data0=keep[:].rearrange("p n s -> p (n s)"),
                                               data1=src[:, p % NB, 3, :], initial=0.0, op0=ALU.mult, op1=ALU.add))
                dve.wait_ge(exps, j + 1)
                ch.tick(dve.tensor_copy(gm[:, b, :, 1], g8[:]))
                ch.link(dve.tensor_copy(gmv[:, :, 1:SUB, 0], g8v[:, :, 0:SUB - 1]))
                gmn = gm[:, b].rearrange("p (n s) m -> p n (s m)", s=SUB)
                mid = g8v[:, :, SUB // 2 - 1:SUB // 2].to_broadcast([P, NS, 2 * SUB])
                end = g8v[:, :, SUB - 1:SUB].to_broadcast([P, NS, 2 * SUB])
                ch.tick(dve.tensor_tensor(dm[:, b].rearrange("p (n s) -> p n s", n=NS), gmn, mid, ALU.subtract))
                ch.link(dve.tensor_tensor(he[:, b].rearrange("p (n s) -> p n s", n=NS), end, gmn, ALU.subtract))
                dve.sem_inc(gm_ready, 1)
                ch.end()

            def grouped(t):
                return t.rearrange("p (a r) t -> p a r t", r=RC)

            def back(i, p, has_q):
                j = i * NP + p
                b = p % 2
                ch = Chain(dve, back_steps, j, 3)
                dve.wait_ge(exps, j + 2 + 1)
                dve.wait_ge(prods, j + 1 + 1)
                ep, hh = (t[:, b].rearrange("p (t m) -> p t m", m=2) for t in (dm, he))
                kk = src[:, p % NB, 0, :].unsqueeze(2).to_broadcast([P, PT, 2])
                aa = src[:, p % NB, 1, :].unsqueeze(2).to_broadcast([P, PT, 2])

                def half(t, c):
                    return t.rearrange("p (u c s) m -> p u c s m", u=PU, c=2)[:, :, c]

                def v3(t):
                    return t.rearrange("p u (s m) -> p u s m", m=2)

                def v3t(t):
                    return t.rearrange("p (s m) u -> p u s m", m=2)

                def full(t):
                    return t.rearrange("p (u s) m -> p u s m", u=PU)

                rd, r8 = rr[:, b, :, 0, :], rr[:, b, 0:CH, 1, :]
                dve.tensor_tensor(v3t(rd), full(kk), full(en[:]), ALU.mult)
                dve.tensor_tensor(v3t(r8), half(kk, 0), half(hh, 0), ALU.mult)
                dve.tensor_tensor(v3(lq[:, b, :, 0:MI]), full(aa), full(ep), ALU.mult)
                gf = ff[:].rearrange("p (u t) m -> p u (t m)", u=PU)
                gfirst, gsec = gf[:, :, CH - 1:CH], gf[:, :, MI - 1:MI]
                if has_q:
                    qv = src[:, p % NB, 4, :].rearrange("p (u t) -> p u t", u=PU)
                    dve.tensor_tensor(lq[:, b, :, MI:MI + CH], qv, ep[:, :, 1].rearrange("p (u t) -> p u t", u=PU), ALU.mult)
                    ffq = ff[:, :, 1].rearrange("p (u t) -> p u t", u=PU)
                    dve.tensor_tensor(lq8[:, b, :, CH:CH + SUB], qv[:, :, SUB:CH], ffq[:, :, SUB:CH], ALU.mult)
                ch.link(dve.tensor_tensor(v3(lq8[:, b, :, 0:CH]), half(aa, 1), half(ff[:], 1), ALU.mult))
                dve.sem_inc(rows_l, 1)
                dve.tensor_tensor(v3(l0[:, :, 0:CH]), half(aa, 0), half(ff[:], 0), ALU.mult)
                dve.tensor_tensor(l0[:, :, CH:MI], lq8[:, b, :, 0:CH], gfirst.to_broadcast([P, PU, CH]), ALU.mult)
                dve.tensor_tensor(v3(re[:, :, CH:MI]), half(kk, 1), half(hh, 1), ALU.mult)
                ch.link(dve.tensor_tensor(re[:, :, 0:CH], r8.rearrange("p m u -> p u m"), gsec.to_broadcast([P, PU, CH]), ALU.mult))
                dve.wait_ge(store1[b], pair(i, p) * 32 + 1)
                if has_q:
                    q0v = rec[:, b, :, RQ0:RAQ].rearrange("p a (t r) -> p a r t", r=RC)
                    dve.tensor_tensor(q0v[:, :, :, 0:SUB], grouped(qv[:, :, 0:SUB]), grouped(ffq[:, :, 0:SUB]), ALU.mult)
                    dve.tensor_tensor(q0v[:, :, :, SUB:CH], grouped(lq8[:, b, :, CH:CH + SUB]),
                                      grouped(gfirst.to_broadcast([P, PU, SUB])), ALU.mult)
                dve.tensor_tensor(rec[:, b, :, RGAM:RQ0].unsqueeze(3), grouped(gfirst), grouped(gsec), ALU.mult)
                dve.wait_ge(vm_ready, j + 1 + 1)
                dve.transpose(lv[:, b, :, 0, :], l0[:])
                dve.transpose(lv[:, b, :, 1, :], vm[:].rearrange("p (u t) m -> p u (t m)", u=PU))
                for a in range(RG):
                    last = dve.transpose(rec[:, b, a, 0:RGAM].rearrange("p (c r) -> p r c", r=RC), re[:, a * RC:(a + 1) * RC, :])
                ch.link(last)
                for s in (tm_ready, rows_ready, src_free):
                    dve.sem_inc(s, 1)
                ch.end()

            def w_turned(c, p):
                j = c * NP + p
                dve.wait_ge(uw_free, 2 * j + 3 + 1)
                for a in range(RG):
                    last = dve.transpose(uwsb[:, p % 2, a, HD * RC:].rearrange("p (m r) -> p r m", r=RC),
                                         wsb[:, p % 2, a * RC:(a + 1) * RC, :])
                last.then_inc(wt_ready, 1)

            def read_q(i, p):
                jq = (i - NOQ) * NP + p
                b = p % 2
                ch = Chain(dve, q_steps, jq, 1)
                dve.wait_ge(prods_free, i * NP + p + 2 + 1)
                pq, pc = dslot[b][:, :, :, MI:LQ], cslot[b][:, :, CH:CH + SUB]
                aqv = rec[:, b, :, RAQ:RW].rearrange("p a (t r) -> p a r t", r=RC)
                settle(dve, passed_dve)
                ch.link(dve.copy_predicated(out=aqv, data=pq, mask=grouped(
                    qmask[:].bitcast(U32).unsqueeze(1).to_broadcast([P, PU, CH]))))
                settle(dve, passed_dve)
                dve.copy_predicated(out=aqv[:, :, :, SUB:CH], data=grouped(pc), mask=grouped(
                    cmask[:].bitcast(U32).unsqueeze(1).to_broadcast([P, PU, SUB]))).then_inc(aq_free, 1)
                ch.end()

            def body(i, has_q, make, solve, out):
                if make:
                    front(i, 0)
                ch = Chain(dve, dve_solve, i - 1, SOLVE_STEPS) if solve else None
                for p in range(NP):
                    if make:
                        if p + 1 < NP:
                            front(i, p + 1)
                        back(i, p, has_q)
                    if solve:
                        if p == 0:
                            dve.wait_ge(mats, i - 1 + 2)
                        solve_rounds(dve, ch, tmpd, 0, HD_DVE, ROUNDS[p], ROUNDS[p + 1])
                    if p and make and has_q:
                        read_q(i, p - 1)
                    if p and out:
                        w_turned(i - 2, p - 1)
                if solve:
                    dve.sem_inc(solved, 1)
                    ch.end()
                if make and has_q:
                    read_q(i, NP - 1)
                if out:
                    w_turned(i - 2, NP - 1)
                if not make:
                    return
                dve.wait_ge(lanes_free, i * NL + 3 + 1)
                for k in range(NB_IN):
                    dve.wait_ge(lanes, i * NL + k + 1 + 1)
                    s0 = 4 * k
                    r0 = 0 if s0 < CH else CH
                    bank = psL[k % 4][:, 0:512].rearrange("p (s h r) -> p s h r", s=4, h=HG)
                    settle(dve, passed_dve)
                    for h in range(HG):
                        last = dve.copy_predicated(out=tl[:, s0:s0 + 4, h, r0:r0 + CH], data=bank[:, :, h, r0:r0 + CH],
                                                   mask=lmask[:, s0 - r0:s0 - r0 + 4, :].bitcast(U32))
                    last.then_inc(lanes_free, 1)

            run(dve, body)

        @block.tensor
        def _(pe):
            def left(t):
                return t.rearrange("p h m -> p (h m)")

            def body(i, has_q, make, solve, out):
                def inverse_products(p):
                    j = (i - 2) * NP + p
                    b = p % 2
                    pe.wait_ge(bdt_in[b], (pair(i - 2, p) + 1) * ((HG + 1) * 16) + 1)
                    for c in range(RG):
                        pe.wait_ge(uw_free, 2 * j + c + 1)
                        for r in range(RC):
                            u, x = c * RC + r, r * 2 * HD
                            n = NMOV if r < RC - 1 else 2 * HD
                            last = nc.tensor.matmul(psW[:, c * 512 + x:c * 512 + x + n], left(bdt[:, b, :, :, u]),
                                                    lvc[:, b, u * 2 * HD:u * 2 * HD + n], start=True, stop=True)
                        last.then_inc(uw, 1)

                def products(p):
                    j = i * NP + p
                    b = p % 2
                    pe.wait_ge(rows_l, j + 1 + 1)
                    pe.wait_ge(bdr_in[b], (pair(i, p) + 1) * (HG * 16) + 1)
                    pe.wait_ge(prods_free, j + 1)
                    if has_q:
                        pe.wait_ge(aq_free, (i - NOQ) * NP + p + 1)
                    for u in range(PU):
                        for ps, o, k, x in ((psD[b], u // RC * 512 + u % RC * LQ, 0, 0), (psC[b], u * (CH + SUB), 1, LQ)):
                            o2 = u * LQS + x
                            last = nc.tensor.matmul(ps[:, o:o + NMOV], left(bda[:, b, :, :, k, u]), lqx[:, b, o2:o2 + NMOV],
                                                    start=True, stop=True)
                    last.then_inc(prods, 1)

                if out:
                    pe.wait_ge(tt_ready, i - 1 + 1)
                if make and solve:
                    pe.wait_ge(lanes_free, i * NL - NB_BACK + 3 + 1)
                for p in range(NP):
                    if out and p + 1 < NP:
                        inverse_products(p)
                    if make:
                        products(p)
                if out:
                    inverse_products(NP - 1)

                def lane_transposes(buf, ns, first):
                    for k in range(ns // 4):
                        pe.wait_ge(lanes_free, i * NL + first + k + 1)
                        for s in range(4):
                            last = nc.tensor.transpose(psL[k % 4][:, s * P:(s + 1) * P], buf(4 * k + s), ident[:])
                        last.then_inc(lanes, 1)

                if make:
                    pe.wait_ge(prods_free, (i + 1) * NP + 1 + 1)
                    if has_q:
                        pe.wait_ge(aq_free, (i + 1 - NOQ) * NP + 1 + 1)
                if solve:
                    pe.wait_ge(solved, 2 * i + 1)
                    lane_transposes(lambda s: tl[:, s].rearrange("p h r -> p (h r)"), MI, -NB_BACK)
                if make:
                    lane_transposes(lambda s: dst[:, :, s], MI, 0)
                    lane_transposes(lambda s: cst[:, :, s], CH, NB_IN)

            pe.wait_ge(setup, 2 + 1)
            run(pe, body)


def chain_states(nc, sems, ctx, scratch):
    def sb(name, shape, dt=F32):
        return ctx.enter_context(nc.sbuf_tensor(f"s_{name}", shape, dt))

    def sem(name):
        return sems.new(nc, f"s_{name}")

    bdw = sb("bdw", [P, 2, NG, HG, MI * RC])
    bdr = sb("bdr", [P, 2, NG, HG, HD * RC])
    bdq = sb("bdq", [P, 2, NG, HG, CH * RC])
    bda = sb("bda", [P, 2, NG, HG, CH * RC])
    u = sb("u", [P, 2, NG, RC, HD])
    gam = sb("gam", [P, 2, NG, RC])
    NF, SPARE = 1, 2
    NPART = NG // NF
    NMOV = (1 + SPARE) * HD
    NOUTC = HG * CH
    S = sb("S", [P, 2, NPART, NF + SPARE, HD])
    X = sb("X", [P, 2, NPART, NF + SPARE, HD])
    GS = sb("GS", [P, NG, HD])
    osb = sb("osb", [HG * CH, 2, RC, NG * HD])
    psP = [ctx.enter_context(nc.psum_tensor(f"s_psP{i}", [P, 512], F32)) for i in range(NPART)]
    psO = [ctx.enter_context(nc.psum_tensor(f"s_psO{i}", [P, 512], F32)) for i in range(2)]
    zeroed = sem("zeroed")
    in_m, in_q = ([sem(f"{m}{b}") for b in range(2)] for m in ("chunk_operands_in", "output_operands_in"))
    used = sem("operands_used")
    x_full, x_done, s_full, s_done, g_done = ([sem(f"{m}{f}") for f in range(NPART)] for m in
                                              ("x_product", "x_ready", "s_product", "s_ready", "decayed"))
    parts = [slice(f * NF, (f + 1) * NF) for f in range(NPART)]
    o_full, o_read = sem("o_product"), sem("o_read")
    o_out = [sem(f"o_stored{b}") for b in range(2)]
    LM = (2 * HG + 2) * 16
    LQ = 2 * HG * 16

    GQ = UN // RC
    cut = (QCH0 - 2 * UN) // RC
    segments = [(0, 0, GQ, False), (1, 0, GQ, False), (2, 0, cut, False), (2, cut, GQ, True), (3, 0, GQ, True)]

    def groups(eng, body):
        n0, o0 = 0, 0
        for q, a, b, out in segments:
            assert (b - a) % 2 == 0
            with eng.Fori(0, (b - a) // 2) as i:
                for par in range(2):
                    body(q, i * 2 + (a + par), i + n0 // 2, i + o0 // 2, par, out)
            n0 += b - a
            o0 += (b - a) if out else 0
        return n0, o0

    def groups_act(eng, body):
        n0, o0 = 0, 0
        for q, a, b, out in segments:
            if out:
                with eng.Fori(0, (b - a) // 2) as i:
                    for par in range(2):
                        body(q, i * 2 + (a + par), i + n0 // 2, i + o0 // 2, par, out)
            n0 += b - a
            o0 += (b - a) if out else 0
        return n0, o0

    def streamed(t, a, g, n=NMOV):
        return t[:, a, g // NF, g % NF:g % NF + n // HD, :].rearrange("p k v -> p (k v)")

    def chunk(t, c):
        return t.rearrange("p h (m r) -> p (h m) r", r=RC)[:, :, c]

    passed_sp, passed_dve, passed_pool = (sem(f"passed_{e}") for e in ("sp", "dve", "pool"))
    sems.prime(nc)

    with nc.Block() as block:
        @block.gpsimd
        def _(pool):
            for t in (S, X, bdw):
                pool.memset(t[:], 0.0).then_inc(zeroed, 1)
            pool.wait_ge(zeroed, 6 + 1)

            def body(q, g0, n2, no2, par, out):
                n = n2 * 2 + par
                pool.wait_ge(in_m[par], n2 * LM + LM + 1)
                for c in range(RC):
                    m = n * RC + c
                    for f, gs in enumerate(parts):
                        pool.wait_ge(s_done[f], m + 1 + 1)
                        pool.tensor_tensor(GS[:, gs], S[:, c % 2, f, 0:NF], gam[:, par, gs, c:c + 1].to_broadcast([P, NF, HD]),
                                           ALU.mult).then_inc(g_done[f], 1)

            groups(pool, body)

        @block.sync
        def _(sp):
            sp.wait_ge(zeroed, 6 + 1)

            def body(q, g0, n2, no2, par, out):
                n, no = n2 * 2 + par, no2 * 2 + par
                c0 = g0 * RC
                sp.wait_ge(used, n + 1)
                settle(sp, passed_sp)
                ug = bass.ds(g0, 1)
                gs = slice(q * NG, (q + 1) * NG)
                for h in range(HG):
                    r = slice(h * HD, (h + 1) * HD)
                    sp.dma_start(bdw[r, par, :, h], scratch["uw"][gs, r, ug, HD * RC:].rearrange("g p u c -> p g (u c)")).then_inc(in_m[par], 16)
                    sp.dma_start(bdr[r, par, :, h], scratch["rec"][gs, r, ug, 0:RGAM].rearrange("g p u c -> p g (u c)")).then_inc(in_m[par], 16)
                sp.dma_start(u[:, par].rearrange("p g r c -> p g (r c)"), scratch["uw"][gs, :, ug, 0:HD * RC].rearrange("g p u c -> p g (u c)")).then_inc(in_m[par], 16)
                sp.dma_start(gam[:, par], scratch["rec"][gs, :, ug, RGAM:RQ0].rearrange("g p u c -> p g (u c)")).then_inc(in_m[par], 16)
                if out:
                    for h in range(HG):
                        r = slice(h * HD, (h + 1) * HD)
                        sp.dma_start(bdq[r, par, :, h], scratch["rec"][gs, r, ug, RQ0:RAQ].rearrange("g p u c -> p g (u c)")).then_inc(in_q[par], 16)
                        sp.dma_start(bda[r, par, :, h], scratch["rec"][gs, r, ug, RAQ:RW].rearrange("g p u c -> p g (u c)")).then_inc(in_q[par], 16)

            groups(sp, body)

        @block.scalar
        def _(act):
            act.sem_inc(o_read, 1)

            def body(q, g0, n2, no2, par, out):
                n, no = n2 * 2 + par, no2 * 2 + par
                c0 = g0 * RC
                if not out:
                    return
                act.wait_ge(o_out[par], no2 * (HG * 16) + 1)
                for c in range(RC):
                    act.wait_ge(o_full, no * RC + c + 1 + 1)
                    act.activation(osb[:, par, c, :], psO[c % 2][0:HG * CH, 0:NG * HD], ACT.Copy).then_inc(o_read, 1)
                act.wait_ge(o_read, no * RC + RC + 1 + 1)
                t0 = c0 * CH + q * QT
                for h in range(HG):
                    dst = scratch["o"][h, bass.ds(t0, RC * CH), :].rearrange("(c t) x -> t c x", t=CH)
                    act.dma_start(dst, osb[h * CH:(h + 1) * CH, par])\
                       .then_inc(o_out[par], 16)

            _, no = groups_act(act, body)
            for par in range(2):
                act.wait_ge(o_out[par], no // 2 * HG * 16 + 1)

        @block.vector
        def _(dve):
            for t in (bdr, bdq, bda):
                dve.memset(t[:], 0.0).then_inc(zeroed, 1)
            dve.wait_ge(zeroed, 6 + 1)
            dve.sem_inc(used, 1)
            for f in range(NPART):
                dve.sem_inc(s_done[f], 1)

            def body(q, g0, n2, no2, par, out):
                n, no = n2 * 2 + par, no2 * 2 + par
                dve.wait_ge(in_m[par], n2 * LM + LM + 1)
                for c in range(RC):
                    m = n * RC + c
                    a, b = c % 2, (c + 1) % 2
                    if out:
                        dve.wait_ge(o_full, no * RC + c - 1 + 1) if c else dve.wait_ge(o_read, no * RC + 1)
                    for f, gs in enumerate(parts):
                        dve.wait_ge(x_full[f], m + 1 + 1)
                        dve.tensor_tensor(X[:, a, f, 0:NF], u[:, par, gs, c, :],
                                          psP[f][:, 0:NF * HD].rearrange("p (g v) -> p g v", v=HD), ALU.add).then_inc(x_done[f], 1)
                    for f, gs in enumerate(parts):
                        dve.wait_ge(g_done[f], m + 1 + 1)
                        dve.wait_ge(s_full[f], m + 1 + 1)
                        dve.tensor_tensor(S[:, b, f, 0:NF], GS[:, gs],
                                          psP[f][:, 0:NF * HD].rearrange("p (g v) -> p g v", v=HD), ALU.add).then_inc(s_done[f], 1)
                if out:
                    dve.wait_ge(o_full, no * RC + RC + 1)
                for f in range(NPART):
                    dve.wait_ge(s_done[f], n * RC + RC + 1 + 1)
                dve.sem_inc(used, 1)

            groups(dve, body)

        @block.tensor
        def _(pe):
            pe.wait_ge(zeroed, 6 + 1)

            def body(q, g0, n2, no2, par, out):
                n, no = n2 * 2 + par, no2 * 2 + par
                pe.wait_ge(in_m[par], n2 * LM + LM + 1)
                if out:
                    pe.wait_ge(in_q[par], no2 * LQ + LQ + 1)
                for c in range(RC):
                    m = n * RC + c
                    a = c % 2
                    for w, rhs, ready, done in ((bdw, S, s_done, x_full), (bdr, X, x_done, s_full)):
                        for f in range(NPART):
                            pe.wait_ge(ready[f], m + 1 + 1)
                            for k in range(NF):
                                g = f * NF + k
                                last = nc.tensor.matmul(psP[f][:, k * HD:k * HD + NMOV], chunk(w[:, par, g], c), streamed(rhs, a, g),
                                                        start=True, stop=True)
                            last.then_inc(done[f], 1)
                    if out:
                        pe.wait_ge(o_read, no * RC + c + 1)
                        for g in range(NG):
                            ps = psO[c % 2][0:HG * CH, g * HD:g * HD + NOUTC]
                            nc.tensor.matmul(ps, chunk(bdq[:, par, g], c), streamed(S, a, g, NOUTC), start=True, stop=False)
                            last = nc.tensor.matmul(ps, chunk(bda[:, par, g], c), streamed(X, a, g, NOUTC), start=False, stop=True)
                        last.then_inc(o_full, 1)

            groups(pe, body)


def finish(nc, sems, ctx, consts, scratch, x_r, out_r, Wo1_d, Wo2_d, lnw_d, Wout_d):
    def sb(name, shape, dt=F32):
        return ctx.enter_context(nc.sbuf_tensor(f"f_{name}", shape, dt))

    def sem(name):
        return sems.new(nc, f"f_{name}")

    ident = consts["ident"]
    wout, wo1, wo2 = sb("wout", [P, KD, D]), sb("wo1", [P, KD, HD]), sb("wo2", [HD, D])
    lnw = sb("lnw", [P, D])
    o, x, r, res = (sb(m, [P, 2, 2, D]) for m in ("o", "x", "r", "res"))
    xn, yn, gate = (sb(m, [P, 2, D]) for m in ("xn", "yn", "gate"))
    xnT, ynT = sb("xnT", [P, KD, 2, P]), sb("ynT", [P, KD, 2, P])
    g1 = sb("g1", [HD, 2, P])

    def norm_tiles(tag):
        return [sb(f"{m}{tag}", [P, 2, c]) for m, c in (("st", 6), ("mv", 2), ("ve", 1), ("lnv", 1), ("rs", 1), ("nt", 1))]

    stats_x, stats_y = norm_tiles("x"), norm_tiles("y")
    psX, psG, psY, psO = (ctx.enter_context(nc.psum_tensor(f"f_ps{m}", [P, 2 * 512], F32)) for m in "XGYO")
    psG1 = psX
    loaded, rows_in, stored = (sem("weights_loaded"), [sem(f"rows_in{b}") for b in range(2)],
                               [sem(f"rows_stored{b}") for b in range(2)])
    var_x, rs_x, ln_x, var_y, rs_y, ln_y = (sem(m) for m in ("var_x", "rs_x", "ln_x", "var_y", "rs_y", "ln_y"))
    xn_r, xT_f, xT_r, g1_f, g1_r, g_f, g_r = (sem(m) for m in ("xn", "xT_full", "xT", "g1_full", "g1", "gate_full", "gate"))
    yn_r, yT_f, yT_r, o_f, res_r = (sem(m) for m in ("yn", "yT_full", "yT", "o_full", "res"))
    dve_gate, dve_out = sem("dve_gate_steps"), sem("dve_out_steps")
    passed_sp, passed_dve = sem("passed_sp"), sem("passed_dve")
    full, tail = divmod(NOUT, P)
    PAIRS = (full + 1) // 2
    assert full % 2 == 1 and PAIRS % 2 == 1
    sems.prime(nc)

    def pairs(eng, body):
        with eng.Fori(0, PAIRS // 2) as i:
            for par in range(2):
                body(i, par, (P, P))
        body(PAIRS // 2, 0, (P, tail))

    def pipelined(eng, make_gate, output, both):
        make_gate(0, 0)
        with eng.Fori(0, PAIRS // 2) as i:
            for par in range(2):
                both(i * 2 + par, i, par, i * 2 + par + 1, i + par, 1 - par)
        output(PAIRS - 1, PAIRS // 2, 0)

    def kept(t, i, par, k, rows):
        first = (i * 4 + 2 * par + k) * (3 * P) + 1
        return t[bass.ds(first, 3 * rows - 2), :][0:3 * rows - 2:3, :]

    with nc.Block() as block:
        @block.sync
        def _(sp):
            sp.dma_start(wo1[:], Wo1_d.rearrange("(k p) n -> p k n", p=P)).then_inc(loaded, 16)
            for g in range(NG):
                sp.dma_start(wout[g * HD:(g + 1) * HD], Wout_d[g * P:(g + 1) * P, :].rearrange("(h v) n -> v h n", h=HG)).then_inc(loaded, 16)
            for h in range(HG):
                sp.dma_start(wo2[:, h * P:(h + 1) * P].rearrange("r (g v) -> r g v", g=NG),
                             Wo2_d.rearrange("r (g h v) -> r h g v", g=NG, h=HG)[:, h]).then_inc(loaded, 16)
                sp.dma_start(lnw[:, h * P:(h + 1) * P].rearrange("p (g v) -> p g v", g=NG),
                             lnw_d.rearrange("(a g h v) -> a h g v", a=1, g=NG, h=HG)[:, h].to_broadcast([P, NG, HD])).then_inc(loaded, 16)

            def body(i, par, rows):
                sp.wait_ge(res_r, i * 2 + par + 1)
                settle(sp, passed_sp)
                for k, n in enumerate(rows):
                    sp.dma_start(x[0:n, par, k], kept(x_r, i, par, k, n)).then_inc(rows_in[par], 16)
                for k, n in enumerate(rows):
                    sp.dma_start(o[0:n, par, k].rearrange("p (h x) -> p h x", h=HG),
                                 scratch["o"][:, bass.ds((i * 4 + 2 * par + k) * P + OUT0, n), :].rearrange("h t x -> t h x"))\
                      .then_inc(rows_in[par], 16)
                    sp.dma_start(r[0:n, par, k], kept(out_r, i, par, k, n)).then_inc(rows_in[par], 16)

            pairs(sp, body)

        @block.scalar
        def _(act):
            def rsqrt(j, stats, var, ln, rs_ready):
                _, _, ve, lnv, rs, _ = stats
                act.wait_ge(var, j + 1 + 1)
                act.activation(lnv[:], ve[:], ACT.Ln).then_inc(ln, 1)
                act.wait_ge(ln, j + 1 + 1)
                act.activation(rs[:], lnv[:], ACT.Exp, scale=-0.5).then_inc(rs_ready, 1)

            def by_tile(ps):
                return ps[:].rearrange("p (a k t) -> p k a t", a=2, k=KD)

            def gate_tail(j):
                act.wait_ge(xT_f, j + 1 + 1)
                act.activation(xnT[:], by_tile(psX), ACT.Copy).then_inc(xT_r, 1)
                act.wait_ge(g1_f, j + 1 + 1)
                act.activation(g1[:].rearrange("r a t -> r (a t)"), psG1[0:HD, 0:2 * P], ACT.Copy).then_inc(g1_r, 1)
                act.wait_ge(g_f, j + 1 + 1)
                act.activation(gate[:].rearrange("p a d -> p (a d)"), psG[:], ACT.Sigmoid).then_inc(g_r, 1)

            def out_copy(j):
                act.wait_ge(yT_f, j + 1 + 1)
                act.activation(ynT[:], by_tile(psY), ACT.Copy).then_inc(yT_r, 1)

            def store(j, i, par, rows):
                act.wait_ge(res_r, j + 2 + 1)
                for k, n in enumerate(rows):
                    act.dma_start(kept(out_r, i, par, k, n), res[0:n, par, k]).then_inc(stored[par], 16)

            def make_gate(j, par):
                rsqrt(j, stats_x, var_x, ln_x, rs_x)
                gate_tail(j)

            def output(j, i, par):
                rsqrt(j, stats_y, var_y, ln_y, rs_y)
                out_copy(j)
                store(j, i, par, (P, tail))

            def both(j, i, par, j1, i1, par1):
                rsqrt(j, stats_y, var_y, ln_y, rs_y)
                rsqrt(j1, stats_x, var_x, ln_x, rs_x)
                out_copy(j)
                gate_tail(j1)
                store(j, i, par, (P, P))

            pipelined(act, make_gate, output, both)
            act.wait_ge(stored[0], (PAIRS + 1) // 2 * 32 + 1)
            act.wait_ge(stored[1], PAIRS // 2 * 32 + 1)

        @block.vector
        def _(dve):
            dve.wait_ge(loaded, (1 + NG + 2 * HG) * 16 + 1)
            dve.sem_inc(res_r, 1)

            def variance(ch, stats, src, var):
                st, mv, ve = stats[:3]
                for k in range(2):
                    ch.link(dve.bn_stats(st[:, k], src[:, k]))
                    settle(dve, passed_dve)
                    ch.link(dve.bn_aggr(mv[:, k], st[:, k]))
                ch.link(dve.tensor_scalar(ve[:], mv[:, :, 1:2], LN_EPS, None, ALU.add))
                dve.sem_inc(var, 1)

            def normalised(ch, j, stats, src, dst, rs_ready):
                _, mv, ve, _, rs, nt = stats
                dve.wait_ge(rs_ready, j + 1 + 1)
                ch.link(dve.tensor_tensor(nt[:], rs[:], rs[:], ALU.mult))
                ch.link(dve.tensor_tensor(nt[:], nt[:], ve[:], ALU.mult))
                ch.link(dve.tensor_scalar(nt[:], nt[:], -0.5, 1.5, ALU.mult, ALU.add))
                ch.link(dve.tensor_tensor(rs[:], nt[:], rs[:], ALU.mult))
                for k in range(2):
                    last = dve.tensor_scalar(dst[:, k], src[:, k], mv[:, k, 0:1], rs[:, k], ALU.subtract, ALU.mult)
                return last

            GATE_STEPS, OUT_STEPS = 5 + 4, 1 + 5 + 4 + 1

            def gate_chain(j):
                return Chain(dve, dve_gate, j, GATE_STEPS)

            def out_chain(j):
                return Chain(dve, dve_out, j, OUT_STEPS)

            def x_variance(ch, j, i, par):
                dve.wait_ge(rows_in[par], i * 96 + 96 + 1)
                variance(ch, stats_x, x[:, par], var_x)

            def x_rows(ch, j, par):
                normalised(ch, j, stats_x, x[:, par], xn, rs_x).then_inc(xn_r, 1)
                ch.end()

            def y_variance(ch, j, par):
                dve.wait_ge(g_r, j + 1 + 1)
                ch.link(dve.tensor_tensor(o[:, par], o[:, par], gate[:], ALU.mult))
                variance(ch, stats_y, o[:, par], var_y)

            def y_rows(ch, j, par):
                ch.link(normalised(ch, j, stats_y, o[:, par], yn, rs_y))
                dve.tensor_tensor(yn[:], yn[:], lnw[:].unsqueeze(1).to_broadcast([P, 2, D]), ALU.mult).then_inc(yn_r, 1)
                ch.end()

            def add(j, i, par):
                dve.wait_ge(o_f, j + 1 + 1)
                dve.wait_ge(stored[par], i * 32 + 1)
                dve.tensor_tensor(res[:, par], psO[:].rearrange("p (a d) -> p a d", a=2), r[:, par], ALU.add).then_inc(res_r, 1)

            def make_gate(j, par):
                ch = gate_chain(j)
                x_variance(ch, j, 0, par)
                x_rows(ch, j, par)

            def output(j, i, par):
                ch = out_chain(j)
                y_variance(ch, j, par)
                y_rows(ch, j, par)
                add(j, i, par)

            def both(j, i, par, j1, i1, par1):
                out, gt = out_chain(j), gate_chain(j1)
                y_variance(out, j, par)
                x_variance(gt, j1, i1, par1)
                y_rows(out, j, par)
                x_rows(gt, j1, par1)
                add(j, i, par)

            pipelined(dve, make_gate, output, both)

        @block.tensor
        def _(pe):
            pe.wait_ge(loaded, (1 + NG + 2 * HG) * 16 + 1)

            def transposes(ps, rows, full_sem):
                for a in range(2):
                    for kd in range(KD):
                        c = (a * KD + kd) * P
                        last = nc.tensor.transpose(ps[:, c:c + P], rows[:, a, kd * P:(kd + 1) * P], ident[:])
                last.then_inc(full_sem, 1)

            def x_transposes(j):
                pe.wait_ge(xn_r, j + 1 + 1)
                transposes(psX, xn, xT_f)

            def gates(j):
                pe.wait_ge(xT_r, j + 1 + 1)
                for kd in range(KD):
                    last = nc.tensor.matmul(psG1[0:HD, 0:2 * P], wo1[:, kd, :], xnT[:, kd].rearrange("p a t -> p (a t)"),
                                            start=(kd == 0), stop=(kd == KD - 1))
                last.then_inc(g1_f, 1)
                pe.wait_ge(g1_r, j + 1 + 1)
                for a in range(2):
                    last = nc.tensor.matmul(psG[:, a * D:(a + 1) * D], g1[:, a], wo2[:], start=True, stop=True)
                last.then_inc(g_f, 1)

            def y_transposes(j):
                pe.wait_ge(yn_r, j + 1 + 1)
                transposes(psY, yn, yT_f)

            def outputs(j):
                pe.wait_ge(yT_r, j + 1 + 1)
                for a in range(2):
                    for kd in range(KD):
                        last = nc.tensor.matmul(psO[:, a * D:(a + 1) * D], ynT[:, kd, a], wout[:, kd, :],
                                                start=(kd == 0), stop=(kd == KD - 1))
                last.then_inc(o_f, 1)

            def make_gate(j, par):
                x_transposes(j)
                gates(j)

            def output(j, i, par):
                y_transposes(j)
                outputs(j)

            def both(j, i, par, j1, i1, par1):
                y_transposes(j)
                x_transposes(j1)
                outputs(j)
                gates(j1)

            pipelined(pe, make_gate, output, both)


_INS = ["L0_attn_x", "L0_attn_Wq", "L0_attn_Wk", "L0_attn_Wv", "L0_attn_Wf1", "L0_attn_Wf2", "L0_attn_Wg",
        "L0_attn_Wo1", "L0_attn_Wo2", "L0_attn_ln_w", "L0_attn_Wout", "L0_ffn_kernel", "L0_ffn_input_scale",
        "L0_ffn_kernel_scale", "L0_ffn_bias"]


def kernel(**inputs):
    import numpy as _np
    import concourse.bacc as _bacc
    from concourse import mybir as _mybir
    from concourse.bass_utils import run_bass_kernel_spmd as _run

    nc = _bacc.Bacc("TRN2", target_bir_lowering=False, num_devices=1)
    arrays, args = {}, []
    for name in _INS:
        a = _np.ascontiguousarray(inputs[name])
        arrays[f"in_{name}"] = a
        args.append(nc.dram_tensor(f"in_{name}", a.shape, _mybir.dt.from_np(a.dtype), kind="ExternalInput").ap())
    out = nc.dram_tensor("out", (1, T, D), F32, kind="ExternalOutput").ap()
    program(nc, *args, out)
    r = _run(nc, [arrays], core_ids=[0])
    return r.results[0]["out"]
```
